# Optimizing a Trainium2 kernel written in Bass

```python
import numpy as np
import jax
import jax.numpy as jnp

def _softmax(x, axis=-1):
    return jax.nn.softmax(x, axis=axis)

def _gelu(x):
    return jax.nn.gelu(x, approximate=True)

def _silu(x):
    return jax.nn.silu(x)

def _sigmoid(x):
    return jax.nn.sigmoid(x)

def _layernorm(x, axis=-1, eps=1e-05):
    m = jnp.mean(x, axis=axis, keepdims=True)
    v = jnp.var(x, axis=axis, keepdims=True)
    return (x - m) / jnp.sqrt(v + eps)

def _scatter_add(tgt, idx, src, axis=0):
    return tgt.at[idx].add(src)

def _segment_sum(src, seg, n):
    return jax.ops.segment_sum(src, seg, n)
kernel_name = 'mk_xattn_seq_d4_seqx_r8_5ea27d'

def setup_inputs(seed: int=0):
    np.random.seed(seed)
    _w = jnp.asarray

    def _rec_inputs():
        import jax
        import jax.numpy as jnp
        _rk = jax.random.key(seed)
        x = -0.000125 + 0.9999 * jax.random.normal(jax.random.fold_in(_rk, 1), (8, 128, 256), jnp.float32)
        _lenS = 128 - jax.random.randint(jax.random.fold_in(_rk, 7), (8,), 0, max(1, 128 // 4) + 1, jnp.int32)
        _lenS2 = 128 - jax.random.randint(jax.random.fold_in(_rk, 8), (8,), 0, max(1, 128 // 4) + 1, jnp.int32)
        _ctx_2048P = jax.random.normal(jax.random.fold_in(_rk, 11), (8, 16, 256), jnp.float32)
        _ctx_2048c = jax.random.dirichlet(jax.random.fold_in(_rk, 511), 0.3 * jnp.ones((16,), jnp.float32), (8, 128))
        _ctx_2048t = jnp.einsum('bsk,bkd->bsd', _ctx_2048c, _ctx_2048P)
        _ctx_2048t = _ctx_2048t * jax.lax.rsqrt(jnp.mean(jnp.square(_ctx_2048t)) + 1e-12) * 0.953939
        ctx_2048 = -1.52775e-05 + 0.999936 * (_ctx_2048t + 0.3 * jax.random.normal(jax.random.fold_in(_rk, 611), (8, 128, 256), jnp.float32))
        _validS = jnp.arange(128)[None, :] < _lenS[:, None]
        _validS2 = jnp.arange(128)[None, :] < _lenS2[:, None]
        _causal = jnp.tril(jnp.ones((128, 128), dtype=bool))
        mask_Bx1x2048_bf1 = jnp.ones((8, 1, 256), dtype=bool)
        mask_1x1xSxS2_fc1 = jnp.where(jnp.broadcast_to(_validS2[0:1, None, None, :], (1, 1, 128, 128)), 1.0, 0.0).astype(jnp.float32)
        mask_Bx1xSxS2_ff1 = jnp.where(jnp.ones((8, 1, 128, 128), dtype=bool), 1.0, 0.0).astype(jnp.float32)
        return (x, ctx_2048, mask_Bx1x2048_bf1, mask_1x1xSxS2_fc1, mask_Bx1xSxS2_ff1)
    x, ctx_2048, mask_Bx1x2048_bf1, mask_1x1xSxS2_fc1, mask_Bx1xSxS2_ff1 = _rec_inputs()

    def _L0_xattn_setup():
        import jax, jax.numpy as jnp
        import numpy as np
        B, C, CI, N = (16, 128, 64, 256)
        EPS = 1e-05

        def _conv1x1(w, b, x):
            return jnp.einsum('oc,bcn->bon', w, x) + b[None, :, None]
        key = jax.random.key(seed)
        ks = jax.random.split(key, 14)
        s = 0.02
        return {'x': jax.random.normal(ks[0], (B, C, N), jnp.float32), 'x_2': jax.random.normal(ks[1], (B, C, N), jnp.float32), 'theta_w': jax.random.normal(ks[2], (CI, C), jnp.float32) * s, 'theta_b': jax.random.normal(ks[3], (CI,), jnp.float32) * s, 'phi_w': jax.random.normal(ks[4], (CI, C), jnp.float32) * s, 'phi_b': jax.random.normal(ks[5], (CI,), jnp.float32) * s, 'g_w': jax.random.normal(ks[6], (CI, C), jnp.float32) * s, 'g_b': jax.random.normal(ks[7], (CI,), jnp.float32) * s, 'w_w': jax.random.normal(ks[8], (C, CI), jnp.float32) * s, 'w_b': jax.random.normal(ks[9], (C,), jnp.float32) * s, 'bn_gamma': jax.random.normal(ks[10], (C,), jnp.float32), 'bn_beta': jax.random.normal(ks[11], (C,), jnp.float32), 'bn_mean': jax.random.normal(ks[12], (C,), jnp.float32), 'bn_var': jax.random.uniform(ks[13], (C,), jnp.float32, 0.5, 1.5)}
    _L0_xattn_all = _L0_xattn_setup()
    _L0_xattn_in = {k: v for k, v in _L0_xattn_all.items() if k in ('theta_w', 'theta_b', 'phi_w', 'phi_b', 'g_w', 'g_b', 'w_w', 'w_b', 'bn_gamma', 'bn_beta', 'bn_mean', 'bn_var')}
    del _L0_xattn_all

    def _L1_xattn_setup():
        import jax, jax.numpy as jnp
        import numpy as np
        import math
        N_HEADS = 16
        EPS = 1e-05

        def _masked_instance_norm(x, mask):
            m = mask.astype(x.dtype)
            x = x * m
            n_valid = jnp.sum(m, axis=-1, keepdims=True)
            mean = jnp.sum(x, axis=-1, keepdims=True) / n_valid
            var = jnp.sum(x * x, axis=-1, keepdims=True) / n_valid - mean * mean
            x = (x - mean) / jnp.sqrt(jax.nn.relu(var) + EPS)
            return x * m
        key = jax.random.key(seed)
        ks = jax.random.split(key, 8)
        bs, c, t1, t2 = (2, 128, 256, 256)
        s = 1.0 / math.sqrt(c)
        return {'x': jax.random.normal(ks[0], (bs, c, t1), jnp.float32), 'mask': jnp.ones((bs, 1, t1), jnp.bool_), 'kv': jax.random.normal(ks[1], (bs, c, t2), jnp.float32), 'kv_mask': jnp.ones((bs, 1, t2), jnp.bool_), 'Wq': jax.random.normal(ks[2], (c, c), jnp.float32) * s, 'bq': jnp.zeros((c,), jnp.float32), 'Wk': jax.random.normal(ks[3], (c, c), jnp.float32) * s, 'bk': jnp.zeros((c,), jnp.float32), 'Wv': jax.random.normal(ks[4], (c, c), jnp.float32) * s, 'bv': jnp.zeros((c,), jnp.float32)}
    _L1_xattn_all = _L1_xattn_setup()
    _L1_xattn_in = {k: v for k, v in _L1_xattn_all.items() if k in ('Wq', 'bq', 'Wk', 'bk', 'Wv', 'bv')}
    del _L1_xattn_all

    def _L2_xattn_setup():
        import jax, jax.numpy as jnp
        import numpy as np
        H = 256
        NH = 16
        HD = H // NH
        EPS = 1e-05

        def gelu(x):
            return 0.5 * x * (1.0 + jnp.tanh(0.7978845608028654 * x * (1.0 + 0.044715 * x * x)))

        def layernorm(x, scale, bias):
            m = jnp.mean(x, axis=-1, keepdims=True)
            v = jnp.mean(jnp.square(x - m), axis=-1, keepdims=True)
            return (x - m) * jax.lax.rsqrt(v + EPS) * scale + bias

        def split_heads(x):
            b, s, _ = x.shape
            return x.reshape(b, s, NH, HD).transpose(0, 2, 1, 3)

        def merge_heads(x):
            b, nh, s, hd = x.shape
            return x.transpose(0, 2, 1, 3).reshape(b, s, nh * hd)

        def attention(q, k, v, mask):
            scores = jnp.einsum('bhqd,bhkd->bhqk', q, k) / jnp.sqrt(jnp.float32(HD))
            scores = scores * mask - 10000.0 * (1.0 - mask)
            probs = jax.nn.softmax(scores, axis=-1)
            return jnp.einsum('bhqk,bhkd->bhqd', probs, v)
        key = jax.random.key(seed)
        ks = jax.random.split(key, 16)
        b, s, t = (2, 128, 128)
        w = lambda k, i, o: jax.random.normal(k, (i, o), jnp.float32) * 0.02
        inp = {'hidden_states': jax.random.normal(ks[0], (b, s, H), jnp.float32), 'encoder_states': jax.random.normal(ks[1], (b, t, H), jnp.float32), 'ltor_mask': jnp.tril(jnp.ones((1, 1, s, s), jnp.float32)), 'cross_mask': jnp.ones((b, 1, s, t), jnp.float32), 'ln1_s': jnp.ones((H,), jnp.float32), 'ln1_b': jnp.zeros((H,), jnp.float32), 'w_qkv': w(ks[2], H, 3 * H), 'b_qkv': jnp.zeros((3 * H,), jnp.float32), 'w_ao': w(ks[3], H, H), 'b_ao': jnp.zeros((H,), jnp.float32), 'ln2_s': jnp.ones((H,), jnp.float32), 'ln2_b': jnp.zeros((H,), jnp.float32), 'w_q': w(ks[4], H, H), 'b_q': jnp.zeros((H,), jnp.float32), 'w_kv': w(ks[5], H, 2 * H), 'b_kv': jnp.zeros((2 * H,), jnp.float32), 'w_co': w(ks[6], H, H), 'b_co': jnp.zeros((H,), jnp.float32), 'ln3_s': jnp.ones((H,), jnp.float32), 'ln3_b': jnp.zeros((H,), jnp.float32), 'w1': w(ks[7], H, 4 * H), 'b1': jnp.zeros((4 * H,), jnp.float32), 'w2': w(ks[8], 4 * H, H), 'b2': jnp.zeros((H,), jnp.float32)}
        return inp
    _L2_xattn_all = _L2_xattn_setup()
    _L2_xattn_in = {k: v for k, v in _L2_xattn_all.items() if k in ('ln1_s', 'ln1_b', 'w_qkv', 'b_qkv', 'w_ao', 'b_ao', 'ln2_s', 'ln2_b', 'w_q', 'b_q', 'w_kv', 'b_kv', 'w_co', 'b_co', 'ln3_s', 'ln3_b', 'w1', 'b1', 'w2', 'b2')}
    del _L2_xattn_all

    def _L3_xattn_setup():
        import jax, jax.numpy as jnp
        import numpy as np
        E, H, L, B = (256, 32, 128, 4)
        S = E // H
        DM, DD = (32, 64)

        def _ln(x, w, b, eps=1e-05):
            m = x.mean(-1, keepdims=True)
            v = ((x - m) ** 2).mean(-1, keepdims=True)
            return (x - m) / jnp.sqrt(v + eps) * w + b

        def _block(x, state, ln1_w, ln1_b, ln2_w, ln2_b, maa_x, maa_w1, maa_w2, maa_stack, time_decay, td_w1, td_w2, u, Wr, Wk, Wv, Wg, Wo, gn_w, gn_b, ffn_maa_k, ffn_maa_r, Wfk, Wfr, Wfv):
            b, l, e = x.shape
            h = u.shape[0]
            s_ = e // h
            xa = _ln(x, ln1_w, ln1_b)
            sx = jnp.concatenate([state[:, 1:2] - xa[:, :1], xa[:, :-1] - xa[:, 1:]], axis=1)
            xxx = jnp.tanh((xa + sx * maa_x) @ maa_w1).reshape(b, l, 5, DM)
            xxx = jnp.einsum('blfd,fde->blfe', xxx, maa_w2)
            xm = xa[:, :, None] + sx[:, :, None] * (maa_stack + xxx)
            xk, xw, xv, xr, xg = (xm[:, :, j] for j in range(5))
            w = jnp.exp(-jnp.exp(time_decay + jnp.tanh(xw @ td_w1) @ td_w2)).reshape(b, l, h, s_)
            r = (xr @ Wr.T).reshape(b, l, h, s_)
            k = (xk @ Wk.T).reshape(b, l, h, s_)
            v = (xv @ Wv.T).reshape(b, l, h, s_)
            g = jax.nn.silu(xg @ Wg.T)
            s0 = state[:, 2:2 + s_].reshape(b, h, s_, s_)

            def step(s, rkvw):
                r_t, k_t, v_t, w_t = rkvw
                a = k_t[..., :, None] * v_t[..., None, :]
                out = jnp.einsum('bhi,bhij->bhj', r_t, u * a + s)
                s = a + w_t[..., :, None] * s
                return (s, out)
            rkvw = tuple((jnp.moveaxis(t, 1, 0) for t in (r, k, v, w)))
            _, out = jax.lax.scan(step, s0, rkvw)
            out = jnp.moveaxis(out, 0, 1).reshape(b, l, e)
            og = out.reshape(b, l, h, s_)
            m = og.mean(-1, keepdims=True)
            va = ((og - m) ** 2).mean(-1, keepdims=True)
            og = ((og - m) / jnp.sqrt(va + 1e-05)).reshape(b, l, e) * gn_w + gn_b
            x1 = x + og * g @ Wo.T
            xc = _ln(x1, ln2_w, ln2_b)
            sx2 = jnp.concatenate([state[:, 0:1] - xc[:, :1], xc[:, :-1] - xc[:, 1:]], axis=1)
            xk2 = xc + sx2 * ffn_maa_k
            xr2 = xc + sx2 * ffn_maa_r
            rr = jax.nn.sigmoid(xr2 @ Wfr.T)
            kk = jnp.square(jax.nn.relu(xk2 @ Wfk.T))
            return x1 + rr * (kk @ Wfv.T)
        key = jax.random.key(seed)
        ks = jax.random.split(key, 24)
        sc = 0.02
        d = {'x': jax.random.normal(ks[0], (B, L, E), jnp.float32), 'state': jax.random.normal(ks[1], (B, 2 + S, E), jnp.float32) * 0.1, 'ln1_w': jnp.ones((E,), jnp.float32), 'ln1_b': jnp.zeros((E,), jnp.float32), 'ln2_w': jnp.ones((E,), jnp.float32), 'ln2_b': jnp.zeros((E,), jnp.float32), 'maa_x': jax.random.normal(ks[2], (E,), jnp.float32) * 0.1, 'maa_w1': jax.random.normal(ks[3], (E, 5 * DM), jnp.float32) * sc, 'maa_w2': jax.random.normal(ks[4], (5, DM, E), jnp.float32) * sc, 'maa_stack': jax.random.normal(ks[5], (1, 5, E), jnp.float32) * 0.1, 'time_decay': jax.random.normal(ks[6], (E,), jnp.float32) * 0.5, 'td_w1': jax.random.normal(ks[7], (E, DD), jnp.float32) * sc, 'td_w2': jax.random.normal(ks[8], (DD, E), jnp.float32) * sc, 'u': jax.random.normal(ks[9], (H, S, 1), jnp.float32) * 0.1, 'Wr': jax.random.normal(ks[10], (E, E), jnp.float32) * sc, 'Wk': jax.random.normal(ks[11], (E, E), jnp.float32) * sc, 'Wv': jax.random.normal(ks[12], (E, E), jnp.float32) * sc, 'Wg': jax.random.normal(ks[13], (E, E), jnp.float32) * sc, 'Wo': jax.random.normal(ks[14], (E, E), jnp.float32) * sc, 'gn_w': jnp.ones((E,), jnp.float32), 'gn_b': jnp.zeros((E,), jnp.float32), 'ffn_maa_k': jax.random.normal(ks[15], (E,), jnp.float32) * 0.1, 'ffn_maa_r': jax.random.normal(ks[16], (E,), jnp.float32) * 0.1, 'Wfk': jax.random.normal(ks[17], (E, E), jnp.float32) * sc, 'Wfr': jax.random.normal(ks[18], (E, E), jnp.float32) * sc, 'Wfv': jax.random.normal(ks[19], (E, E), jnp.float32) * sc}
        return d
    _L3_xattn_all = _L3_xattn_setup()
    _L3_xattn_in = {k: v for k, v in _L3_xattn_all.items() if k in ('ln1_w', 'ln1_b', 'ln2_w', 'ln2_b', 'maa_x', 'maa_w1', 'maa_w2', 'maa_stack', 'time_decay', 'td_w1', 'td_w2', 'u', 'Wr', 'Wk', 'Wv', 'Wg', 'Wo', 'gn_w', 'gn_b', 'ffn_maa_k', 'ffn_maa_r', 'Wfk', 'Wfr', 'Wfv')}
    del _L3_xattn_all
    return {'x': x, 'ctx_2048': ctx_2048, 'mask_Bx1x2048_bf1': mask_Bx1x2048_bf1, 'mask_1x1xSxS2_fc1': mask_1x1xSxS2_fc1, 'mask_Bx1xSxS2_ff1': mask_Bx1xSxS2_ff1, 'L0_xattn_theta_w': _L0_xattn_in['theta_w'], 'L0_xattn_theta_b': _L0_xattn_in['theta_b'], 'L0_xattn_phi_w': _L0_xattn_in['phi_w'], 'L0_xattn_phi_b': _L0_xattn_in['phi_b'], 'L0_xattn_g_w': _L0_xattn_in['g_w'], 'L0_xattn_g_b': _L0_xattn_in['g_b'], 'L0_xattn_w_w': _L0_xattn_in['w_w'], 'L0_xattn_w_b': _L0_xattn_in['w_b'], 'L0_xattn_bn_gamma': _L0_xattn_in['bn_gamma'], 'L0_xattn_bn_beta': _L0_xattn_in['bn_beta'], 'L0_xattn_bn_mean': _L0_xattn_in['bn_mean'], 'L0_xattn_bn_var': _L0_xattn_in['bn_var'], 'L1_xattn_Wq': _L1_xattn_in['Wq'], 'L1_xattn_bq': _L1_xattn_in['bq'], 'L1_xattn_Wk': _L1_xattn_in['Wk'], 'L1_xattn_bk': _L1_xattn_in['bk'], 'L1_xattn_Wv': _L1_xattn_in['Wv'], 'L1_xattn_bv': _L1_xattn_in['bv'], 'L2_xattn_ln1_s': _L2_xattn_in['ln1_s'], 'L2_xattn_ln1_b': _L2_xattn_in['ln1_b'], 'L2_xattn_w_qkv': _L2_xattn_in['w_qkv'], 'L2_xattn_b_qkv': _L2_xattn_in['b_qkv'], 'L2_xattn_w_ao': _L2_xattn_in['w_ao'], 'L2_xattn_b_ao': _L2_xattn_in['b_ao'], 'L2_xattn_ln2_s': _L2_xattn_in['ln2_s'], 'L2_xattn_ln2_b': _L2_xattn_in['ln2_b'], 'L2_xattn_w_q': _L2_xattn_in['w_q'], 'L2_xattn_b_q': _L2_xattn_in['b_q'], 'L2_xattn_w_kv': _L2_xattn_in['w_kv'], 'L2_xattn_b_kv': _L2_xattn_in['b_kv'], 'L2_xattn_w_co': _L2_xattn_in['w_co'], 'L2_xattn_b_co': _L2_xattn_in['b_co'], 'L2_xattn_ln3_s': _L2_xattn_in['ln3_s'], 'L2_xattn_ln3_b': _L2_xattn_in['ln3_b'], 'L2_xattn_w1': _L2_xattn_in['w1'], 'L2_xattn_b1': _L2_xattn_in['b1'], 'L2_xattn_w2': _L2_xattn_in['w2'], 'L2_xattn_b2': _L2_xattn_in['b2'], 'L3_xattn_ln1_w': _L3_xattn_in['ln1_w'], 'L3_xattn_ln1_b': _L3_xattn_in['ln1_b'], 'L3_xattn_ln2_w': _L3_xattn_in['ln2_w'], 'L3_xattn_ln2_b': _L3_xattn_in['ln2_b'], 'L3_xattn_maa_x': _L3_xattn_in['maa_x'], 'L3_xattn_maa_w1': _L3_xattn_in['maa_w1'], 'L3_xattn_maa_w2': _L3_xattn_in['maa_w2'], 'L3_xattn_maa_stack': _L3_xattn_in['maa_stack'], 'L3_xattn_time_decay': _L3_xattn_in['time_decay'], 'L3_xattn_td_w1': _L3_xattn_in['td_w1'], 'L3_xattn_td_w2': _L3_xattn_in['td_w2'], 'L3_xattn_u': _L3_xattn_in['u'], 'L3_xattn_Wr': _L3_xattn_in['Wr'], 'L3_xattn_Wk': _L3_xattn_in['Wk'], 'L3_xattn_Wv': _L3_xattn_in['Wv'], 'L3_xattn_Wg': _L3_xattn_in['Wg'], 'L3_xattn_Wo': _L3_xattn_in['Wo'], 'L3_xattn_gn_w': _L3_xattn_in['gn_w'], 'L3_xattn_gn_b': _L3_xattn_in['gn_b'], 'L3_xattn_ffn_maa_k': _L3_xattn_in['ffn_maa_k'], 'L3_xattn_ffn_maa_r': _L3_xattn_in['ffn_maa_r'], 'L3_xattn_Wfk': _L3_xattn_in['Wfk'], 'L3_xattn_Wfr': _L3_xattn_in['Wfr'], 'L3_xattn_Wfv': _L3_xattn_in['Wfv']}

def reference(x, ctx_2048, mask_Bx1x2048_bf1, mask_1x1xSxS2_fc1, mask_Bx1xSxS2_ff1, L0_xattn_theta_w, L0_xattn_theta_b, L0_xattn_phi_w, L0_xattn_phi_b, L0_xattn_g_w, L0_xattn_g_b, L0_xattn_w_w, L0_xattn_w_b, L0_xattn_bn_gamma, L0_xattn_bn_beta, L0_xattn_bn_mean, L0_xattn_bn_var, L1_xattn_Wq, L1_xattn_bq, L1_xattn_Wk, L1_xattn_bk, L1_xattn_Wv, L1_xattn_bv, L2_xattn_ln1_s, L2_xattn_ln1_b, L2_xattn_w_qkv, L2_xattn_b_qkv, L2_xattn_w_ao, L2_xattn_b_ao, L2_xattn_ln2_s, L2_xattn_ln2_b, L2_xattn_w_q, L2_xattn_b_q, L2_xattn_w_kv, L2_xattn_b_kv, L2_xattn_w_co, L2_xattn_b_co, L2_xattn_ln3_s, L2_xattn_ln3_b, L2_xattn_w1, L2_xattn_b1, L2_xattn_w2, L2_xattn_b2, L3_xattn_ln1_w, L3_xattn_ln1_b, L3_xattn_ln2_w, L3_xattn_ln2_b, L3_xattn_maa_x, L3_xattn_maa_w1, L3_xattn_maa_w2, L3_xattn_maa_stack, L3_xattn_time_decay, L3_xattn_td_w1, L3_xattn_td_w2, L3_xattn_u, L3_xattn_Wr, L3_xattn_Wk, L3_xattn_Wv, L3_xattn_Wg, L3_xattn_Wo, L3_xattn_gn_w, L3_xattn_gn_b, L3_xattn_ffn_maa_k, L3_xattn_ffn_maa_r, L3_xattn_Wfk, L3_xattn_Wfr, L3_xattn_Wfv):
    import jax
    import jax.numpy as jnp

    def _L0_xattn_ref(x, x_2, theta_w, theta_b, phi_w, phi_b, g_w, g_b, w_w, w_b, bn_gamma, bn_beta, bn_mean, bn_var):
        import jax, jax.numpy as jnp
        import numpy as np
        B, C, CI, N = (16, 128, 64, 256)
        EPS = 1e-05

        def _conv1x1(w, b, x):
            return jnp.einsum('oc,bcn->bon', w, x) + b[None, :, None]
        g_x = _conv1x1(g_w, g_b, x_2).transpose(0, 2, 1)
        theta_x = _conv1x1(theta_w, theta_b, x).transpose(0, 2, 1)
        phi_x = _conv1x1(phi_w, phi_b, x_2)
        W = jnp.einsum('bnc,bcm->bnm', theta_x, phi_x) / phi_x.shape[-1]
        y = jnp.einsum('bnm,bmc->bnc', W, g_x).transpose(0, 2, 1)
        wy = _conv1x1(w_w, w_b, y)
        inv_std = jax.lax.rsqrt(bn_var + EPS)
        wy = bn_gamma[None, :, None] * (wy - bn_mean[None, :, None]) * inv_std[None, :, None] + bn_beta[None, :, None]
        return wy + x

    def _L1_xattn_ref(x, mask, kv, kv_mask, Wq, bq, Wk, bk, Wv, bv):
        import jax, jax.numpy as jnp
        import numpy as np
        import math
        N_HEADS = 16
        EPS = 1e-05

        def _masked_instance_norm(x, mask):
            m = mask.astype(x.dtype)
            x = x * m
            n_valid = jnp.sum(m, axis=-1, keepdims=True)
            mean = jnp.sum(x, axis=-1, keepdims=True) / n_valid
            var = jnp.sum(x * x, axis=-1, keepdims=True) / n_valid - mean * mean
            x = (x - mean) / jnp.sqrt(jax.nn.relu(var) + EPS)
            return x * m
        bs, c, t1 = x.shape
        h = N_HEADS
        d = c // h
        scale = 1.0 / math.sqrt(d)
        q = jnp.einsum('oc,bct->bot', Wq, x) + bq[None, :, None]
        k = jnp.einsum('oc,bct->bot', Wk, kv) + bk[None, :, None]
        v = jnp.einsum('oc,bct->bot', Wv, kv) + bv[None, :, None]
        q = q.reshape(bs, h, d, t1).transpose(0, 1, 3, 2)
        k = k.reshape(bs, h, d, -1)
        v = v.reshape(bs, h, d, -1).transpose(0, 1, 3, 2)
        attn = jnp.einsum('bhqd,bhdk->bhqk', q * scale, k)
        attn = jnp.where(kv_mask[:, :, None, :], attn, -jnp.inf)
        attn = jax.nn.softmax(attn, axis=-1)
        mean = jnp.einsum('bhqk,bhkd->bhqd', attn, v)
        ex2 = jnp.einsum('bhqk,bhkd->bhqd', attn, v * v)
        std = jnp.sqrt(jax.nn.relu(ex2 - mean * mean))
        mean = mean.transpose(0, 1, 3, 2).reshape(bs, c, t1)
        std = std.transpose(0, 1, 3, 2).reshape(bs, c, t1)
        xn = _masked_instance_norm(x, mask)
        out = (xn * std + mean) * mask.astype(x.dtype)
        return out

    def _L2_xattn_ref(hidden_states, encoder_states, ltor_mask, cross_mask, ln1_s, ln1_b, w_qkv, b_qkv, w_ao, b_ao, ln2_s, ln2_b, w_q, b_q, w_kv, b_kv, w_co, b_co, ln3_s, ln3_b, w1, b1, w2, b2):
        import jax, jax.numpy as jnp
        import numpy as np
        H = 256
        NH = 16
        HD = H // NH
        EPS = 1e-05

        def gelu(x):
            return 0.5 * x * (1.0 + jnp.tanh(0.7978845608028654 * x * (1.0 + 0.044715 * x * x)))

        def layernorm(x, scale, bias):
            m = jnp.mean(x, axis=-1, keepdims=True)
            v = jnp.mean(jnp.square(x - m), axis=-1, keepdims=True)
            return (x - m) * jax.lax.rsqrt(v + EPS) * scale + bias

        def split_heads(x):
            b, s, _ = x.shape
            return x.reshape(b, s, NH, HD).transpose(0, 2, 1, 3)

        def merge_heads(x):
            b, nh, s, hd = x.shape
            return x.transpose(0, 2, 1, 3).reshape(b, s, nh * hd)

        def attention(q, k, v, mask):
            scores = jnp.einsum('bhqd,bhkd->bhqk', q, k) / jnp.sqrt(jnp.float32(HD))
            scores = scores * mask - 10000.0 * (1.0 - mask)
            probs = jax.nn.softmax(scores, axis=-1)
            return jnp.einsum('bhqk,bhkd->bhqd', probs, v)
        ln_out = layernorm(hidden_states, ln1_s, ln1_b)
        qkv = ln_out @ w_qkv + b_qkv
        q, k, v = jnp.split(qkv, 3, axis=-1)
        ctx = merge_heads(attention(split_heads(q), split_heads(k), split_heads(v), ltor_mask))
        attn_out = ctx @ w_ao + b_ao
        x = hidden_states + attn_out
        ln_out = layernorm(x, ln2_s, ln2_b)
        q = ln_out @ w_q + b_q
        kv = encoder_states @ w_kv + b_kv
        k, v = jnp.split(kv, 2, axis=-1)
        ctx = merge_heads(attention(split_heads(q), split_heads(k), split_heads(v), cross_mask))
        cross_out = ctx @ w_co + b_co
        x = x + cross_out
        ln_out = layernorm(x, ln3_s, ln3_b)
        mlp_out = gelu(ln_out @ w1 + b1) @ w2 + b2
        return x + mlp_out

    def _L3_xattn_ref(x, state, ln1_w, ln1_b, ln2_w, ln2_b, maa_x, maa_w1, maa_w2, maa_stack, time_decay, td_w1, td_w2, u, Wr, Wk, Wv, Wg, Wo, gn_w, gn_b, ffn_maa_k, ffn_maa_r, Wfk, Wfr, Wfv):
        import jax, jax.numpy as jnp
        import numpy as np
        E, H, L, B = (256, 32, 128, 4)
        S = E // H
        DM, DD = (32, 64)

        def _ln(x, w, b, eps=1e-05):
            m = x.mean(-1, keepdims=True)
            v = ((x - m) ** 2).mean(-1, keepdims=True)
            return (x - m) / jnp.sqrt(v + eps) * w + b

        def _block(x, state, ln1_w, ln1_b, ln2_w, ln2_b, maa_x, maa_w1, maa_w2, maa_stack, time_decay, td_w1, td_w2, u, Wr, Wk, Wv, Wg, Wo, gn_w, gn_b, ffn_maa_k, ffn_maa_r, Wfk, Wfr, Wfv):
            b, l, e = x.shape
            h = u.shape[0]
            s_ = e // h
            xa = _ln(x, ln1_w, ln1_b)
            sx = jnp.concatenate([state[:, 1:2] - xa[:, :1], xa[:, :-1] - xa[:, 1:]], axis=1)
            xxx = jnp.tanh((xa + sx * maa_x) @ maa_w1).reshape(b, l, 5, DM)
            xxx = jnp.einsum('blfd,fde->blfe', xxx, maa_w2)
            xm = xa[:, :, None] + sx[:, :, None] * (maa_stack + xxx)
            xk, xw, xv, xr, xg = (xm[:, :, j] for j in range(5))
            w = jnp.exp(-jnp.exp(time_decay + jnp.tanh(xw @ td_w1) @ td_w2)).reshape(b, l, h, s_)
            r = (xr @ Wr.T).reshape(b, l, h, s_)
            k = (xk @ Wk.T).reshape(b, l, h, s_)
            v = (xv @ Wv.T).reshape(b, l, h, s_)
            g = jax.nn.silu(xg @ Wg.T)
            s0 = state[:, 2:2 + s_].reshape(b, h, s_, s_)

            def step(s, rkvw):
                r_t, k_t, v_t, w_t = rkvw
                a = k_t[..., :, None] * v_t[..., None, :]
                out = jnp.einsum('bhi,bhij->bhj', r_t, u * a + s)
                s = a + w_t[..., :, None] * s
                return (s, out)
            rkvw = tuple((jnp.moveaxis(t, 1, 0) for t in (r, k, v, w)))
            _, out = jax.lax.scan(step, s0, rkvw)
            out = jnp.moveaxis(out, 0, 1).reshape(b, l, e)
            og = out.reshape(b, l, h, s_)
            m = og.mean(-1, keepdims=True)
            va = ((og - m) ** 2).mean(-1, keepdims=True)
            og = ((og - m) / jnp.sqrt(va + 1e-05)).reshape(b, l, e) * gn_w + gn_b
            x1 = x + og * g @ Wo.T
            xc = _ln(x1, ln2_w, ln2_b)
            sx2 = jnp.concatenate([state[:, 0:1] - xc[:, :1], xc[:, :-1] - xc[:, 1:]], axis=1)
            xk2 = xc + sx2 * ffn_maa_k
            xr2 = xc + sx2 * ffn_maa_r
            rr = jax.nn.sigmoid(xr2 @ Wfr.T)
            kk = jnp.square(jax.nn.relu(xk2 @ Wfk.T))
            return x1 + rr * (kk @ Wfv.T)
        return _block(x, state, ln1_w, ln1_b, ln2_w, ln2_b, maa_x, maa_w1, maa_w2, maa_stack, time_decay, td_w1, td_w2, u, Wr, Wk, Wv, Wg, Wo, gn_w, gn_b, ffn_maa_k, ffn_maa_r, Wfk, Wfr, Wfv)
    x = _L0_xattn_ref(x, ctx_2048, L0_xattn_theta_w, L0_xattn_theta_b, L0_xattn_phi_w, L0_xattn_phi_b, L0_xattn_g_w, L0_xattn_g_b, L0_xattn_w_w, L0_xattn_w_b, L0_xattn_bn_gamma, L0_xattn_bn_beta, L0_xattn_bn_mean, L0_xattn_bn_var)
    x = _L1_xattn_ref(x, mask_Bx1x2048_bf1, ctx_2048, mask_Bx1x2048_bf1, L1_xattn_Wq, L1_xattn_bq, L1_xattn_Wk, L1_xattn_bk, L1_xattn_Wv, L1_xattn_bv)
    x = _L2_xattn_ref(x, ctx_2048, mask_1x1xSxS2_fc1, mask_Bx1xSxS2_ff1, L2_xattn_ln1_s, L2_xattn_ln1_b, L2_xattn_w_qkv, L2_xattn_b_qkv, L2_xattn_w_ao, L2_xattn_b_ao, L2_xattn_ln2_s, L2_xattn_ln2_b, L2_xattn_w_q, L2_xattn_b_q, L2_xattn_w_kv, L2_xattn_b_kv, L2_xattn_w_co, L2_xattn_b_co, L2_xattn_ln3_s, L2_xattn_ln3_b, L2_xattn_w1, L2_xattn_b1, L2_xattn_w2, L2_xattn_b2)
    x = _L3_xattn_ref(x, ctx_2048, L3_xattn_ln1_w, L3_xattn_ln1_b, L3_xattn_ln2_w, L3_xattn_ln2_b, L3_xattn_maa_x, L3_xattn_maa_w1, L3_xattn_maa_w2, L3_xattn_maa_stack, L3_xattn_time_decay, L3_xattn_td_w1, L3_xattn_td_w2, L3_xattn_u, L3_xattn_Wr, L3_xattn_Wk, L3_xattn_Wv, L3_xattn_Wg, L3_xattn_Wo, L3_xattn_gn_w, L3_xattn_gn_b, L3_xattn_ffn_maa_k, L3_xattn_ffn_maa_r, L3_xattn_Wfk, L3_xattn_Wfr, L3_xattn_Wfv)
    return x

_drawn_inputs = setup_inputs


def setup_inputs(seed=0):
    import zlib

    import numpy as np

    out = dict(_drawn_inputs(seed))
    spreads = {'L1_xattn_bq': (0.0, 0.1),
     'L1_xattn_bk': (0.0, 2.0),
     'L1_xattn_bv': (0.0, 0.353),
     'L2_xattn_ln1_s': (1.0, 0.6),
     'L2_xattn_ln1_b': (0.0, 0.8),
     'L2_xattn_b_qkv': (0.0, 0.295),
     'L2_xattn_b_ao': (0.0, 0.1),
     'L2_xattn_ln2_s': (1.0, 0.6),
     'L2_xattn_ln2_b': (0.0, 2.0),
     'L2_xattn_b_q': (0.0, 2.0),
     'L2_xattn_b_kv': (0.0, 0.271),
     'L2_xattn_b_co': (0.0, 0.1),
     'L2_xattn_ln3_s': (1.0, 0.6),
     'L2_xattn_ln3_b': (0.0, 0.697),
     'L2_xattn_b1': (0.0, 0.1),
     'L2_xattn_b2': (0.0, 0.1),
     'L3_xattn_ln1_w': (1.0, 0.583),
     'L3_xattn_ln1_b': (0.0, 0.583),
     'L3_xattn_ln2_w': (1.0, 0.6),
     'L3_xattn_ln2_b': (0.0, 0.8),
     'L3_xattn_gn_w': (1.0, 0.6),
     'L3_xattn_gn_b': (0.0, 0.8)}
    factors = {'L0_xattn_theta_w': 8.0,
     'L0_xattn_theta_b': 8.0,
     'L0_xattn_phi_w': 8.0,
     'L0_xattn_phi_b': 8.0,
     'L0_xattn_g_w': 8.0,
     'L0_xattn_g_b': 8.0,
     'L0_xattn_w_w': 8.0,
     'L0_xattn_w_b': 7.013,
     'L2_xattn_w_qkv': 4.616,
     'L2_xattn_w_q': 8.0,
     'L3_xattn_maa_x': 8.0,
     'L3_xattn_maa_w1': 8.0,
     'L3_xattn_maa_w2': 8.0,
     'L3_xattn_maa_stack': 3.023,
     'L3_xattn_time_decay': 2.994,
     'L3_xattn_td_w1': 8.0,
     'L3_xattn_td_w2': 8.0,
     'L3_xattn_u': 6.135,
     'L3_xattn_ffn_maa_k': 8.0,
     'L3_xattn_ffn_maa_r': 8.0,
     'L3_xattn_Wfk': 3.015,
     'L3_xattn_Wfr': 8.0,
     'L3_xattn_Wfv': 2.778}
    for name, (base, spread) in spreads.items():
        noise = np.random.default_rng([zlib.crc32(name.encode()), seed]).standard_normal(out[name].shape)
        drawn = base * np.exp(spread * noise) if base else spread * noise
        out[name] = jnp.asarray(drawn.astype(out[name].dtype))
    for name, factor in factors.items():
        out[name] = (out[name] * factor).astype(out[name].dtype)
    return out
```

```python
from contextlib import ExitStack

import concourse.bass as bass
from concourse import mybir
import numpy as np

F32 = mybir.dt.float32
BF16 = mybir.dt.bfloat16
U8 = mybir.dt.uint8
ALU = mybir.AluOpType
ACT = mybir.ActivationFunctionType
AX = mybir.AxisListType

P = 128
NB = 8
PAIR = 2
TRIPS = NB // PAIR
C = 128
N = 256
T = PAIR * C
CI = 64
H1, D1 = 16, 8
H2, D2 = 16, 16
G = 4
HT = H2 // G
FF = 4 * N
H3, D3 = 32, 8
HC = P // D3
NF, DM, DD = 5, 32, 64
EPS = 1e-5
VC = 2 * D1 + 1
NSPLIT = 3
KSTACK = NSPLIT * NSPLIT * D1
ROW_MASK = KSTACK
ROW_MAX = 96
K_SCORES = ROW_MAX
K_SHIFTED = ROW_MAX + NSPLIT

COLS = {}
for _name, _n in (("bn_gamma", 1), ("bn_beta", 1), ("bn_mean", 1), ("bn_var", 1), ("w_b", 1), ("bq1", 1), ("bk1", 1),
                  ("theta_b", 1), ("ln1_s", 2), ("ln1_b", 2), ("ln2_s", 2), ("ln2_b", 2), ("ln3_s", 2), ("ln3_b", 2),
                  ("bq_self", 4), ("bk_self", 4), ("bq_cross", 4), ("bk_cross", 4), ("b1", 8),
                  ("l3ln1_s", 2), ("l3ln1_b", 2), ("l3ln2_s", 2), ("l3ln2_b", 2), ("maa_x", 2), ("stack", 10),
                  ("decay", 2), ("u", 2), ("gn_w", 2), ("gn_b", 2), ("mk", 2), ("mr", 2)):
    COLS[_name] = (sum(n for _, n in COLS.values()), _n)
NCOL = sum(n for _, n in COLS.values())
ROWS = {}
for _name, _n in (("phi_g_b", 128), ("bv1", 128), ("bv_self", 256), ("bv_cross", 256), ("b_ao", 256), ("b_co", 256),
                  ("b2", 256)):
    ROWS[_name] = (sum(n for _, n in ROWS.values()), _n)
NROW = sum(n for _, n in ROWS.values())

CHAIN = {"dve_a": 32, "dve_b": 41, "act_b": 1}


def four_layers(nc, x, ctxt, kv_mask, self_mask, cross_mask, cols, rows, wa, ww_t, theta_w, wh, wo, w_ff1, w_ff2,
                w3, maa_w1, maa_w2, td_w1, td_w2, sel, gather, out):
    with ExitStack() as stack:
        def sb(name, shape, dt=F32):
            return stack.enter_context(nc.sbuf_tensor(name, shape, dt))

        per_trip = {}

        def sem(name, n=1):
            s = stack.enter_context(nc.semaphore(name))
            per_trip[name] = n
            names[id(s)] = name
            keep.append(s)
            return s

        names, keep = {}, []

        def due(s, it, k):
            return it * per_trip[names[id(s)]] + k

        q_dram = nc.dram_tensor("q_parts", (NSPLIT, C, PAIR * N), BF16, kind="Internal").ap()
        k_dram = nc.dram_tensor("k_parts", (NSPLIT, C, PAIR * N), BF16, kind="Internal").ap()
        max_dram = nc.dram_tensor("max_parts", (PAIR, H1, NSPLIT, N), BF16, kind="Internal").ap()
        mask_dram = nc.dram_tensor("mask_rows", (H1, PAIR * N), BF16, kind="Internal").ap()

        col = sb("col", [P, NCOL])
        row = sb("row", [P, NROW])
        WA = sb("WA", [P, 5, 128])
        WWT = sb("WWT", [CI, 128])
        THW = sb("THW", [CI, 128])
        WH = sb("WH", [P, 2, 6 * N])
        WO = sb("WO", [P, 2, HT, N])
        W1 = sb("W1", [P, 2, FF])
        W2 = sb("W2", [P, FF // P, N])
        W3 = sb("W3", [P, 2, 8, N])
        MW1 = sb("MW1", [P, 2, NF * DM])
        MW2 = sb("MW2", [P, N])
        MW2B = sb("MW2B", [DM, N])
        TW1 = sb("TW1", [P, 2, DD])
        TW2 = sb("TW2", [DD, N])
        SEL = sb("SEL", [P, 3 + D3, 128])
        GATHER = sb("GATHER", [P, P + D3 - 1])
        ident = sb("ident", [P, P])
        ones = sb("ones", [P, 32])
        bn_s = sb("bn_s", [P, 3])
        bq1s = sb("bq1s", [P, 1])

        def cv(name, i=0, parts=P):
            o = COLS[name][0] + i
            return col[0:parts, o:o + 1]

        def rv(name):
            o, n = ROWS[name]
            return row[:, o:o + n]

        X0 = sb("X0", [P, PAIR, N])
        CTX = sb("CTX", [P, PAIR, N])
        MASK8 = sb("MASK8", [P, PAIR, N], U8)
        MF = sb("MF", [P, PAIR, N])
        MBIAS = sb("MBIAS", [P, PAIR * N], BF16)
        MT = sb("MT", [CI, PAIR, CI])
        AT = sb("AT", [CI, PAIR, 128])
        BT = sb("BT", [P, PAIR, 128])
        SH = sb("SH", [P, PAIR])
        X1 = sb("X1", [P, PAIR, N])
        QS = sb("QS", [P, H1, PAIR * N], BF16)
        KS = sb("KS", [P, H1, PAIR * N], BF16)
        VV = sb("VV", [P, PAIR * 2, H1 * VC + 32 - VC])
        VH = VV[:, :, 0:H1 * VC].rearrange("p a (h c) -> p a h c", c=VC)
        MX = sb("MX", [P, PAIR, 2, H1])
        NMP = sb("NMP", [H1, NSPLIT, N], BF16)
        AREA_A = sb("AREA_A", [P, 2 * G * 2 * N])
        PT = AREA_A[:, :].rearrange("p (s k n) -> p s k n", s=2 * G, k=2)
        QK = AREA_A[:, 0:1024].rearrange("p (i n) -> p i n", i=2)
        RES = AREA_A[:, 1024:2048].rearrange("p (i n) -> p i n", i=2)
        QKP = AREA_A[:, 2048:3584].bitcast(BF16).rearrange("p (i s n) -> p i s n", i=2, s=NSPLIT)
        PG = AREA_A[:, 3584:4096].rearrange("p (a n) -> p a n", n=128)
        OT = sb("OT", [P, HT, N])
        NM = OT[0:H1, 0:2, :]
        SQ = OT[:, 0:2, :].rearrange("p a (b n) -> p (a b) n", n=128)
        RSUM = sb("RSUM", [P, H1])
        MN = sb("MN", [P, PAIR * 2, 128])
        EX = CTX[:, :, :].rearrange("p b (q c) -> p (b q) c", q=2)
        IST = sb("IST", [P, 8, PAIR])
        XN = X0
        ENC = sb("ENC", [P, 2, T])
        X2 = sb("X2", [P, PAIR, N])

        AREA_B = sb("AREA_B", [P, 6144])
        QT = AREA_B[:, 0:1024].rearrange("p (t n) -> p t n", t=HT)
        KT = AREA_B[:, 1024:2048].rearrange("p (t n) -> p t n", t=HT)
        SM = AREA_B[:, 2048:4096].rearrange("p (h k) -> p h k", h=H2)
        PT2 = SM
        HF = AREA_B[:, 2048:4096].rearrange("p (o n) -> p o n", n=T)
        RS2 = AREA_B[:, 4096:4608].rearrange("p (t n) -> p t n", t=HT)
        CT2 = AREA_B[:, 4608:5120].rearrange("p (t n) -> p t n", t=HT)
        XMX = AREA_B[:, 0:2560].rearrange("p (f e n) -> p f e n", f=NF, e=2)
        KV3 = AREA_B[:, 0:2048].rearrange("p (j b n) -> p j b n", j=D3, b=PAIR)
        ST3 = AREA_B[:, 2048:6144].rearrange("p (e j n) -> p e j n", e=2, j=D3)
        SMASK = sb("SMASK", [P, C])
        SFILL = sb("SFILL", [P, C])
        CMASK = sb("CMASK", [P, PAIR, C])
        CFILL = sb("CFILL", [P, PAIR, C])
        X3 = sb("X3", [P, PAIR, N])
        XH = sb("XH", [P, PAIR, N])
        BST = sb("BST", [P, PAIR, 6])
        BMV = sb("BMV", [P, PAIR, 2])
        VE = sb("VE", [P, PAIR])
        cell = sb("cell", [P, 1])
        SDV = sb("SDV", [P, PAIR])
        RSD = sb("RSD", [P, PAIR])
        LNT = sb("LNT", [P, 2, T])
        V2 = sb("V2", [P, PAIR, N + 32 - D2])
        MX2 = sb("MX2", [P, H2])
        NMX2 = sb("NMX2", [P, H2])
        SX = sb("SX", [P, 2, T])
        XI = sb("XI", [P, 2, T])
        TX = sb("TX", [P, T])
        TD = TX[0:DD, :]
        TXB = sb("TXB", [DM, T])
        WS = sb("WS", [P, 2, PAIR, C])
        R3 = sb("R3", [P, 2, T])
        K3 = sb("K3", [P, 2, T])
        V3 = sb("V3", [P, 2, T])
        G3 = sb("G3", [P, 2, T])
        S0 = sb("S0", [P, 2, PAIR, D3])
        RUK = sb("RUK", [P, 2, T])
        EX3 = RUK
        O3 = sb("O3", [P, 2, T])
        XR = O3
        Q3 = sb("Q3", [P, 2, T])
        FR = R3

        PA = stack.enter_context(nc.psum_tensor("PA", [P, 4, 512], F32))
        PB = stack.enter_context(nc.psum_tensor("PB", [P, 4, 512], F32))

        wa_in, wb_in = sem("wa_in"), sem("wb_in")
        const_step, const_ready, bn_ready = sem("const_step"), sem("const_ready"), sem("bn_ready")
        zero_ready = sem("zero_ready")
        bn_sd, bn_var1 = sem("bn_sd"), sem("bn_var1")
        pair_in, out_stored = sem("pair_in", 3 * 16), sem("out_stored", 16)
        cross_in = sem("cross_in", 16)
        state_in = sem("state_in", PAIR * 2 * 16)
        parts_out, mask_out = sem("parts_out", 2 * 16), sem("mask_out", 16)
        stack_in = sem("stack_in", 19 * 16)
        maxp_out, maxp_in = sem("maxp_out", PAIR * 16), [sem(f"maxp_in{b}", 16) for b in range(PAIR)]
        enc_tr, enc_ready = sem("enc_tr"), sem("enc_ready")
        pg_mm, pg_ready = sem("pg_mm"), sem("pg_ready")
        mt_mm, mt_ready = sem("mt_mm"), sem("mt_ready")
        at_mm, at_ready = sem("at_mm"), sem("at_ready")
        bt_mm, bt_ready, sh_ready = sem("bt_mm"), sem("bt_ready"), sem("sh_ready")
        y_mm, y_added, x1_ready = sem("y_mm"), sem("y_added"), sem("x1_ready")
        k_mm, q_mm, v_mm = sem("k_mm"), sem("q_mm"), sem("v_mm")
        k_ready, q_ready, v_ready = sem("k_ready"), sem("q_ready"), sem("v_ready")
        kp_ready, qp_ready, mbias_ready = sem("kp_ready"), sem("qp_ready"), sem("mbias_ready")
        vsq_ready = sem("vsq_ready")
        s_mm, s_max = sem("s_mm", PAIR * H1), sem("s_max", PAIR * H1)
        m_tr, m_parts = sem("m_tr", PAIR), sem("m_parts", PAIR)
        t_mm, t_exp = sem("t_mm", PAIR * H1), sem("t_exp", PAIR * H1)
        pv_mm, pv_out = sem("pv_mm", PAIR * HT), sem("pv_out", PAIR * HT)
        ot_tr, ot_out = sem("ot_tr", PAIR * 2), sem("ot_out", PAIR * 2)
        var_ready, std_ready = sem("var_ready"), sem("std_ready")
        ivar_ready, istd_ready = sem("ivar_ready"), sem("istd_ready")
        ms_tr, x2_ready = sem("ms_tr"), sem("x2_ready")
        ln_var, ln_sd, ln_hat = sem("ln_var", 5), sem("ln_sd", 5), sem("ln_hat", 5)
        ln_tr, ln_ready = sem("ln_tr", 5), sem("ln_ready", 5)
        qp_mm, kp_mm, vp_mm = sem("qp_mm", 2), sem("kp_mm", 2), sem("vp_mm", 2)
        qt_ready, kt_ready, v2_ready = sem("qt_ready", 2), sem("kt_ready", 2), sem("v2_ready", 2)
        sc_mm, sc_masked, sc_filled = sem("sc_mm", 4), sem("sc_masked", 4), sem("sc_filled", 4)
        sc_nmax, sc_exp = sem("sc_nmax", 4), sem("sc_exp", 4)
        p_tr, p_out_act, p_out_dve = sem("p_tr", 4), sem("p_out_act", 4), sem("p_out_dve", 4)
        ctx_mm, ctx_ready, ao_mm = sem("ctx_mm", 4), sem("ctx_ready", 4), sem("ao_mm", 4)
        res_half, res_ready = sem("res_half", 4), sem("res_ready", 2)
        ff_mm, ff_act, ff2_mm, x4_ready = sem("ff_mm", 8), sem("ff_act", 8), sem("ff2_mm"), sem("x4_ready")
        sx_ready, xi_ready = sem("sx_ready", 2), sem("xi_ready")
        tx_mm, tx_ready = sem("tx_mm"), sem("tx_ready")
        mix_mm, mix_used, mix_ready = sem("mix_mm", NF), sem("mix_used", NF), sem("mix_ready", NF)
        td1_mm, td1_ready, td2_mm, td2_used, w_ready = sem("td1_mm"), sem("td1_ready"), sem("td2_mm"), sem("td2_used"), sem("w_ready")
        v3_mm, k3_mm, r3_mm, g3_mm = sem("v3_mm"), sem("k3_mm"), sem("r3_mm"), sem("g3_mm")
        v3_ready, k3_ready, r3_ready = sem("v3_ready"), sem("k3_ready"), sem("r3_ready")
        g3_exp, g3_ready = sem("g3_exp"), sem("g3_ready")
        sp_mm, kv_ready = sem("sp_mm", 4), sem("kv_ready", 4)
        sc_done, y3_ready, ruk_ready = sem("sc_done", 2), sem("y3_ready", 2), sem("ruk_ready")
        o3_mm, bonus_mm, o3_ready = sem("o3_mm"), sem("bonus_mm"), sem("o3_ready")
        cen_mm, cen_sq, gvar_mm, gvar_ready, gsd_ready, og_ready = (
            sem("cen_mm"), sem("cen_sq"), sem("gvar_mm"), sem("gvar_ready"), sem("gsd_ready"), sem("og_ready"))
        wo_mm, x5_ready = sem("wo_mm"), sem("x5_ready")
        xk_ready, fk_mm, fr_mm = sem("xk_ready"), sem("fk_mm"), sem("fr_mm")
        fk_relu, fk_ready, fr_exp, fv_mm, yo_ready = sem("fk_relu"), sem("fk_ready"), sem("fr_exp"), sem("fv_mm"), sem("yo_ready")
        chain_sem = {k: sem(k, n) for k, n in CHAIN.items()}
        chain_at = {}

        def link(eng, name, it, ins):
            chain_at[name] = chain_at.get(name, 0) + 1
            ins.then_inc(chain_sem[name], 1)
            eng.wait_ge(chain_sem[name], it * CHAIN[name] + chain_at[name])

        def chain_end(name):
            assert chain_at.get(name, 0) == CHAIN[name], (name, chain_at.get(name, 0))
            chain_at[name] = 0

        block = stack.enter_context(nc.Block())

        def sp_pair_loads(sp, at):
            sp.dma_start(CTX[:, :, :], ctxt[bass.ds(at, PAIR)].rearrange("b c n -> c b n")).then_inc(pair_in, 16)
            sp.dma_start(X0[:, :, :], x[bass.ds(at, PAIR)].rearrange("b c n -> c b n")).then_inc(pair_in, 16)
            sp.dma_start(MASK8[:, :, :], kv_mask[bass.ds(at, PAIR)].partition_broadcast(P)).then_inc(pair_in, 16)
            sp.dma_start(CMASK[:, :, :], cross_mask[bass.ds(at, PAIR)].rearrange("b s t -> s b t")).then_inc(cross_in, 16)
            for b in range(PAIR):
                for e in range(2):
                    sp.dma_start(S0[:, e, b, :], ctxt[bass.ds(at + b, 1), 2:2 + D3, :].rearrange("o r n -> (o r n)")
                                 .rearrange("(e p j) -> e p j", e=2, j=D3)[e]).then_inc(state_in, 16)

        def sp_stage_a(sp, it):
            sp.wait_ge(mbias_ready, due(mbias_ready, it, 1))
            sp.dma_start(mask_dram, MBIAS[0:H1, :]).then_inc(mask_out, 16)
            sp.wait_ge(kp_ready, due(kp_ready, it, 1))
            sp.dma_start(k_dram.rearrange("s c n -> c s n"), QKP[:, 1, :, :]).then_inc(parts_out, 16)
            sp.wait_ge(mask_out, due(mask_out, it, 16))
            sp.dma_start(KS[ROW_MASK:ROW_MASK + 1, :, :], mask_dram.rearrange("(o h) n -> o h n", o=1)).then_inc(stack_in, 16)
            sp.wait_ge(parts_out, due(parts_out, it, 16))
            for i in range(NSPLIT * NSPLIT):
                sp.dma_start(KS[D1 * i:D1 * i + D1, :, :],
                             k_dram[i % NSPLIT].rearrange("(h d) n -> d h n", d=D1)).then_inc(stack_in, 16)
            sp.wait_ge(qp_ready, due(qp_ready, it, 1))
            sp.dma_start(q_dram.rearrange("s c n -> c s n"), QKP[:, 0, :, :]).then_inc(parts_out, 16)
            sp.wait_ge(parts_out, due(parts_out, it, 32))
            for i in range(NSPLIT * NSPLIT):
                sp.dma_start(QS[D1 * i:D1 * i + D1, :, :],
                             q_dram[i // NSPLIT].rearrange("(h d) n -> d h n", d=D1)).then_inc(stack_in, 16)
            for b in range(PAIR):
                sp.wait_ge(m_parts, due(m_parts, it, b + 1))
                sp.dma_start(max_dram[b], NMP[:, :, :]).then_inc(maxp_out, 16)
                sp.wait_ge(maxp_out, due(maxp_out, it, 16 * (b + 1)))
                sp.dma_start(QS[ROW_MAX:ROW_MAX + NSPLIT, :, b * N:(b + 1) * N],
                             max_dram[b].rearrange("h s n -> s h n")).then_inc(maxp_in[b], 16)

        @block.sync
        def _(sp):
            sp.dma_start(col[:, :], cols).then_inc(wa_in, 16)
            sp.dma_start(row[:, :], rows.partition_broadcast(P)).then_inc(wa_in, 16)
            sp.dma_start(WA[:, 0:4, :], wa).then_inc(wa_in, 16)
            sp.dma_start(WWT[:, :], ww_t).then_inc(wa_in, 16)
            sp.dma_start(THW[:, :], theta_w).then_inc(wa_in, 16)
            sp.wait_ge(const_ready, 1)
            sp.wait_ge(zero_ready, 3)
            with sp.Fori(0, TRIPS) as it:
                at = sp.snap(it * PAIR)
                sp_pair_loads(sp, at)
                sp_stage_a(sp, it)
                sp.wait_ge(yo_ready, due(yo_ready, it, 1))
                sp.dma_start(out[bass.ds(at, PAIR)].rearrange("b s n -> s b n"), FR[:, :, :]).then_inc(out_stored, 16)
            sp.wait_ge(out_stored, 16 * TRIPS)

        def pool_stage_a(pool, it):
            pool.wait_ge(v_ready, due(v_ready, it, 1))
            nc.gpsimd.tensor_tensor(VH[:, :, :, D1:2 * D1], VH[:, :, :, 0:D1], VH[:, :, :, 0:D1], ALU.mult).then_inc(vsq_ready, 1)

        def pool_stage_b(pool, it):
            for u in range(4):
                a, b = u // 2, u % 2
                fill = SFILL[:, :] if a == 0 else CFILL[:, b, :]
                pool.wait_ge(sc_masked, due(sc_masked, it, u + 1))
                nc.gpsimd.tensor_tensor(SM[:, :, :], SM[:, :, :], fill.unsqueeze(1).to_broadcast([P, H2, C]),
                                        ALU.add).then_inc(sc_filled, 1)
            for f in range(NF):
                pool.wait_ge(mix_used, due(mix_used, it, f + 1))
                nc.gpsimd.tensor_tensor(XMX[:, f, :, :], XMX[:, f, :, :], LNT[:, :, :], ALU.add).then_inc(mix_ready, 1)
            pool.wait_ge(fk_relu, due(fk_relu, it, 1))
            nc.gpsimd.tensor_tensor(Q3[:, :, :], Q3[:, :, :], Q3[:, :, :], ALU.mult).then_inc(fk_ready, 1)

        @block.gpsimd
        def _(pool):
            pool.memset(ident[:, :], 0.0).then_inc(const_step, 1)
            pool.wait_ge(const_step, 1)
            pool.affine_select(out=ident[:, :], in_=ident[:, :], compare_op=ALU.not_equal, fill=1.0, base=0,
                               pattern=[[-1, P]], channel_multiplier=1).then_inc(const_step, 1)
            pool.wait_ge(zero_ready, 1)
            pool.wait_ge(const_step, 2)
            pool.affine_select(out=QS[64:ROW_MAX, :, :], in_=QS[64:ROW_MAX, :, :], compare_op=ALU.not_equal, fill=1.0,
                               base=64 - ROW_MASK, pattern=[[0, H1], [0, PAIR * N]], channel_multiplier=1).then_inc(const_ready, 1)
            with pool.Fori(0, TRIPS) as it:
                pool_stage_a(pool, it)
                pool_stage_b(pool, it)
                pool.wait_ge(out_stored, due(out_stored, it, 16))

        def act_stage_a(act, it):
            act.wait_ge(enc_tr, due(enc_tr, it, 1))
            nc.scalar.activation(ENC[:, :, :], PA[:, 3, :], ACT.Copy).then_inc(enc_ready, 1)
            act.wait_ge(mt_mm, due(mt_mm, it, 1))
            nc.scalar.activation(MT[:, :, :], PA[0:CI, 1, 0:PAIR * CI], ACT.Copy, scale=1.0 / N).then_inc(mt_ready, 1)
            act.wait_ge(k_mm, due(k_mm, it, 1))
            nc.scalar.activation(QK[:, 1, :], PA[:, 3, :], ACT.Identity, bias=cv("bk1")).then_inc(k_ready, 1)
            act.wait_ge(bt_mm, due(bt_mm, it, 1))
            nc.scalar.activation(BT[:, :, :], PA[:, 1, 0:N], ACT.Copy).then_inc(bt_ready, 1)
            act.wait_ge(y_added, due(y_added, it, 1))
            for b in range(PAIR):
                last = nc.scalar.activation(X1[:, b, :], X1[:, b, :], ACT.Identity, bias=SH[:, b:b + 1])
            last.then_inc(x1_ready, 1)
            act.wait_ge(q_mm, due(q_mm, it, 1))
            nc.scalar.activation(QK[:, 0, :], PA[:, 1, :], ACT.Identity, bias=bq1s[:, :], scale=float(D1) ** -0.5).then_inc(q_ready, 1)
            act.wait_ge(ivar_ready, due(ivar_ready, it, 1))
            nc.scalar.activation(IST[:, 6, :], IST[:, 5, :], ACT.Sqrt).then_inc(istd_ready, 1)
            for u in range(PAIR * H1):
                act.wait_ge(t_mm, due(t_mm, it, u + 1))
                if u >= 2 * G:
                    act.wait_ge(pv_mm, due(pv_mm, it, (u - 2 * G) // G + 1))
                nc.scalar.activation(PT[:, u % (2 * G), :, :], PA[:, u % 2, :], ACT.Exp).then_inc(t_exp, 1)
            act.wait_ge(var_ready, due(var_ready, it, 1))
            nc.scalar.activation(SQ[:, :, :], EX[:, :, :], ACT.Sqrt).then_inc(std_ready, 1)

        def act_ln(act, it, i, s, b):
            act.wait_ge(ln_var, due(ln_var, it, i + 1))
            nc.scalar.activation(SDV[:, :], VE[:, :], ACT.Sqrt).then_inc(ln_sd, 1)
            act.wait_ge(ln_tr, due(ln_tr, it, i + 1))
            for c in range(2):
                last = nc.scalar.activation(LNT[:, c, :], PB[:, 0, c * T:(c + 1) * T], ACT.Identity,
                                            bias=cv(b, c), scale=cv(s, c))
            last.then_inc(ln_ready, 1)

        def act_stage_b(act, it):
            for a in range(2):
                act_ln(act, it, a, *(("ln1_s", "ln1_b"), ("ln2_s", "ln2_b"))[a])
                act.wait_ge(kp_mm, due(kp_mm, it, a + 1))
                for t in range(HT):
                    last = nc.scalar.activation(KT[:, t, :], PB[:, 2 + t // 2, (t % 2) * T:(t % 2 + 1) * T], ACT.Identity,
                                                bias=cv(("bk_self", "bk_cross")[a], t))
                last.then_inc(kt_ready, 1)
                for b in range(PAIR):
                    u = 2 * a + b
                    act.wait_ge(sc_nmax, due(sc_nmax, it, u + 1))
                    for h in range(H2):
                        last = nc.scalar.activation(SM[:, h, :], SM[:, h, :], ACT.Exp, bias=NMX2[:, h:h + 1])
                    last.then_inc(sc_exp, 1)
                    act.wait_ge(p_tr, due(p_tr, it, u + 1))
                    nc.scalar.activation(PT2[:, 0:8, :], PB[:, 0:2, :], ACT.Copy).then_inc(p_out_act, 1)
            act_ln(act, it, 2, "ln3_s", "ln3_b")
            for o in range(FF // P):
                act.wait_ge(ff_mm, due(ff_mm, it, o // 2 * 2 + 2))
                nc.scalar.activation(HF[:, o, :], PB[:, o // 2, (o % 2) * T:(o % 2 + 1) * T], ACT.Gelu_apprx_tanh,
                                     bias=cv("b1", o)).then_inc(ff_act, 1)
            act_ln(act, it, 3, "l3ln1_s", "l3ln1_b")
            act.wait_ge(tx_mm, due(tx_mm, it, 1))
            nc.scalar.activation(TX[:, :], PB[:, 0, 0:T], ACT.Tanh)
            nc.scalar.activation(TXB[:, :], PB[0:DM, 0, T:2 * T], ACT.Tanh).then_inc(tx_ready, 1)
            act.wait_ge(td1_mm, due(td1_mm, it, 1))
            nc.scalar.activation(TD[:, :], PB[0:DD, 1, 0:T], ACT.Tanh).then_inc(td1_ready, 1)
            act.wait_ge(td2_mm, due(td2_mm, it, 1))
            for e in range(2):
                last = nc.scalar.activation(EX3[:, e, :], PB[:, 1, e * T:(e + 1) * T], ACT.Exp, bias=cv("decay", e))
            link(act, "act_b", it, last)
            nc.scalar.activation(WS[:, :, :, 1:C].rearrange("p e b t -> p (e b) t"),
                                 EX3[:, :, :].rearrange("p e (b t) -> p (e b) t", b=PAIR)[:, :, 0:C - 1], ACT.Exp,
                                 scale=-1.0).then_inc(w_ready, 1)
            act.wait_ge(k3_mm, due(k3_mm, it, 1))
            nc.scalar.activation(K3[:, :, :], PB[:, 3, :], ACT.Copy).then_inc(k3_ready, 1)
            act.wait_ge(r3_mm, due(r3_mm, it, 1))
            nc.scalar.activation(R3[:, :, :], PB[:, 0, :], ACT.Copy).then_inc(r3_ready, 1)
            act.wait_ge(g3_mm, due(g3_mm, it, 1))
            nc.scalar.activation(Q3[:, :, :], PB[:, 1, :], ACT.Exp, scale=-1.0).then_inc(g3_exp, 1)
            act.wait_ge(cen_mm, due(cen_mm, it, 1))
            nc.scalar.activation(Q3[:, :, :], PB[:, 2, :], ACT.Square).then_inc(cen_sq, 1)
            act.wait_ge(gvar_ready, due(gvar_ready, it, 1))
            nc.scalar.activation(XI[:, :, :], RUK[:, :, :], ACT.Sqrt).then_inc(gsd_ready, 1)
            act_ln(act, it, 4, "l3ln2_s", "l3ln2_b")
            act.wait_ge(fk_mm, due(fk_mm, it, 1))
            nc.scalar.activation(Q3[:, :, :], PB[:, 0, :], ACT.Relu).then_inc(fk_relu, 1)
            act.wait_ge(fr_mm, due(fr_mm, it, 1))
            nc.scalar.activation(FR[:, :, :], PB[:, 1, :], ACT.Exp, scale=-1.0).then_inc(fr_exp, 1)
            chain_end("act_b")

        @block.scalar
        def _(act):
            act.dma_start(WH[:, :, :], wh).then_inc(wb_in, 16)
            act.dma_start(WO[:, :, :, :], wo).then_inc(wb_in, 16)
            act.dma_start(SMASK[:, :], self_mask).then_inc(wb_in, 16)
            act.dma_start(W1[:, :, :], w_ff1).then_inc(wb_in, 16)
            act.dma_start(W2[:, :, :], w_ff2).then_inc(wb_in, 16)
            act.dma_start(W3[:, :, :, :], w3).then_inc(wb_in, 16)
            act.dma_start(MW1[:, :, :], maa_w1.rearrange("(c p) n -> p c n", p=P)).then_inc(wb_in, 16)
            act.dma_start(MW2[:, :], maa_w2[0:P]).then_inc(wb_in, 16)
            act.dma_start(MW2B[:, :], maa_w2[P:P + DM]).then_inc(wb_in, 16)
            act.dma_start(TW1[:, :, :], td_w1.rearrange("(c p) n -> p c n", p=P)).then_inc(wb_in, 16)
            act.dma_start(TW2[:, :], td_w2).then_inc(wb_in, 16)
            act.dma_start(SEL[:, :, :], sel).then_inc(wb_in, 16)
            act.dma_start(GATHER[:, :], gather).then_inc(wb_in, 16)
            act.wait_ge(bn_var1, 1)
            nc.scalar.activation(bn_s[:, 1:2], bn_s[:, 2:3], ACT.Sqrt).then_inc(bn_sd, 1)
            nc.scalar.activation(bq1s[:, :], cv("bq1"), ACT.Copy, scale=float(D1) ** -0.5).then_inc(bn_sd, 1)
            act.wait_ge(bn_sd, 2)
            with act.Fori(0, TRIPS) as it:
                act_stage_a(act, it)
                act_stage_b(act, it)
                act.wait_ge(out_stored, due(out_stored, it, 16))
            act.wait_ge(out_stored, 16 * TRIPS)

        def dve_stage_a(dve, it):
            v = nc.vector

            def step(ins):
                link(dve, "dve_a", it, ins)

            def split(i):
                step(v.tensor_copy(QKP[:, i, 0, :], QK[:, i, :]))
                step(v.tensor_tensor(RES[:, i, :], QK[:, i, :], QKP[:, i, 0, :], ALU.subtract))
                step(v.tensor_copy(QKP[:, i, 1, :], RES[:, i, :]))
                return v.tensor_tensor(QKP[:, i, 2, :], RES[:, i, :], QKP[:, i, 1, :], ALU.subtract)

            dve.wait_ge(pair_in, due(pair_in, it, 48))
            v.tensor_copy(MF[:, :, :], MASK8[:, :, :])
            v.tensor_scalar(MBIAS[:, :].rearrange("p (b n) -> p b n", b=PAIR), MASK8[:, :, :], -1.0, 1e30, ALU.add,
                            ALU.mult).then_inc(mbias_ready, 1)
            dve.wait_ge(pg_mm, due(pg_mm, it, 1))
            v.tensor_tensor(PG[:, :, :], PA[:, 0, :].rearrange("p (a n) -> p a n", n=128),
                            rv("phi_g_b").unsqueeze(1).to_broadcast([P, 4, 128]), ALU.add).then_inc(pg_ready, 1)
            dve.wait_ge(at_mm, due(at_mm, it, 1))
            v.tensor_copy(AT[:, :, :], PA[0:CI, 2, 0:N].rearrange("p (b n) -> p b n", b=PAIR)).then_inc(at_ready, 1)
            dve.wait_ge(k_ready, due(k_ready, it, 1))
            split(1).then_inc(kp_ready, 1)
            dve.wait_ge(bt_ready, due(bt_ready, it, 1))
            v.tensor_scalar(SH[:, :], PA[:, 1, N:N + PAIR], bn_s[:, 0:1], bn_s[:, 2:3], ALU.mult, ALU.add).then_inc(sh_ready, 1)
            dve.wait_ge(y_mm, due(y_mm, it, 1))
            v.scalar_tensor_tensor(out=X1[:, :, :], in0=PA[:, 0, :].rearrange("p (b n) -> p b n", b=PAIR), scalar=bn_s[:, 0:1],
                                   in1=X0[:, :, :], op0=ALU.mult, op1=ALU.add).then_inc(y_added, 1)
            dve.wait_ge(v_mm, due(v_mm, it, 1))
            v.tensor_tensor(VH[:, :, :, 0:D1], PA[:, 2, :].rearrange("p (a h d) -> p a h d", a=4, d=D1),
                            rv("bv1").rearrange("p (h d) -> p h d", d=D1).unsqueeze(1).to_broadcast([P, 4, H1, D1]),
                            ALU.add).then_inc(v_ready, 1)
            dve.wait_ge(q_ready, due(q_ready, it, 1))
            split(0).then_inc(qp_ready, 1)
            dve.wait_ge(mbias_ready, due(mbias_ready, it, 1))
            step(v.tensor_tensor(X1[:, :, :], X1[:, :, :], MF[:, :, :], ALU.mult))
            step(v.tensor_tensor(XN[:, :, :], X1[:, :, :], X1[:, :, :], ALU.mult))
            v.tensor_reduce(IST[:, 0, :], MF[:, :, :], AX.X, ALU.add)
            v.tensor_reduce(IST[:, 1, :], X1[:, :, :], AX.X, ALU.add)
            step(v.tensor_reduce(IST[:, 2, :], XN[:, :, :], AX.X, ALU.add))
            step(v.reciprocal(IST[:, 3, :], IST[:, 0, :]))
            step(v.tensor_tensor(IST[:, 4, :], IST[:, 1, :], IST[:, 3, :], ALU.mult))
            v.tensor_tensor(IST[:, 2, :], IST[:, 2, :], IST[:, 3, :], ALU.mult)
            step(v.tensor_tensor(IST[:, 5, :], IST[:, 4, :], IST[:, 4, :], ALU.mult))
            step(v.tensor_tensor(IST[:, 5, :], IST[:, 2, :], IST[:, 5, :], ALU.subtract))
            v.tensor_scalar(IST[:, 5, :], IST[:, 5, :], 0.0, EPS, ALU.max, ALU.add).then_inc(ivar_ready, 1)
            dve.wait_ge(istd_ready, due(istd_ready, it, 1))
            step(v.reciprocal(IST[:, 7, :], IST[:, 6, :]))
            for b in range(PAIR):
                last = v.tensor_scalar(XN[:, b, :], X1[:, b, :], IST[:, 4, b:b + 1], IST[:, 7, b:b + 1], ALU.subtract, ALU.mult)
            step(last)
            step(v.tensor_tensor(XN[:, :, :], XN[:, :, :], MF[:, :, :], ALU.mult))
            for b in range(PAIR):
                for h in range(H1):
                    u = b * H1 + h
                    dve.wait_ge(s_mm, due(s_mm, it, u + 1))
                    v.tensor_reduce(MX[:, b, :, h], PA[:, u % 2, :].rearrange("p (q k) -> p q k", q=2), AX.X,
                                    ALU.max).then_inc(s_max, 1)
                dve.wait_ge(m_tr, due(m_tr, it, b + 1))
                if b:
                    dve.wait_ge(maxp_out, due(maxp_out, it, 16 * b))
                step(v.tensor_scalar(NM[:, 0, :], PA[0:H1, 3, 0:N], -1.0, None, ALU.mult))
                step(v.tensor_copy(NMP[:, 0, :], NM[:, 0, :]))
                step(v.tensor_tensor(NM[:, 1, :], NM[:, 0, :], NMP[:, 0, :], ALU.subtract))
                step(v.tensor_copy(NMP[:, 1, :], NM[:, 1, :]))
                v.tensor_tensor(NMP[:, 2, :], NM[:, 1, :], NMP[:, 1, :], ALU.subtract).then_inc(m_parts, 1)
            for b in range(PAIR):
                for t in range(HT):
                    dve.wait_ge(pv_mm, due(pv_mm, it, b * HT + t + 1))
                    if b and t == 0:
                        dve.wait_ge(ot_tr, due(ot_tr, it, 2 * b))
                    v.tensor_copy(OT[:, t, :], PA[:, 2 + t % 2, 0:N]).then_inc(pv_out, 1)
                for q in range(2):
                    dve.wait_ge(ot_tr, due(ot_tr, it, 2 * b + q + 1))
                    heads = PA[:, 2, :].rearrange("p (h d) -> p h d", d=32)
                    step(v.reciprocal(RSUM[:, :], heads[:, :, 2 * D1]))
                    scale = RSUM[:, :].unsqueeze(2).to_broadcast([P, H1, D1])
                    v.tensor_tensor(MN[:, 2 * b + q, :].rearrange("p (h d) -> p h d", d=D1), heads[:, :, 0:D1], scale, ALU.mult)
                    v.tensor_tensor(EX[:, 2 * b + q, :].rearrange("p (h d) -> p h d", d=D1), heads[:, :, D1:2 * D1], scale,
                                    ALU.mult).then_inc(ot_out, 1)
            dve.wait_ge(ot_out, due(ot_out, it, 4))
            step(v.tensor_tensor(SQ[:, :, :], MN[:, :, :], MN[:, :, :], ALU.mult))
            step(v.tensor_tensor(EX[:, :, :], EX[:, :, :], SQ[:, :, :], ALU.subtract))
            v.tensor_scalar(EX[:, :, :], EX[:, :, :], 0.0, None, ALU.max).then_inc(var_ready, 1)
            dve.wait_ge(ms_tr, due(ms_tr, it, 1))
            step(v.tensor_tensor(XN[:, :, :], XN[:, :, :], PA[:, 3, :].rearrange("p (b n) -> p b n", b=PAIR), ALU.mult))
            step(v.tensor_tensor(XN[:, :, :], XN[:, :, :], PA[:, 2, :].rearrange("p (b n) -> p b n", b=PAIR), ALU.add))
            v.tensor_tensor(X2[:, :, :], XN[:, :, :], MF[:, :, :], ALU.mult).then_inc(x2_ready, 1)
            dve.wait_ge(x2_ready, due(x2_ready, it, 1))
            chain_end("dve_a")

        def dve_stage_b(dve, it):
            v = nc.vector

            def step(ins):
                link(dve, "dve_b", it, ins)

            def ln(i, src):
                for b in range(PAIR):
                    last = v.bn_stats(BST[:, b, :], src[:, b, :])
                step(last)
                v.memset(cell[:, :], 0.0)
                for b in range(PAIR):
                    last = v.bn_aggr(BMV[:, b, :], BST[:, b, :])
                step(last)
                v.tensor_scalar(VE[:, :], BMV[:, :, 1], EPS, None, ALU.add).then_inc(ln_var, 1)
                dve.wait_ge(ln_sd, due(ln_sd, it, i + 1))
                step(v.reciprocal(RSD[:, :], SDV[:, :]))
                for b in range(PAIR):
                    last = v.tensor_scalar(XH[:, b, :], src[:, b, :], BMV[:, b, 0:1], RSD[:, b:b + 1], ALU.subtract, ALU.mult)
                last.then_inc(ln_hat, 1)

            dve.wait_ge(wb_in, 16 * 13)
            dve.wait_ge(cross_in, due(cross_in, it, 16))
            v.tensor_scalar(CFILL[:, :, :], CMASK[:, :, :], -1.0, 10000.0, ALU.add, ALU.mult)
            step(v.tensor_scalar(SFILL[:, :], SMASK[:, :], -1.0, 10000.0, ALU.add, ALU.mult))
            for a in range(2):
                src, dst = ((X2, X3), (X3, X3))[a]
                ln(a, src)
                dve.wait_ge(qp_mm, due(qp_mm, it, a + 1))
                o = COLS[("bq_self", "bq_cross")[a]][0]
                bias = col[:, o:o + HT]
                v.tensor_tensor(QT[:, :, :], PB[:, 0:2, :].rearrange("p x (y n) -> p (x y) n", n=T),
                                bias.unsqueeze(2).to_broadcast([P, HT, T]), ALU.add).then_inc(qt_ready, 1)
                dve.wait_ge(vp_mm, due(vp_mm, it, a + 1))
                v.tensor_tensor(V2[:, :, 0:N].rearrange("p b (h d) -> p b h d", d=D2), PB[:, 0, :].rearrange("p (b h d) -> p b h d", b=PAIR, d=D2),
                                rv(("bv_self", "bv_cross")[a]).rearrange("p (h d) -> p h d", d=D2).unsqueeze(1)
                                .to_broadcast([P, PAIR, H2, D2]), ALU.add).then_inc(v2_ready, 1)
                for b in range(PAIR):
                    u = 2 * a + b
                    mask = SMASK[:, :] if a == 0 else CMASK[:, b, :]
                    dve.wait_ge(sc_mm, due(sc_mm, it, u + 1))
                    v.scalar_tensor_tensor(out=SM[:, :, :], in0=PB[:, :, :].rearrange("p g (t k) -> p (g t) k", k=C),
                                           scalar=float(D2) ** -0.5, in1=mask.unsqueeze(1).to_broadcast([P, H2, C]),
                                           op0=ALU.mult, op1=ALU.mult).then_inc(sc_masked, 1)
                    dve.wait_ge(sc_filled, due(sc_filled, it, u + 1))
                    step(v.tensor_reduce(MX2[:, :], SM[:, :, :], AX.X, ALU.max))
                    v.tensor_scalar(NMX2[:, :], MX2[:, :], -1.0, None, ALU.mult).then_inc(sc_nmax, 1)
                    dve.wait_ge(p_tr, due(p_tr, it, u + 1))
                    v.tensor_copy(PT2[:, 8:16, :], PB[:, 2:4, :].rearrange("p g (t k) -> p (g t) k", k=C)).then_inc(p_out_dve, 1)
                    dve.wait_ge(ctx_mm, due(ctx_mm, it, u + 1))
                    step(v.reciprocal(RS2[:, :, :], PB[:, 1, :].rearrange("p (t k) -> p t k", k=C)))
                    v.tensor_tensor(CT2[:, :, :], PB[:, 0, :].rearrange("p (t k) -> p t k", k=C), RS2[:, :, :],
                                    ALU.mult).then_inc(ctx_ready, 1)
                    dve.wait_ge(ao_mm, due(ao_mm, it, u + 1))
                    v.tensor_tensor(dst[:, b, :], src[:, b, :], PB[:, 2, b * N:(b + 1) * N], ALU.add).then_inc(res_half, 1)
                dve.wait_ge(res_half, due(res_half, it, 2 * a + 2))
                v.tensor_tensor(dst[:, :, :], dst[:, :, :], rv(("b_ao", "b_co")[a]).unsqueeze(1).to_broadcast([P, PAIR, N]),
                                ALU.add).then_inc(res_ready, 1)
                dve.wait_ge(res_ready, due(res_ready, it, a + 1))
            ln(2, X3)
            dve.wait_ge(ff2_mm, due(ff2_mm, it, 1))
            step(v.tensor_tensor(X3[:, :, :], X3[:, :, :], PB[:, 0, :].rearrange("p (b n) -> p b n", b=PAIR), ALU.add))
            v.tensor_tensor(X3[:, :, :], X3[:, :, :], rv("b2").unsqueeze(1).to_broadcast([P, PAIR, N]), ALU.add).then_inc(x4_ready, 1)
            dve.wait_ge(x4_ready, due(x4_ready, it, 1))

            def shift(i):
                dve.wait_ge(ln_ready, due(ln_ready, it, 4 + i))
                new = LNT[:, :, :].rearrange("p e (b t) -> p (e b) t", b=PAIR)
                old = ENC[:, :, :].rearrange("p e (b t) -> p (e b) t", b=PAIR)
                to = SX[:, :, :].rearrange("p e (b t) -> p (e b) t", b=PAIR)
                v.tensor_tensor(to[:, :, 1:C], new[:, :, 0:C - 1], new[:, :, 1:C], ALU.subtract)
                step(v.tensor_tensor(to[:, :, 0:1], old[:, :, 1 - i:2 - i], new[:, :, 0:1], ALU.subtract))

            ln(3, X3)
            shift(0)
            for e in range(2):
                last = v.scalar_tensor_tensor(out=XI[:, e, :], in0=SX[:, e, :], scalar=cv("maa_x", e), in1=LNT[:, e, :],
                                              op0=ALU.mult, op1=ALU.add)
            last.then_inc(xi_ready, 1)
            for f in range(NF):
                dve.wait_ge(mix_mm, due(mix_mm, it, f + 1))
                for e in range(2):
                    last = v.scalar_tensor_tensor(out=XMX[:, f, e, :], in0=PB[:, f % 4, e * T:(e + 1) * T],
                                                  scalar=cv("stack", 2 * f + e), in1=SX[:, e, :], op0=ALU.add, op1=ALU.mult)
                last.then_inc(mix_used, 1)
            dve.wait_ge(v3_mm, due(v3_mm, it, 1))
            v.tensor_copy(V3[:, :, :], PB[:, 2, :].rearrange("p (e t) -> p e t", e=2)).then_inc(v3_ready, 1)
            dve.wait_ge(g3_exp, due(g3_exp, it, 1))
            step(v.tensor_scalar(Q3[:, :, :], Q3[:, :, :], 1.0, None, ALU.add))
            step(v.reciprocal(Q3[:, :, :], Q3[:, :, :]))
            v.tensor_tensor(G3[:, :, :], PB[:, 1, :].rearrange("p (e t) -> p e t", e=2), Q3[:, :, :], ALU.mult).then_inc(g3_ready, 1)
            dve.wait_ge(k3_ready, due(k3_ready, it, 1))
            dve.wait_ge(r3_ready, due(r3_ready, it, 1))
            dve.wait_ge(w_ready, due(w_ready, it, 1))
            dve.wait_ge(state_in, due(state_in, it, 64))
            for e in range(2):
                step(v.scalar_tensor_tensor(out=RUK[:, e, :], in0=R3[:, e, :], scalar=cv("u", e), in1=K3[:, e, :],
                                            op0=ALU.mult, op1=ALU.mult))
                v.tensor_copy(KV3[:, :, :, 0:1].rearrange("p j b o -> p j (b o)"), S0[:, e, :, :].rearrange("p b j -> p j b"))
                for half in range(2):
                    dve.wait_ge(sp_mm, due(sp_mm, it, 2 * e + half + 1))
                    js = slice(4 * half, 4 * half + 4)
                    k = K3[:, e, :].rearrange("p (b t) -> p b t", b=PAIR)[:, :, 0:C - 1]
                    v.tensor_tensor(KV3[:, js, :, 1:C],
                                    PB[:, 2 * half:2 * half + 2, :].rearrange("p x (y b t) -> p (x y) b t", y=2, b=PAIR)[:, :, :, 0:C - 1],
                                    k.unsqueeze(1).to_broadcast([P, 4, PAIR, C - 1]), ALU.mult).then_inc(kv_ready, 1)
                dve.wait_ge(kv_ready, due(kv_ready, it, 2 * e + 2))
                for j in range(D3):
                    last = v.tensor_tensor_scan(ST3[:, e, j, :], WS[:, e, :, :].rearrange("p b t -> p (b t)"),
                                                KV3[:, j, :, :].rearrange("p b t -> p (b t)"), 0.0, ALU.mult, ALU.add)
                step(last)
                v.tensor_tensor(ST3[:, e, :, :], ST3[:, e, :, :], R3[:, e, :].unsqueeze(1).to_broadcast([P, D3, T]),
                                ALU.mult).then_inc(y3_ready, 1)
            dve.wait_ge(bonus_mm, due(bonus_mm, it, 1))
            step(v.tensor_tensor(O3[:, :, :], PB[:, 1, :].rearrange("p (e t) -> p e t", e=2), V3[:, :, :], ALU.mult))
            v.tensor_tensor(O3[:, :, :], O3[:, :, :], PB[:, 0, :].rearrange("p (e t) -> p e t", e=2), ALU.add).then_inc(o3_ready, 1)
            dve.wait_ge(gvar_mm, due(gvar_mm, it, 1))
            v.tensor_scalar(RUK[:, :, :], PB[:, 3, :].rearrange("p (e t) -> p e t", e=2), EPS, None, ALU.add).then_inc(gvar_ready, 1)
            dve.wait_ge(gsd_ready, due(gsd_ready, it, 1))
            step(v.reciprocal(XI[:, :, :], XI[:, :, :]))
            step(v.tensor_tensor(XI[:, :, :], PB[:, 2, :].rearrange("p (e t) -> p e t", e=2), XI[:, :, :], ALU.mult))
            for e in range(2):
                last = v.tensor_scalar(XI[:, e, :], XI[:, e, :], cv("gn_w", e), cv("gn_b", e), ALU.mult, ALU.add)
            step(last)
            v.tensor_tensor(XI[:, :, :], XI[:, :, :], G3[:, :, :], ALU.mult).then_inc(og_ready, 1)
            dve.wait_ge(wo_mm, due(wo_mm, it, 1))
            step(v.tensor_tensor(X3[:, :, :], X3[:, :, :], PB[:, 0, :].rearrange("p (b n) -> p b n", b=PAIR), ALU.add))
            ln(4, X3)
            shift(1)
            for e in range(2):
                v.scalar_tensor_tensor(out=XI[:, e, :], in0=SX[:, e, :], scalar=cv("mk", e), in1=LNT[:, e, :],
                                       op0=ALU.mult, op1=ALU.add)
                last = v.scalar_tensor_tensor(out=XR[:, e, :], in0=SX[:, e, :], scalar=cv("mr", e), in1=LNT[:, e, :],
                                              op0=ALU.mult, op1=ALU.add)
            last.then_inc(xk_ready, 1)
            dve.wait_ge(fr_exp, due(fr_exp, it, 1))
            step(v.tensor_scalar(FR[:, :, :], FR[:, :, :], 1.0, None, ALU.add))
            step(v.reciprocal(FR[:, :, :], FR[:, :, :]))
            dve.wait_ge(fv_mm, due(fv_mm, it, 1))
            step(v.tensor_tensor(FR[:, :, :], PB[:, 2, :].rearrange("p (b n) -> p b n", b=PAIR), FR[:, :, :], ALU.mult))
            v.tensor_tensor(FR[:, :, :], FR[:, :, :], X3[:, :, :], ALU.add).then_inc(yo_ready, 1)
            chain_end("dve_b")

        @block.vector
        def _(dve):
            U32 = mybir.dt.uint32
            nc.vector.memset(QS[64:P, :, :].bitcast(U32), 0).then_inc(zero_ready, 1)
            nc.vector.memset(KS[64:P, :, :].bitcast(U32), 0).then_inc(zero_ready, 1)
            dve.wait_ge(zero_ready, 2)
            nc.vector.memset(KS[ROW_MAX:P, :, :], 1.0)
            nc.vector.memset(VV[:, :, :], 1.0)
            nc.vector.memset(V2[:, :, N:], 0.0)
            nc.vector.memset(ones[:, :], 1.0)
            nc.vector.memset(WS[:, :, :, 0:1], 0.0).then_inc(zero_ready, 1)
            dve.wait_ge(zero_ready, 3)
            dve.wait_ge(wa_in, 16 * 5)
            nc.vector.tensor_scalar(bn_s[:, 2:3], cv("bn_var"), EPS, None, ALU.add).then_inc(bn_var1, 1)
            dve.wait_ge(bn_sd, 1)
            nc.vector.reciprocal(bn_s[:, 1:2], bn_s[:, 1:2]).then_inc(bn_ready, 1)
            dve.wait_ge(bn_ready, 1)
            nc.vector.tensor_tensor(bn_s[:, 0:1], cv("bn_gamma"), bn_s[:, 1:2], ALU.mult)
            nc.vector.tensor_tensor(bn_s[:, 2:3], cv("w_b"), cv("bn_mean"), ALU.subtract).then_inc(bn_ready, 1)
            dve.wait_ge(bn_ready, 2)
            nc.vector.scalar_tensor_tensor(out=bn_s[:, 2:3], in0=bn_s[:, 2:3], scalar=bn_s[:, 0:1], in1=cv("bn_beta"),
                                           op0=ALU.mult, op1=ALU.add).then_inc(bn_ready, 1)
            dve.wait_ge(bn_ready, 3)
            dve.wait_ge(const_ready, 1)
            with dve.Fori(0, TRIPS) as it:
                dve_stage_a(dve, it)
                dve_stage_b(dve, it)
                dve.wait_ge(out_stored, due(out_stored, it, 16))

        def pe_stage_a(pe, it):
            mm, tr = nc.tensor.matmul, nc.tensor.transpose
            pe.wait_ge(pair_in, due(pair_in, it, 48))
            for b in range(PAIR):
                for j in range(2):
                    last = mm(PA[:, 0, (2 * b + j) * 128:(2 * b + j + 1) * 128], CTX[:, b, j * 128:(j + 1) * 128], WA[:, 0, :],
                              start=True, stop=True)
            last.then_inc(pg_mm, 1)
            for c in range(2):
                for b in range(PAIR):
                    last = tr(PA[:, 3, (2 * c + b) * 128:(2 * c + b + 1) * 128], CTX[:, b, c * 128:(c + 1) * 128], ident[:, :])
            last.then_inc(enc_tr, 1)
            pe.wait_ge(pg_ready, due(pg_ready, it, 1))
            for b in range(PAIR):
                for j in range(2):
                    last = mm(PA[0:CI, 1, b * CI:(b + 1) * CI], PG[:, 2 * b + j, CI:2 * CI], PG[:, 2 * b + j, 0:CI],
                              start=(j == 0), stop=(j == 1))
            last.then_inc(mt_mm, 1)
            pe.wait_ge(enc_ready, due(enc_ready, it, 1))
            pe.wait_ge(mt_ready, due(mt_ready, it, 1))
            mm(PA[:, 3, :], WA[:, 2, :], CTX[:, :, :], start=True, stop=True).then_inc(k_mm, 1)
            for b in range(PAIR):
                last = mm(PA[0:CI, 2, b * 128:(b + 1) * 128], MT[:, b, :], WWT[:, :], start=True, stop=True)
            last.then_inc(at_mm, 1)
            pe.wait_ge(at_ready, due(at_ready, it, 1))
            mm(PA[:, 1, 0:N], THW[:, :], AT[:, :, :], start=True, stop=True)
            for b in range(PAIR):
                last = mm(PA[:, 1, N + b:N + b + 1], AT[:, b, :], cv("theta_b", 0, CI), start=True, stop=True)
            last.then_inc(bt_mm, 1)
            for b in range(PAIR):
                for j in range(2):
                    last = mm(PA[:, 2, (2 * b + j) * 128:(2 * b + j + 1) * 128], CTX[:, b, j * 128:(j + 1) * 128], WA[:, 3, :],
                              start=True, stop=True)
            last.then_inc(v_mm, 1)
            pe.wait_ge(bt_ready, due(bt_ready, it, 1))
            for b in range(PAIR):
                last = mm(PA[:, 0, b * N:(b + 1) * N], BT[:, b, :], X0[:, b, :], start=True, stop=True)
            last.then_inc(y_mm, 1)
            pe.wait_ge(sh_ready, due(sh_ready, it, 1))
            pe.wait_ge(x1_ready, due(x1_ready, it, 1))
            mm(PA[:, 1, :], WA[:, 1, :], X1[:, :, :], start=True, stop=True).then_inc(q_mm, 1)
            pe.wait_ge(q_ready, due(q_ready, it, 1))
            pe.wait_ge(k_ready, due(k_ready, it, 1))
            pe.wait_ge(v_ready, due(v_ready, it, 1))
            pe.wait_ge(stack_in, due(stack_in, it, 19 * 16))

            def scores(b):
                for h in range(H1):
                    u = b * H1 + h
                    if u >= 2:
                        pe.wait_ge(s_max, due(s_max, it, u - 1))
                    for q in range(2):
                        o = b * N + q * 128
                        last = mm(PA[:, u % 2, q * N:(q + 1) * N], QS[0:K_SCORES, h, o:o + 128], KS[0:K_SCORES, h, b * N:(b + 1) * N],
                                  start=True, stop=True)
                    last.then_inc(s_mm, 1)
                pe.wait_ge(s_max, due(s_max, it, (b + 1) * H1))
                if b:
                    pe.wait_ge(m_parts, due(m_parts, it, b))
                for q in range(2):
                    last = tr(PA[0:H1, 3, q * 128:(q + 1) * 128], MX[:, b, q, :], ident[:, :])
                last.then_inc(m_tr, 1)

            def shifted(b):
                pe.wait_ge(maxp_in[b], due(maxp_in[b], it, 16))
                for h in range(H1 + G):
                    u = b * H1 + h
                    if h < H1:
                        if u >= 2:
                            pe.wait_ge(t_exp, due(t_exp, it, u - 1))
                        for k in range(2):
                            o = b * N + k * 128
                            last = mm(PA[:, u % 2, k * N:(k + 1) * N], KS[0:K_SHIFTED, h, o:o + 128],
                                      QS[0:K_SHIFTED, h, b * N:(b + 1) * N], start=True, stop=True)
                        last.then_inc(t_mm, 1)
                    if h >= G and h % G == G - 1:
                        t = h // G - 1
                        n = b * HT + t
                        pe.wait_ge(t_exp, due(t_exp, it, b * H1 + (t + 1) * G))
                        if b and t == 0:
                            pe.wait_ge(ot_out, due(ot_out, it, 2 * b))
                        if n >= 2:
                            pe.wait_ge(pv_out, due(pv_out, it, n - 1))
                        for k in range(2):
                            for g in range(G):
                                hh = G * t + g
                                last = mm(PA[32 * g:32 * g + 32, 2 + t % 2, 0:N], VV[:, 2 * b + k, VC * hh:VC * hh + 32],
                                          PT[:, (b * H1 + hh) % (2 * G), k, :], start=(k == 0), stop=(k == 1),
                                          skip_group_check=True)
                        last.then_inc(pv_mm, 1)
                pe.wait_ge(pv_out, due(pv_out, it, (b + 1) * HT))
                for q in range(2):
                    if 2 * b + q:
                        pe.wait_ge(ot_out, due(ot_out, it, 2 * b + q))
                    for t in range(HT):
                        last = tr(PA[:, 2, t * 128:(t + 1) * 128], OT[:, t, q * 128:(q + 1) * 128], ident[:, :])
                    last.then_inc(ot_tr, 1)

            scores(0)
            scores(1)
            pe.wait_ge(m_parts, due(m_parts, it, PAIR))
            pe.wait_ge(vsq_ready, due(vsq_ready, it, 1))
            shifted(0)
            shifted(1)
            pe.wait_ge(std_ready, due(std_ready, it, 1))
            for i in range(2 * PAIR):
                tr(PA[:, 2, i * 128:(i + 1) * 128], MN[:, i, :], ident[:, :])
            for i in range(2 * PAIR):
                last = tr(PA[:, 3, i * 128:(i + 1) * 128], SQ[:, i, :], ident[:, :])
            last.then_inc(ms_tr, 1)

        def pe_stage_b(pe, it):
            mm, tr = nc.tensor.matmul, nc.tensor.transpose

            def ln(i):
                pe.wait_ge(ln_hat, due(ln_hat, it, i + 1))
                for c in range(2):
                    for b in range(PAIR):
                        last = tr(PB[:, 0, (2 * c + b) * 128:(2 * c + b + 1) * 128], XH[:, b, c * 128:(c + 1) * 128], ident[:, :])
                last.then_inc(ln_tr, 1)

            def project(bank, w, src):
                for e in range(2):
                    for c in range(2):
                        last = mm(PB[:, bank, e * T:(e + 1) * T], w(c, e), src(c), start=(c == 0), stop=(c == 1))
                return last

            def project_rows(bank, w, src, n=2):
                for b in range(PAIR):
                    for c in range(n):
                        last = mm(PB[:, bank, b * N:(b + 1) * N], src(c, b), w(c), start=(c == 0), stop=(c == n - 1))
                return last

            def project_heads(bank, at, src):
                for t in range(HT):
                    for c in range(2):
                        for g in range(G):
                            w = at + D2 * (G * t + g)
                            last = mm(PB[32 * g:32 * g + 32, bank + t // 2, (t % 2) * T:(t % 2 + 1) * T], WH[:, c, w:w + 32],
                                      src[:, c, :], start=(c == 0), stop=(c == 1), skip_group_check=True)
                return last

            pe.wait_ge(wb_in, 16 * 13)
            for a in range(2):
                ln(a)
                pe.wait_ge(ln_ready, due(ln_ready, it, a + 1))
                kv = LNT if a == 0 else ENC
                project_heads(0, 3 * a * N, LNT).then_inc(qp_mm, 1)
                project_heads(2, (3 * a + 1) * N, kv).then_inc(kp_mm, 1)
                pe.wait_ge(qt_ready, due(qt_ready, it, a + 1))
                project_rows(0, lambda c: WH[:, c, (3 * a + 2) * N:(3 * a + 3) * N], lambda c, b: kv[:, c, b * C:(b + 1) * C]).then_inc(vp_mm, 1)
                pe.wait_ge(kt_ready, due(kt_ready, it, a + 1))
                pe.wait_ge(v2_ready, due(v2_ready, it, a + 1))
                for b in range(PAIR):
                    u = 2 * a + b
                    for t in range(HT):
                        for g in range(G):
                            last = mm(PB[:, g, t * C:(t + 1) * C], QT[32 * g:32 * g + D2, t, b * C:(b + 1) * C],
                                      KT[32 * g:32 * g + D2, t, b * C:(b + 1) * C], start=True, stop=True)
                    last.then_inc(sc_mm, 1)
                    pe.wait_ge(sc_exp, due(sc_exp, it, u + 1))
                    for h in range(H2):
                        last = tr(PB[:, h // 4, (h % 4) * C:(h % 4 + 1) * C], SM[:, h, :], ident[:, :])
                    last.then_inc(p_tr, 1)
                    pe.wait_ge(p_out_act, due(p_out_act, it, u + 1))
                    pe.wait_ge(p_out_dve, due(p_out_dve, it, u + 1))
                    for t in range(HT):
                        for g in range(G):
                            mm(PB[32 * g:32 * g + 32, 0, t * C:(t + 1) * C], V2[:, b, D2 * (G * t + g):D2 * (G * t + g) + 32], PT2[:, 4 * g + t, :],
                               start=True, stop=True, skip_group_check=True)
                        for g in range(G):
                            last = mm(PB[32 * g:32 * g + 32, 1, t * C:(t + 1) * C], ones[:, :], PT2[:, 4 * g + t, :],
                                      start=True, stop=True, skip_group_check=True)
                    last.then_inc(ctx_mm, 1)
                    pe.wait_ge(ctx_ready, due(ctx_ready, it, u + 1))
                    for t in range(HT):
                        last = mm(PB[:, 2, b * N:(b + 1) * N], CT2[:, t, :], WO[:, a, t, :], start=(t == 0), stop=(t == HT - 1))
                    last.then_inc(ao_mm, 1)
                    pe.wait_ge(res_half, due(res_half, it, u + 1))
            ln(2)
            pe.wait_ge(ln_ready, due(ln_ready, it, 3))
            for o in range(FF // P):
                for c in range(2):
                    last = mm(PB[:, o // 2, (o % 2) * T:(o % 2 + 1) * T], W1[:, c, o * P:(o + 1) * P], LNT[:, c, :],
                              start=(c == 0), stop=(c == 1))
                last.then_inc(ff_mm, 1)
            pe.wait_ge(ff_act, due(ff_act, it, 8))
            project_rows(0, lambda c: W2[:, c, :], lambda c, b: HF[:, c, b * C:(b + 1) * C], FF // P).then_inc(ff2_mm, 1)
            ln(3)
            pe.wait_ge(xi_ready, due(xi_ready, it, 1))
            for c in range(2):
                mm(PB[:, 0, 0:T], MW1[:, c, 0:128], XI[:, c, :], start=(c == 0), stop=(c == 1))
            for c in range(2):
                last = mm(PB[0:DM, 0, T:2 * T], MW1[:, c, 128:160], XI[:, c, :], start=(c == 0), stop=(c == 1))
            last.then_inc(tx_mm, 1)
            pe.wait_ge(tx_ready, due(tx_ready, it, 1))
            for f in range(4):
                for e in range(2):
                    last = mm(PB[:, f, e * T:(e + 1) * T], MW2[DM * f:DM * f + DM, e * P:(e + 1) * P], TX[DM * f:DM * f + DM, :],
                              start=True, stop=True)
                last.then_inc(mix_mm, 1)
            pe.wait_ge(mix_used, due(mix_used, it, 1))
            for e in range(2):
                last = mm(PB[:, 0, e * T:(e + 1) * T], MW2B[:, e * P:(e + 1) * P], TXB[:, :], start=True, stop=True)
            last.then_inc(mix_mm, 1)
            pe.wait_ge(mix_ready, due(mix_ready, it, 2))
            for c in range(2):
                last = mm(PB[0:DD, 1, 0:T], TW1[:, c, :], XMX[:, 1, c, :], start=(c == 0), stop=(c == 1))
            last.then_inc(td1_mm, 1)
            pe.wait_ge(mix_ready, due(mix_ready, it, 3))
            project(2, lambda c, e: W3[:, c, 2, e * P:(e + 1) * P], lambda c: XMX[:, 2, c, :]).then_inc(v3_mm, 1)
            pe.wait_ge(td1_ready, due(td1_ready, it, 1))
            for e in range(2):
                last = mm(PB[:, 1, e * T:(e + 1) * T], TW2[:, e * P:(e + 1) * P], TD[:, :], start=True, stop=True)
            last.then_inc(td2_mm, 1)
            pe.wait_ge(mix_ready, due(mix_ready, it, 4))
            project(3, lambda c, e: W3[:, c, 1, e * P:(e + 1) * P], lambda c: XMX[:, 0, c, :]).then_inc(k3_mm, 1)
            pe.wait_ge(mix_ready, due(mix_ready, it, 5))
            project(0, lambda c, e: W3[:, c, 0, e * P:(e + 1) * P], lambda c: XMX[:, 3, c, :]).then_inc(r3_mm, 1)
            pe.wait_ge(w_ready, due(w_ready, it, 1))
            project(1, lambda c, e: W3[:, c, 3, e * P:(e + 1) * P], lambda c: XMX[:, 4, c, :]).then_inc(g3_mm, 1)
            pe.wait_ge(v3_ready, due(v3_ready, it, 1))
            pe.wait_ge(k3_ready, due(k3_ready, it, 1))
            pe.wait_ge(r3_ready, due(r3_ready, it, 1))
            pe.wait_ge(g3_ready, due(g3_ready, it, 1))
            for e in range(2):
                for half in range(2):
                    if e:
                        pe.wait_ge(kv_ready, due(kv_ready, it, half + 1))
                    for j in range(4 * half, 4 * half + 4):
                        last = mm(PB[:, j // 2, (j % 2) * T:(j % 2 + 1) * T], SEL[:, 3 + j, :], V3[:, e, :], start=True, stop=True)
                    last.then_inc(sp_mm, 1)
            pe.wait_ge(kv_ready, due(kv_ready, it, 4))
            for e in range(2):
                pe.wait_ge(y3_ready, due(y3_ready, it, e + 1))
                for j in range(D3):
                    last = mm(PB[:, 0, e * T:(e + 1) * T], GATHER[:, D3 - 1 - j:D3 - 1 - j + P], ST3[:, e, j, :], start=(j == 0), stop=(j == D3 - 1))
            for e in range(2):
                last = mm(PB[:, 1, e * T:(e + 1) * T], SEL[:, 0, :], RUK[:, e, :], start=True, stop=True)
            last.then_inc(bonus_mm, 1)
            pe.wait_ge(o3_ready, due(o3_ready, it, 1))
            mm(PB[:, 2, :], SEL[:, 1, :], O3[:, :, :], start=True, stop=True).then_inc(cen_mm, 1)
            pe.wait_ge(cen_sq, due(cen_sq, it, 1))
            mm(PB[:, 3, :], SEL[:, 2, :], Q3[:, :, :], start=True, stop=True).then_inc(gvar_mm, 1)
            pe.wait_ge(og_ready, due(og_ready, it, 1))
            project_rows(0, lambda c: W3[:, c, 4, :], lambda c, b: XI[:, c, b * C:(b + 1) * C]).then_inc(wo_mm, 1)
            ln(4)
            pe.wait_ge(xk_ready, due(xk_ready, it, 1))
            project(0, lambda c, e: W3[:, c, 5, e * P:(e + 1) * P], lambda c: XI[:, c, :]).then_inc(fk_mm, 1)
            project_rows(1, lambda c: W3[:, c, 6, :], lambda c, b: XR[:, c, b * C:(b + 1) * C]).then_inc(fr_mm, 1)
            pe.wait_ge(fk_ready, due(fk_ready, it, 1))
            project_rows(2, lambda c: W3[:, c, 7, :], lambda c, b: Q3[:, c, b * C:(b + 1) * C]).then_inc(fv_mm, 1)

        @block.tensor
        def _(pe):
            pe.wait_ge(wa_in, 16 * 5)
            pe.wait_ge(const_ready, 1)
            pe.wait_ge(zero_ready, 3)
            with pe.Fori(0, TRIPS) as it:
                pe_stage_a(pe, it)
                pe_stage_b(pe, it)
                pe.wait_ge(out_stored, due(out_stored, it, 16))


def kernel(**inputs):
    import concourse.bacc as _bacc
    from concourse.bass_utils import run_bass_kernel_spmd as _run

    a = {k: np.ascontiguousarray(v) for k, v in inputs.items()}
    l0, l1, l2, l3 = ({k[9:]: v for k, v in a.items() if k.startswith(f"L{i}_")} for i in range(4))
    halves = lambda w: w.reshape(-1, P, w.shape[-1]).transpose(1, 0, 2)

    def head_cols(w):
        o = np.zeros((w.shape[0], HT, G, 32), w.dtype)
        o[..., 0:D2] = w.reshape(-1, HT, G, D2)
        return o.reshape(w.shape[0], HT * 128)

    def head_rows(w):
        o = np.zeros((HT, G, 32, w.shape[1]), w.dtype)
        o[:, :, 0:D2] = w.reshape(HT, G, D2, -1)
        return o.reshape(HT, P, -1).transpose(1, 0, 2)

    def column(v):
        v = v.reshape(-1)
        if v.size < P:
            v = np.concatenate([v, np.zeros(P - v.size, v.dtype)])
        return v.reshape(-1, P).T

    padded = lambda v: head_cols(v.reshape(1, -1)).reshape(-1)
    vectors = dict(
        bn_gamma=l0["bn_gamma"], bn_beta=l0["bn_beta"], bn_mean=l0["bn_mean"], bn_var=l0["bn_var"], w_b=l0["w_b"],
        bq1=l1["bq"], bk1=l1["bk"], theta_b=l0["theta_b"], ln1_s=l2["ln1_s"], ln1_b=l2["ln1_b"], ln2_s=l2["ln2_s"],
        ln2_b=l2["ln2_b"], ln3_s=l2["ln3_s"], ln3_b=l2["ln3_b"], bq_self=padded(l2["b_qkv"][0:N]),
        bk_self=padded(l2["b_qkv"][N:2 * N]), bq_cross=padded(l2["b_q"]), bk_cross=padded(l2["b_kv"][0:N]), b1=l2["b1"],
        l3ln1_s=l3["ln1_w"], l3ln1_b=l3["ln1_b"], l3ln2_s=l3["ln2_w"], l3ln2_b=l3["ln2_b"], maa_x=l3["maa_x"],
        stack=l3["maa_stack"], decay=l3["time_decay"], u=l3["u"], gn_w=l3["gn_w"], gn_b=l3["gn_b"],
        mk=l3["ffn_maa_k"], mr=l3["ffn_maa_r"])
    rows = np.concatenate([l0["phi_b"], l0["g_b"], l1["bv"], l2["b_qkv"][2 * N:], l2["b_kv"][N:], l2["b_ao"], l2["b_co"], l2["b2"]])
    channel = np.arange(P)
    same_head = (channel[:, None] // D3 == channel[None, :] // D3).astype(np.float32)
    eye = np.eye(P, dtype=np.float32)
    spread = [same_head * (channel[:, None] % D3 == j) for j in range(D3)]
    sel = np.stack([same_head, eye - same_head / D3, same_head / D3] + spread, 1).astype(np.float32)
    gather = (np.arange(P + D3 - 1)[None, :] == D3 * (channel[:, None] // D3) + D3 - 1).astype(np.float32)
    laid = dict(
        x=a["x"], ctxt=a["ctx_2048"], kv_mask=a["mask_Bx1x2048_bf1"].reshape(NB, N).view(np.uint8),
        self_mask=a["mask_1x1xSxS2_fc1"].reshape(C, C), cross_mask=a["mask_Bx1xSxS2_ff1"].reshape(NB, C, C),
        cols=np.concatenate([column(vectors[k]) for k in COLS], 1), rows=rows,
        wa=np.stack([np.concatenate([l0["phi_w"], l0["g_w"]], 0).T, l1["Wq"].T, l1["Wk"].T, l1["Wv"].T], 1),
        ww_t=l0["w_w"].T, theta_w=l0["theta_w"],
        wh=np.concatenate([halves(l2["w_qkv"]), halves(l2["w_q"]), halves(l2["w_kv"])], 2),
        wo=np.stack([head_rows(l2["w_ao"]), head_rows(l2["w_co"])], 1),
        w_ff1=halves(l2["w1"]), w_ff2=halves(l2["w2"]),
        w3=np.stack([halves(l3[k].T) for k in ("Wr", "Wk", "Wv", "Wg", "Wo", "Wfk", "Wfr", "Wfv")], 2),
        maa_w1=l3["maa_w1"], maa_w2=l3["maa_w2"].reshape(NF * DM, N), td_w1=l3["td_w1"], td_w2=l3["td_w2"], sel=sel, gather=gather)
    nc = _bacc.Bacc("TRN2", target_bir_lowering=False, num_devices=1)
    arrays, ap = {}, {}
    for name, v in laid.items():
        v = np.ascontiguousarray(v)
        arrays[f"in_{name}_dram"] = v
        ap[name] = nc.dram_tensor(f"in_{name}_dram", v.shape, mybir.dt.from_np(v.dtype), kind="ExternalInput").ap()
    ap["out"] = nc.dram_tensor("out_0_dram", (NB, C, N), F32, kind="ExternalOutput").ap()
    four_layers(nc, **ap)
    return _run(nc, [arrays], core_ids=[0]).results[0]["out_0_dram"]
```

```python
from contextlib import ExitStack

import concourse.bass as bass
from concourse import mybir
import numpy as np

F32 = mybir.dt.float32
BF16 = mybir.dt.bfloat16
U8 = mybir.dt.uint8
ALU = mybir.AluOpType
ACT = mybir.ActivationFunctionType
AX = mybir.AxisListType

P = 128
NB = 8
PAIR = 2
TRIPS = NB // PAIR
C = 128
N = 256
T = PAIR * C
CI = 64
H1, D1 = 16, 8
H2, D2 = 16, 16
G = 4
HT = H2 // G
FF = 4 * N
H3, D3 = 32, 8
HC = P // D3
NF, DM, DD = 5, 32, 64
EPS = 1e-5
VC = 2 * D1 + 1
NSPLIT = 3
KSTACK = NSPLIT * NSPLIT * D1
ROW_MASK = KSTACK
ROW_MAX = 96
K_SCORES = ROW_MAX
K_SHIFTED = ROW_MAX + NSPLIT

COLS = {}
for _name, _n in (("bn_gamma", 1), ("bn_beta", 1), ("bn_mean", 1), ("bn_var", 1), ("w_b", 1), ("bq1", 1), ("bk1", 1),
                  ("theta_b", 1), ("ln1_s", 2), ("ln1_b", 2), ("ln2_s", 2), ("ln2_b", 2), ("ln3_s", 2), ("ln3_b", 2),
                  ("bq_self", 4), ("bk_self", 2), ("bq_cross", 4), ("bk_cross", 2), ("b1", 8), ("parity", 2),
                  ("l3ln1_s", 2), ("l3ln1_b", 2), ("l3ln2_s", 2), ("l3ln2_b", 2), ("maa_x", 2), ("stack", 10),
                  ("decay", 2), ("u", 2), ("gn_w", 2), ("gn_b", 2), ("mk", 2), ("mr", 2)):
    COLS[_name] = (sum(n for _, n in COLS.values()), _n)
NCOL = sum(n for _, n in COLS.values())
ROWS = {}
for _name, _n in (("phi_g_b", 128), ("bv1", 128), ("bv_self", 256), ("bv_cross", 256), ("b_ao", 256), ("b_co", 256),
                  ("b2", 256)):
    ROWS[_name] = (sum(n for _, n in ROWS.values()), _n)
NROW = sum(n for _, n in ROWS.values())

CHAIN = {"dve_a": 32, "dve_b": 52, "act_b": 2}


def four_layers(nc, x, ctxt, kv_mask, self_mask, cross_mask, cols, rows, wa, ww_t, theta_w, wh, wo, w_ff1, w_ff2,
                w3, maa_w1, maa_w2, td_w1, td_w2, sel, gather, out):
    with ExitStack() as stack:
        def sb(name, shape, dt=F32):
            return stack.enter_context(nc.sbuf_tensor(name, shape, dt))

        per_trip = {}

        def sem(name, n=1):
            s = stack.enter_context(nc.semaphore(name))
            per_trip[name] = n
            names[id(s)] = name
            keep.append(s)
            return s

        names, keep = {}, []

        def due(s, it, k):
            return it * per_trip[names[id(s)]] + k

        q_dram = nc.dram_tensor("q_parts", (NSPLIT, C, PAIR * N), BF16, kind="Internal").ap()
        k_dram = nc.dram_tensor("k_parts", (NSPLIT, C, PAIR * N), BF16, kind="Internal").ap()
        max_dram = nc.dram_tensor("max_parts", (PAIR, H1, NSPLIT, N), BF16, kind="Internal").ap()
        mask_dram = nc.dram_tensor("mask_rows", (H1, PAIR * N), BF16, kind="Internal").ap()

        col = sb("col", [P, NCOL])
        row = sb("row", [P, NROW])
        WA = sb("WA", [P, 5, 128])
        WWT = sb("WWT", [CI, 128])
        THW = sb("THW", [CI, 128])
        WH = sb("WH", [P, 2, 6 * N])
        WO = sb("WO", [P, 2, 2, N])
        W1 = sb("W1", [P, 2, FF])
        W2 = sb("W2", [P, FF // P, N])
        W3 = sb("W3", [P, 2, 8, N])
        MW1 = sb("MW1", [P, 2, NF * DM])
        MW2 = sb("MW2", [P, N])
        MW2B = sb("MW2B", [DM, N])
        TW1 = sb("TW1", [P, 2, DD])
        TW2 = sb("TW2", [DD, N])
        SEL = sb("SEL", [P, 3 + D3, 128])
        GATHER = sb("GATHER", [P, P + D3 - 1])
        ident = sb("ident", [P, P])
        bn_s = sb("bn_s", [P, 3])
        bq1s = sb("bq1s", [P, 1])

        eps = sb("eps", [P, 1])

        def cv(name, i=0, parts=P):
            o = COLS[name][0] + i
            return col[0:parts, o:o + 1]

        def rv(name):
            o, n = ROWS[name]
            return row[:, o:o + n]

        X0 = sb("X0", [P, PAIR, N])
        CTX = sb("CTX", [P, PAIR, N])
        MASK8 = sb("MASK8", [P, PAIR, N], U8)
        MF = sb("MF", [P, PAIR, N])
        MBIAS = sb("MBIAS", [P, PAIR * N], BF16)
        MT = sb("MT", [CI, PAIR, CI])
        AT = sb("AT", [CI, PAIR, 128])
        BT = sb("BT", [P, PAIR, 128])
        SH = sb("SH", [P, PAIR])
        X1 = sb("X1", [P, PAIR, N])
        QS = sb("QS", [P, H1, PAIR * N], BF16)
        KS = sb("KS", [P, H1, PAIR * N], BF16)
        VV = sb("VV", [P, PAIR * 2, H1 * VC + 32 - VC])
        VH = VV[:, :, 0:H1 * VC].rearrange("p a (h c) -> p a h c", c=VC)
        MX = sb("MX", [P, PAIR, 2, H1])
        NMP = sb("NMP", [H1, NSPLIT, N], BF16)
        AREA_A = sb("AREA_A", [P, 2 * G * 2 * N])
        PT = AREA_A[:, :].rearrange("p (s k n) -> p s k n", s=2 * G, k=2)
        QK = AREA_A[:, 0:1024].rearrange("p (i n) -> p i n", i=2)
        RES = AREA_A[:, 1024:2048].rearrange("p (i n) -> p i n", i=2)
        QKP = AREA_A[:, 2048:3584].bitcast(BF16).rearrange("p (i s n) -> p i s n", i=2, s=NSPLIT)
        PG = AREA_A[:, 3584:4096].rearrange("p (a n) -> p a n", n=128)
        OT = sb("OT", [P, HT, N])
        NM = OT[0:H1, 0:2, :]
        SQ = OT[:, 0:2, :].rearrange("p a (b n) -> p (a b) n", n=128)
        RSUM = sb("RSUM", [P, H1])
        MN = sb("MN", [P, PAIR * 2, 128])
        EX = CTX[:, :, :].rearrange("p b (q c) -> p (b q) c", q=2)
        IST = sb("IST", [P, 8, PAIR])
        XN = X0
        ENC = sb("ENC", [P, 2, T])
        X2 = sb("X2", [P, PAIR, N])
        ENC_A, ENC = ENC, sb("ENC_B", [P, 2, T])

        AREA_B = sb("AREA_B", [P, 6144])
        QT = AREA_B[:, 0:1024].rearrange("p (t n) -> p t n", t=HT)
        KT = AREA_B[:, 1024:1536].rearrange("p (c n) -> p c n", c=2)
        SM = AREA_B[:, 2048:4096].rearrange("p (h k) -> p h k", h=H2)
        PT2 = SM
        HF = AREA_B[:, 2048:4096].rearrange("p (o n) -> p o n", n=T)
        CT2 = AREA_B[:, 4096:4352].rearrange("p (c n) -> p c n", c=2)
        XMX = AREA_B[:, 0:2560].rearrange("p (f e n) -> p f e n", f=NF, e=2)
        KV3 = AREA_B[:, 0:2048].rearrange("p (j b n) -> p j b n", j=D3, b=PAIR)
        ST3 = AREA_B[:, 2048:6144].rearrange("p (e j n) -> p e j n", e=2, j=D3)
        SMASK = sb("SMASK", [P, C])
        SFILL = sb("SFILL", [P, C])
        CMASK = sb("CMASK", [P, PAIR, C])
        CFILL = sb("CFILL", [P, PAIR, C])
        X3 = sb("X3", [P, PAIR, N])
        BST = sb("BST", [P, PAIR, 6])
        BMV = sb("BMV", [P, PAIR, 2])
        cell = sb("cell", [P, 1])
        SDV = sb("SDV", [P, PAIR])
        RSD = sb("RSD", [P, PAIR])
        LNT = sb("LNT", [P, 2, T])
        V2 = sb("V2", [P, PAIR, H2, 2 * D2])
        RS2 = sb("RS2", [P, H2])
        RR2 = sb("RR2", [P, H2])
        MX2 = sb("MX2", [P, H2])
        NMX2 = sb("NMX2", [P, H2])
        SX = sb("SX", [P, 2, T])
        XH = SX
        XI = sb("XI", [P, 2, T])
        TX = sb("TX", [P, T])
        TD = TX[0:DD, :]
        TXB = sb("TXB", [DM, T])
        WS = sb("WS", [P, 2, PAIR, C])
        R3 = sb("R3", [P, 2, T])
        K3 = sb("K3", [P, 2, T])
        V3 = sb("V3", [P, 2, T])
        G3 = sb("G3", [P, 2, T])
        S0 = sb("S0", [P, 2, PAIR, D3])
        RUK = sb("RUK", [P, 2, T])
        EX3 = RUK
        O3 = sb("O3", [P, 2, T])
        XR = O3
        Q3 = sb("Q3", [P, 2, T])
        FR = R3

        PA = stack.enter_context(nc.psum_tensor("PA", [P, 4, 512], F32))
        PB = stack.enter_context(nc.psum_tensor("PB", [P, 4, 512], F32))

        wa_in, wb_in = sem("wa_in"), sem("wb_in")
        const_step, const_ready, bn_ready = sem("const_step"), sem("const_ready"), sem("bn_ready")
        zero_ready = sem("zero_ready")
        bn_sd, bn_var1 = sem("bn_sd"), sem("bn_var1")
        pair_in, out_stored = sem("pair_in", 3 * 16), sem("out_stored", 16)
        cross_in = sem("cross_in", 16)
        state_in = sem("state_in", PAIR * 2 * 16)
        parts_out, mask_out = sem("parts_out", 2 * 16), sem("mask_out", 16)
        stack_in = sem("stack_in", 19 * 16)
        maxp_out, maxp_in = sem("maxp_out", PAIR * 16), [sem(f"maxp_in{b}", 16) for b in range(PAIR)]
        enc_tr, enc_ready = sem("enc_tr"), sem("enc_ready")
        pg_mm, pg_ready = sem("pg_mm"), sem("pg_ready")
        mt_mm, mt_ready = sem("mt_mm"), sem("mt_ready")
        at_mm, at_ready = sem("at_mm"), sem("at_ready")
        bt_mm, bt_ready, sh_ready = sem("bt_mm"), sem("bt_ready"), sem("sh_ready")
        y_mm, y_added, x1_ready = sem("y_mm"), sem("y_added"), sem("x1_ready")
        k_mm, q_mm, v_mm = sem("k_mm"), sem("q_mm"), sem("v_mm")
        k_ready, q_ready, v_ready = sem("k_ready"), sem("q_ready"), sem("v_ready")
        kp_ready, qp_ready, mbias_ready = sem("kp_ready"), sem("qp_ready"), sem("mbias_ready")
        vsq_ready = sem("vsq_ready")
        s_mm, s_max = sem("s_mm", PAIR * H1), sem("s_max", PAIR * H1)
        m_tr, m_parts = sem("m_tr", PAIR), sem("m_parts", PAIR)
        t_mm, t_exp = sem("t_mm", PAIR * H1), sem("t_exp", PAIR * H1)
        pv_mm, pv_out = sem("pv_mm", PAIR * HT), sem("pv_out", PAIR * HT)
        ot_tr, ot_out = sem("ot_tr", PAIR * 2), sem("ot_out", PAIR * 2)
        var_ready, std_ready = sem("var_ready"), sem("std_ready")
        ivar_ready, istd_ready = sem("ivar_ready"), sem("istd_ready")
        ms_tr, x2_ready = sem("ms_tr"), sem("x2_ready")
        ln_var, ln_sd, ln_hat = sem("ln_var", 5), sem("ln_sd", 5), sem("ln_hat", 5)
        enc_moved = sem("enc_moved")
        ln_tr, ln_ready_act, ln_ready_dve = sem("ln_tr", 5), sem("ln_ready_act", 5), sem("ln_ready_dve", 5)
        qp_mm, kp_mm, vp_mm = sem("qp_mm", 2), sem("kp_mm", 2), sem("vp_mm", 2)
        qt_ready, kt_ready, v2_ready = sem("qt_ready", 2), sem("kt_ready", 2), sem("v2_ready", 2)
        sc_mm, sc_nmax, sc_exp = sem("sc_mm", 8), sem("sc_nmax", 8), sem("sc_exp", 8)
        rsum_inv, p_norm_pool, p_norm_dve = sem("rsum_inv", 4), sem("p_norm_pool", 4), sem("p_norm_dve", 4)
        p_tr, p_out_dve, p_out_act = sem("p_tr", 8), sem("p_out_dve", 8), sem("p_out_act", 4)
        ctx_mm, ct_ready = sem("ctx_mm", 4), sem("ct_ready", 4)
        ao_mm, res_ready = sem("ao_mm", 4), sem("res_ready", 4)
        ff_mm, ff_act, ff2_mm, x4_ready = sem("ff_mm", 8), sem("ff_act", 8), sem("ff2_mm"), sem("x4_ready")
        sx_ready, xi_ready = sem("sx_ready", 2), sem("xi_ready")
        tx_mm, tx_ready = sem("tx_mm"), sem("tx_ready")
        mix_mm, mix_used, mix_ready = sem("mix_mm", NF), sem("mix_used", NF), sem("mix_ready", NF)
        td1_mm, td1_ready, td2_mm, td2_used, w_ready = sem("td1_mm"), sem("td1_ready"), sem("td2_mm"), sem("td2_used"), sem("w_ready")
        v3_mm, k3_mm, r3_mm, g3_mm = sem("v3_mm"), sem("k3_mm"), sem("r3_mm"), sem("g3_mm")
        v3_ready, k3_ready, r3_ready = sem("v3_ready"), sem("k3_ready"), sem("r3_ready")
        g3_tanh, g3_ready = sem("g3_tanh"), sem("g3_ready")
        sp_mm, kv_ready = sem("sp_mm", 4), sem("kv_ready", 4)
        sc_done, y3_ready, ruk_ready = sem("sc_done", 2), sem("y3_ready", 2), sem("ruk_ready")
        o3_mm, bonus_mm, o3_ready = sem("o3_mm"), sem("bonus_mm"), sem("o3_ready")
        cen_mm, cen_sq, gvar_mm, gsd_ready, og_ready = (
            sem("cen_mm"), sem("cen_sq"), sem("gvar_mm"), sem("gsd_ready"), sem("og_ready"))
        wo_mm, x5_ready = sem("wo_mm"), sem("x5_ready")
        xk_ready, fk_mm, fr_mm = sem("xk_ready"), sem("fk_mm"), sem("fr_mm")
        fk_ready, fr_tanh, fv_mm, yo_ready = sem("fk_ready"), sem("fr_tanh"), sem("fv_mm"), sem("yo_ready")
        chain_sem = {k: sem(k, n) for k, n in CHAIN.items()}
        chain_at = {}

        def link(eng, name, it, ins):
            chain_at[name] = chain_at.get(name, 0) + 1
            ins.then_inc(chain_sem[name], 1)
            eng.wait_ge(chain_sem[name], it * CHAIN[name] + chain_at[name])

        def chain_end(name):
            assert chain_at.get(name, 0) == CHAIN[name], (name, chain_at.get(name, 0))
            chain_at[name] = 0

        def half_at(u, i):
            return 2 * ((u + i) % 2)

        def layer_ln(i):
            return [("ln", i), ("hat", i)]

        PHASES_A = ["pg", "mt", "k", "bt", "y", "q", "norm", "unit"]
        PHASES_A += [("s", 0, h) for h in range(H1)] + [("max", 0)]
        PHASES_A += [("s", 1, h) for h in range(H1)] + [("max", 1)]
        for b in range(PAIR):
            PHASES_A += [("t", b, h) for h in range(H1 + G)] + [("o", b, 0), ("o", b, 1)]
        PHASES_A += ["var", "x2"]
        PHASES_B = []
        for a in range(2):
            PHASES_B += layer_ln(a) + [("qk", a), ("v", a)]
            for u in (2 * a, 2 * a + 1):
                PHASES_B += [("score", u, 0)] + ([("tail", u - 1)] if u % 2 else []) + [("exp", u, 0), ("score", u, 1), ("exp", u, 1)]
                PHASES_B += [("norm", u, 0), ("norm", u, 1), ("turn", u, 0), ("turn", u, 1), ("ctx", u, 0), ("ctx", u, 1)]
            PHASES_B += [("tail", 2 * a + 1)]
        PHASES_B += layer_ln(2) + [("ff", k) for k in range(4)] + ["ff2"]
        PHASES_B += layer_ln(3) + ["xi", "tx"] + [("mix", f) for f in range(NF)]
        PHASES_B += ["td1", "v3", "td2", "k3", "r3", "g3", "ruk"]
        PHASES_B += [("spread", e, half) for e in range(2) for half in range(2)]
        PHASES_B += ["sum", "bonus", "centre", "gvar", "og", "wo"] + layer_ln(4) + ["xk", "fr", "fv"]
        assert len(set(PHASES_A)) == len(PHASES_A) and len(set(PHASES_B)) == len(PHASES_B)

        def order():
            at, done = [], 0
            for i, phase in enumerate(PHASES_B):
                at.append(("B", phase))
                upto = min(len(PHASES_A), round((i + 1) * len(PHASES_A) / (len(PHASES_B) - 6)))
                at += [("A", p) for p in PHASES_A[done:upto]]
                done = upto
            return at + [("A", p) for p in PHASES_A[done:]]

        def walk(**stages):
            now = {k: next(g, None) for k, g in stages.items()}
            for k, phase in order():
                if k in stages and now[k] == phase:
                    now[k] = next(stages[k], None)
            assert all(v is None for v in now.values()), now

        def trips(eng, stage_a, stage_b):
            walk(A=stage_a(eng, 0))
            with eng.Fori(1, TRIPS) as it:
                walk(A=stage_a(eng, it), B=stage_b(eng, it - 1))
            walk(B=stage_b(eng, TRIPS - 1))

        block = stack.enter_context(nc.Block())

        def sp_stage_a(sp, it):
            at = it * PAIR if isinstance(it, int) else sp.snap(it * PAIR)
            yield "pg"
            if not isinstance(it, int):
                sp.wait_ge(x2_ready, due(x2_ready, it, 0))
            sp.dma_start(CTX[:, :, :], ctxt[bass.ds(at, PAIR)].rearrange("b c n -> c b n")).then_inc(pair_in, 16)
            sp.dma_start(X0[:, :, :], x[bass.ds(at, PAIR)].rearrange("b c n -> c b n")).then_inc(pair_in, 16)
            sp.dma_start(MASK8[:, :, :], kv_mask[bass.ds(at, PAIR)].partition_broadcast(P)).then_inc(pair_in, 16)
            yield "k"
            sp.wait_ge(mbias_ready, due(mbias_ready, it, 1))
            sp.dma_start(mask_dram, MBIAS[0:H1, :]).then_inc(mask_out, 16)
            sp.wait_ge(kp_ready, due(kp_ready, it, 1))
            sp.dma_start(k_dram.rearrange("s c n -> c s n"), QKP[:, 1, :, :]).then_inc(parts_out, 16)
            sp.wait_ge(mask_out, due(mask_out, it, 16))
            sp.dma_start(KS[ROW_MASK:ROW_MASK + 1, :, :], mask_dram.rearrange("(o h) n -> o h n", o=1)).then_inc(stack_in, 16)
            sp.wait_ge(parts_out, due(parts_out, it, 16))
            for i in range(NSPLIT * NSPLIT):
                sp.dma_start(KS[D1 * i:D1 * i + D1, :, :],
                             k_dram[i % NSPLIT].rearrange("(h d) n -> d h n", d=D1)).then_inc(stack_in, 16)
            yield "q"
            sp.wait_ge(qp_ready, due(qp_ready, it, 1))
            sp.dma_start(q_dram.rearrange("s c n -> c s n"), QKP[:, 0, :, :]).then_inc(parts_out, 16)
            sp.wait_ge(parts_out, due(parts_out, it, 32))
            for i in range(NSPLIT * NSPLIT):
                sp.dma_start(QS[D1 * i:D1 * i + D1, :, :],
                             q_dram[i // NSPLIT].rearrange("(h d) n -> d h n", d=D1)).then_inc(stack_in, 16)
            for b in range(PAIR):
                yield ("max", b)
                sp.wait_ge(m_parts, due(m_parts, it, b + 1))
                sp.dma_start(max_dram[b], NMP[:, :, :]).then_inc(maxp_out, 16)
                sp.wait_ge(maxp_out, due(maxp_out, it, 16 * (b + 1)))
                sp.dma_start(QS[ROW_MAX:ROW_MAX + NSPLIT, :, b * N:(b + 1) * N],
                             max_dram[b].rearrange("h s n -> s h n")).then_inc(maxp_in[b], 16)

        def nothing(eng, it):
            return
            yield

        @block.sync
        def _(sp):
            sp.dma_start(col[:, :], cols).then_inc(wa_in, 16)
            sp.dma_start(row[:, :], rows.partition_broadcast(P)).then_inc(wa_in, 16)
            sp.dma_start(WA[:, 0:4, :], wa).then_inc(wa_in, 16)
            sp.dma_start(WWT[:, :], ww_t).then_inc(wa_in, 16)
            sp.dma_start(THW[:, :], theta_w).then_inc(wa_in, 16)
            sp.wait_ge(const_ready, 1)
            sp.wait_ge(zero_ready, 3)
            trips(sp, sp_stage_a, nothing)
            sp.wait_ge(out_stored, 16 * (TRIPS + 1))

        def pool_stage_a(pool, it):
            yield "bt"
            pool.wait_ge(v_ready, due(v_ready, it, 1))
            nc.gpsimd.tensor_tensor(VH[:, :, :, D1:2 * D1], VH[:, :, :, 0:D1], VH[:, :, :, 0:D1], ALU.mult).then_inc(vsq_ready, 1)

            yield "x2"
            pool.wait_ge(x2_ready, due(x2_ready, it, 1))
            pool.wait_ge(const_step, 1)

        def pool_stage_b(pool, it):
            for u in range(4):
                yield ("norm", u, 0)
                hs = slice(4 * half_at(u, 0), 4 * half_at(u, 0) + 8)
                pool.wait_ge(rsum_inv, due(rsum_inv, it, u + 1))
                nc.gpsimd.tensor_tensor(SM[:, hs, :], SM[:, hs, :], RR2[:, hs].unsqueeze(2).to_broadcast([P, 8, C]),
                                        ALU.mult).then_inc(p_norm_pool, 1)
            for f in range(NF):
                yield ("mix", f)
                pool.wait_ge(mix_used, due(mix_used, it, f + 1))
                nc.gpsimd.tensor_tensor(XMX[:, f, :, :], XMX[:, f, :, :], LNT[:, :, :], ALU.add).then_inc(mix_ready, 1)
            yield "fv"
            pool.wait_ge(yo_ready, due(yo_ready, it, 1))
            pool.wait_ge(const_step, 1)

        @block.gpsimd
        def _(pool):
            pool.memset(ident[:, :], 0.0).then_inc(const_step, 1)
            pool.wait_ge(const_step, 1)
            pool.affine_select(out=ident[:, :], in_=ident[:, :], compare_op=ALU.not_equal, fill=1.0, base=0,
                               pattern=[[-1, P]], channel_multiplier=1).then_inc(const_step, 1)
            pool.wait_ge(zero_ready, 1)
            pool.wait_ge(const_step, 2)
            pool.affine_select(out=QS[64:ROW_MAX, :, :], in_=QS[64:ROW_MAX, :, :], compare_op=ALU.not_equal, fill=1.0,
                               base=64 - ROW_MASK, pattern=[[0, H1], [0, PAIR * N]], channel_multiplier=1).then_inc(const_ready, 1)
            trips(pool, pool_stage_a, pool_stage_b)

        def load_stage_b(act, at):
            act.dma_start(CMASK[:, :, :], cross_mask[bass.ds(at, PAIR)].rearrange("b s t -> s b t")).then_inc(cross_in, 16)
            for b in range(PAIR):
                for e in range(2):
                    act.dma_start(S0[:, e, b, :], ctxt[bass.ds(at + b, 1), 2:2 + D3, :].rearrange("o r n -> (o r n)")
                                  .rearrange("(e p j) -> e p j", e=2, j=D3)[e]).then_inc(state_in, 16)

        def act_stage_a(act, it):
            yield "pg"
            if not isinstance(it, int):
                act.wait_ge(enc_moved, due(enc_moved, it, 0))
            act.wait_ge(enc_tr, due(enc_tr, it, 1))
            nc.scalar.activation(ENC_A[:, :, :], PA[:, 3, :], ACT.Copy).then_inc(enc_ready, 1)
            yield "mt"
            act.wait_ge(mt_mm, due(mt_mm, it, 1))
            nc.scalar.activation(MT[:, :, :], PA[0:CI, 1, 0:PAIR * CI], ACT.Copy, scale=1.0 / N).then_inc(mt_ready, 1)
            yield "k"
            act.wait_ge(k_mm, due(k_mm, it, 1))
            nc.scalar.activation(QK[:, 1, :], PA[:, 3, :], ACT.Identity, bias=cv("bk1")).then_inc(k_ready, 1)
            yield "bt"
            act.wait_ge(bt_mm, due(bt_mm, it, 1))
            nc.scalar.activation(BT[:, :, :], PA[:, 1, 0:N], ACT.Copy).then_inc(bt_ready, 1)
            yield "y"
            act.wait_ge(y_added, due(y_added, it, 1))
            for b in range(PAIR):
                last = nc.scalar.activation(X1[:, b, :], X1[:, b, :], ACT.Identity, bias=SH[:, b:b + 1])
            last.then_inc(x1_ready, 1)
            yield "q"
            act.wait_ge(q_mm, due(q_mm, it, 1))
            nc.scalar.activation(QK[:, 0, :], PA[:, 1, :], ACT.Identity, bias=bq1s[:, :], scale=float(D1) ** -0.5).then_inc(q_ready, 1)
            yield "norm"
            act.wait_ge(ivar_ready, due(ivar_ready, it, 1))
            nc.scalar.activation(IST[:, 6, :], IST[:, 5, :], ACT.Sqrt).then_inc(istd_ready, 1)
            for u in range(PAIR * H1):
                yield ("t", u // H1, u % H1)
                act.wait_ge(t_mm, due(t_mm, it, u + 1))
                if u >= 2 * G:
                    act.wait_ge(pv_mm, due(pv_mm, it, (u - 2 * G) // G + 1))
                nc.scalar.activation(PT[:, u % (2 * G), :, :], PA[:, u % 2, :], ACT.Exp).then_inc(t_exp, 1)
            yield "var"
            act.wait_ge(var_ready, due(var_ready, it, 1))
            nc.scalar.activation(SQ[:, :, :], EX[:, :, :], ACT.Sqrt).then_inc(std_ready, 1)
            yield "x2"
            act.wait_ge(x2_ready, due(x2_ready, it, 1))

        def act_ln(act, it, i, s, b):
            yield ("ln", i)
            act.wait_ge(ln_var, due(ln_var, it, i + 1))
            nc.scalar.activation(SDV[:, :], BMV[:, :, 1], ACT.Sqrt, bias=eps[:, :]).then_inc(ln_sd, 1)
            if i == 0:
                nc.scalar.activation(ENC[:, :, :], ENC_A[:, :, :], ACT.Copy).then_inc(enc_moved, 1)
            yield ("hat", i)
            act.wait_ge(ln_tr, due(ln_tr, it, i + 1))
            nc.scalar.activation(LNT[:, 0, :], PB[:, 0, 0:T], ACT.Identity, bias=cv(b, 0), scale=cv(s, 0)).then_inc(ln_ready_act, 1)

        def act_tail(act, it, u):
            yield ("tail", u)
            act.wait_ge(ctx_mm, due(ctx_mm, it, u + 1))
            nc.scalar.activation(CT2[:, :, :], PB[:, half_at(u, 0), 0:N], ACT.Copy).then_inc(ct_ready, 1)

        def act_stage_b(act, it):
            for a in range(2):
                yield from act_ln(act, it, a, *(("ln1_s", "ln1_b"), ("ln2_s", "ln2_b"))[a])
                yield ("qk", a)
                act.wait_ge(kp_mm, due(kp_mm, it, a + 1))
                for c in range(2):
                    last = nc.scalar.activation(KT[:, c, :], PB[:, 1, c * T:(c + 1) * T], ACT.Identity,
                                                bias=cv(("bk_self", "bk_cross")[a], c))
                last.then_inc(kt_ready, 1)
                for b in range(PAIR):
                    u = 2 * a + b
                    if b:
                        yield from act_tail(act, it, u - 1)
                    for i in range(2):
                        yield ("exp", u, i)
                        act.wait_ge(sc_nmax, due(sc_nmax, it, 2 * u + i + 1))
                        for h in range(4 * half_at(u, i), 4 * half_at(u, i) + 8):
                            last = nc.scalar.activation(SM[:, h, :], SM[:, h, :], ACT.Exp, bias=NMX2[:, h:h + 1],
                                                        accum_out=RS2[:, h:h + 1])
                        last.then_inc(sc_exp, 1)
                    yield ("turn", u, 1)
                    act.wait_ge(p_tr, due(p_tr, it, 2 * u + 2))
                    k = half_at(u, 1)
                    nc.scalar.activation(PT2[:, 4 * k:4 * k + 4, :], PB[:, k, :], ACT.Copy).then_inc(p_out_act, 1)
                yield from act_tail(act, it, 2 * a + 1)
            yield from act_ln(act, it, 2, "ln3_s", "ln3_b")
            for o in range(FF // P):
                if o % 2 == 0:
                    yield ("ff", o // 2)
                act.wait_ge(ff_mm, due(ff_mm, it, o // 2 * 2 + 2))
                nc.scalar.activation(HF[:, o, :], PB[:, o // 2, (o % 2) * T:(o % 2 + 1) * T], ACT.Gelu_apprx_tanh,
                                     bias=cv("b1", o)).then_inc(ff_act, 1)
            yield from act_ln(act, it, 3, "l3ln1_s", "l3ln1_b")
            yield "tx"
            act.wait_ge(tx_mm, due(tx_mm, it, 1))
            nc.scalar.activation(TX[:, :], PB[:, 0, 0:T], ACT.Tanh)
            nc.scalar.activation(TXB[:, :], PB[0:DM, 0, T:2 * T], ACT.Tanh).then_inc(tx_ready, 1)
            yield "td1"
            act.wait_ge(td1_mm, due(td1_mm, it, 1))
            nc.scalar.activation(TD[:, :], PB[0:DD, 1, 0:T], ACT.Tanh).then_inc(td1_ready, 1)
            yield "td2"
            act.wait_ge(td2_mm, due(td2_mm, it, 1))
            for e in range(2):
                last = nc.scalar.activation(EX3[:, e, :], PB[:, 1, e * T:(e + 1) * T], ACT.Exp, bias=cv("decay", e))
            link(act, "act_b", it, last)
            nc.scalar.activation(WS[:, :, :, 1:C].rearrange("p e b t -> p (e b) t"),
                                 EX3[:, :, :].rearrange("p e (b t) -> p (e b) t", b=PAIR)[:, :, 0:C - 1], ACT.Exp,
                                 scale=-1.0).then_inc(w_ready, 1)
            yield "k3"
            act.wait_ge(k3_mm, due(k3_mm, it, 1))
            nc.scalar.activation(K3[:, :, :], PB[:, 3, :], ACT.Copy).then_inc(k3_ready, 1)
            yield "r3"
            act.wait_ge(r3_mm, due(r3_mm, it, 1))
            act.wait_ge(out_stored, due(out_stored, it, 16))
            nc.scalar.activation(R3[:, :, :], PB[:, 0, :], ACT.Copy).then_inc(r3_ready, 1)
            yield "g3"
            act.wait_ge(g3_mm, due(g3_mm, it, 1))
            nc.scalar.activation(Q3[:, :, :], PB[:, 1, :], ACT.Tanh, scale=0.5).then_inc(g3_tanh, 1)
            yield "centre"
            act.wait_ge(cen_mm, due(cen_mm, it, 1))
            nc.scalar.activation(Q3[:, :, :], PB[:, 2, :], ACT.Square).then_inc(cen_sq, 1)
            yield "gvar"
            act.wait_ge(gvar_mm, due(gvar_mm, it, 1))
            nc.scalar.activation(XI[:, :, :], PB[:, 3, :], ACT.Sqrt, bias=eps[:, :]).then_inc(gsd_ready, 1)
            yield from act_ln(act, it, 4, "l3ln2_s", "l3ln2_b")
            yield "xk"
            act.wait_ge(fk_mm, due(fk_mm, it, 1))
            link(act, "act_b", it, nc.scalar.activation(Q3[:, :, :], PB[:, 0, :], ACT.Relu))
            nc.scalar.activation(Q3[:, :, :], Q3[:, :, :], ACT.Square).then_inc(fk_ready, 1)
            yield "fr"
            act.wait_ge(fr_mm, due(fr_mm, it, 1))
            nc.scalar.activation(FR[:, :, :], PB[:, 1, :], ACT.Tanh, scale=0.5).then_inc(fr_tanh, 1)
            yield "fv"
            at = it * PAIR if isinstance(it, int) else act.snap(it * PAIR)
            act.wait_ge(yo_ready, due(yo_ready, it, 1))
            act.dma_start(out[bass.ds(at, PAIR)].rearrange("b s n -> s b n"), FR[:, :, :]).then_inc(out_stored, 16)
            if not isinstance(it, int):
                load_stage_b(act, act.snap((it + 1) * PAIR))
            chain_end("act_b")

        @block.scalar
        def _(act):
            act.dma_start(WH[:, :, :], wh).then_inc(wb_in, 16)
            act.dma_start(WO[:, :, :, :], wo).then_inc(wb_in, 16)
            act.dma_start(SMASK[:, :], self_mask).then_inc(wb_in, 16)
            act.dma_start(W1[:, :, :], w_ff1).then_inc(wb_in, 16)
            act.dma_start(W2[:, :, :], w_ff2).then_inc(wb_in, 16)
            act.dma_start(W3[:, :, :, :], w3).then_inc(wb_in, 16)
            act.dma_start(MW1[:, :, :], maa_w1.rearrange("(c p) n -> p c n", p=P)).then_inc(wb_in, 16)
            act.dma_start(MW2[:, :], maa_w2[0:P]).then_inc(wb_in, 16)
            act.dma_start(MW2B[:, :], maa_w2[P:P + DM]).then_inc(wb_in, 16)
            act.dma_start(TW1[:, :, :], td_w1.rearrange("(c p) n -> p c n", p=P)).then_inc(wb_in, 16)
            act.dma_start(TW2[:, :], td_w2).then_inc(wb_in, 16)
            act.dma_start(SEL[:, :, :], sel).then_inc(wb_in, 16)
            act.dma_start(GATHER[:, :], gather).then_inc(wb_in, 16)
            load_stage_b(act, 0)
            act.wait_ge(bn_var1, 1)
            nc.scalar.activation(bn_s[:, 1:2], bn_s[:, 2:3], ACT.Sqrt).then_inc(bn_sd, 1)
            nc.scalar.activation(bq1s[:, :], cv("bq1"), ACT.Copy, scale=float(D1) ** -0.5).then_inc(bn_sd, 1)
            act.wait_ge(bn_sd, 2)
            nc.scalar.activation(R3[:, 0, 0:1], cv("bq1"), ACT.Copy).then_inc(out_stored, 16)
            trips(act, act_stage_a, act_stage_b)
            act.wait_ge(out_stored, 16 * (TRIPS + 1))

        def dve_stage_a(dve, it):
            v = nc.vector

            def step(ins):
                link(dve, "dve_a", it, ins)

            def split(i):
                step(v.tensor_copy(QKP[:, i, 0, :], QK[:, i, :]))
                step(v.tensor_tensor(RES[:, i, :], QK[:, i, :], QKP[:, i, 0, :], ALU.subtract))
                step(v.tensor_copy(QKP[:, i, 1, :], RES[:, i, :]))
                return v.tensor_tensor(QKP[:, i, 2, :], RES[:, i, :], QKP[:, i, 1, :], ALU.subtract)

            yield "pg"
            dve.wait_ge(pair_in, due(pair_in, it, 48))
            v.tensor_copy(MF[:, :, :], MASK8[:, :, :])
            v.tensor_scalar(MBIAS[:, :].rearrange("p (b n) -> p b n", b=PAIR), MASK8[:, :, :], -1.0, 1e30, ALU.add,
                            ALU.mult).then_inc(mbias_ready, 1)
            dve.wait_ge(pg_mm, due(pg_mm, it, 1))
            v.tensor_tensor(PG[:, :, :], PA[:, 0, :].rearrange("p (a n) -> p a n", n=128),
                            rv("phi_g_b").unsqueeze(1).to_broadcast([P, 4, 128]), ALU.add).then_inc(pg_ready, 1)
            yield "k"
            dve.wait_ge(at_mm, due(at_mm, it, 1))
            v.tensor_copy(AT[:, :, :], PA[0:CI, 2, 0:N].rearrange("p (b n) -> p b n", b=PAIR)).then_inc(at_ready, 1)
            dve.wait_ge(k_ready, due(k_ready, it, 1))
            split(1).then_inc(kp_ready, 1)
            yield "bt"
            dve.wait_ge(bt_ready, due(bt_ready, it, 1))
            v.tensor_scalar(SH[:, :], PA[:, 1, N:N + PAIR], bn_s[:, 0:1], bn_s[:, 2:3], ALU.mult, ALU.add).then_inc(sh_ready, 1)
            dve.wait_ge(v_mm, due(v_mm, it, 1))
            v.tensor_tensor(VH[:, :, :, 0:D1], PA[:, 2, :].rearrange("p (a h d) -> p a h d", a=4, d=D1),
                            rv("bv1").rearrange("p (h d) -> p h d", d=D1).unsqueeze(1).to_broadcast([P, 4, H1, D1]),
                            ALU.add).then_inc(v_ready, 1)
            yield "y"
            dve.wait_ge(y_mm, due(y_mm, it, 1))
            v.scalar_tensor_tensor(out=X1[:, :, :], in0=PA[:, 0, :].rearrange("p (b n) -> p b n", b=PAIR), scalar=bn_s[:, 0:1],
                                   in1=X0[:, :, :], op0=ALU.mult, op1=ALU.add).then_inc(y_added, 1)
            yield "q"
            dve.wait_ge(q_ready, due(q_ready, it, 1))
            split(0).then_inc(qp_ready, 1)
            yield "norm"
            dve.wait_ge(mbias_ready, due(mbias_ready, it, 1))
            step(v.tensor_tensor(X1[:, :, :], X1[:, :, :], MF[:, :, :], ALU.mult))
            step(v.tensor_tensor(XN[:, :, :], X1[:, :, :], X1[:, :, :], ALU.mult))
            v.tensor_reduce(IST[:, 0, :], MF[:, :, :], AX.X, ALU.add)
            v.tensor_reduce(IST[:, 1, :], X1[:, :, :], AX.X, ALU.add)
            step(v.tensor_reduce(IST[:, 2, :], XN[:, :, :], AX.X, ALU.add))
            step(v.reciprocal(IST[:, 3, :], IST[:, 0, :]))
            step(v.tensor_tensor(IST[:, 4, :], IST[:, 1, :], IST[:, 3, :], ALU.mult))
            v.tensor_tensor(IST[:, 2, :], IST[:, 2, :], IST[:, 3, :], ALU.mult)
            step(v.tensor_tensor(IST[:, 5, :], IST[:, 4, :], IST[:, 4, :], ALU.mult))
            step(v.tensor_tensor(IST[:, 5, :], IST[:, 2, :], IST[:, 5, :], ALU.subtract))
            v.tensor_scalar(IST[:, 5, :], IST[:, 5, :], 0.0, EPS, ALU.max, ALU.add).then_inc(ivar_ready, 1)
            yield "unit"
            dve.wait_ge(istd_ready, due(istd_ready, it, 1))
            step(v.reciprocal(IST[:, 7, :], IST[:, 6, :]))
            for b in range(PAIR):
                last = v.tensor_scalar(XN[:, b, :], X1[:, b, :], IST[:, 4, b:b + 1], IST[:, 7, b:b + 1], ALU.subtract, ALU.mult)
            step(last)
            step(v.tensor_tensor(XN[:, :, :], XN[:, :, :], MF[:, :, :], ALU.mult))
            for b in range(PAIR):
                for h in range(H1):
                    u = b * H1 + h
                    yield ("s", b, h)
                    dve.wait_ge(s_mm, due(s_mm, it, u + 1))
                    v.tensor_reduce(MX[:, b, :, h], PA[:, u % 2, :].rearrange("p (q k) -> p q k", q=2), AX.X,
                                    ALU.max).then_inc(s_max, 1)
                yield ("max", b)
                dve.wait_ge(m_tr, due(m_tr, it, b + 1))
                if b:
                    dve.wait_ge(maxp_out, due(maxp_out, it, 16 * b))
                step(v.tensor_scalar(NM[:, 0, :], PA[0:H1, 3, 0:N], -1.0, None, ALU.mult))
                step(v.tensor_copy(NMP[:, 0, :], NM[:, 0, :]))
                step(v.tensor_tensor(NM[:, 1, :], NM[:, 0, :], NMP[:, 0, :], ALU.subtract))
                step(v.tensor_copy(NMP[:, 1, :], NM[:, 1, :]))
                v.tensor_tensor(NMP[:, 2, :], NM[:, 1, :], NMP[:, 1, :], ALU.subtract).then_inc(m_parts, 1)
            for b in range(PAIR):
                for t in range(HT):
                    yield ("t", b, G * t + 2 * G - 1)
                    dve.wait_ge(pv_mm, due(pv_mm, it, b * HT + t + 1))
                    if b and t == 0:
                        dve.wait_ge(ot_tr, due(ot_tr, it, 2 * b))
                    v.tensor_copy(OT[:, t, :], PA[:, 2 + t % 2, 0:N]).then_inc(pv_out, 1)
                for q in range(2):
                    yield ("o", b, q)
                    dve.wait_ge(ot_tr, due(ot_tr, it, 2 * b + q + 1))
                    heads = PA[:, 2, :].rearrange("p (h d) -> p h d", d=32)
                    step(v.reciprocal(RSUM[:, :], heads[:, :, 2 * D1]))
                    scale = RSUM[:, :].unsqueeze(2).to_broadcast([P, H1, D1])
                    v.tensor_tensor(MN[:, 2 * b + q, :].rearrange("p (h d) -> p h d", d=D1), heads[:, :, 0:D1], scale, ALU.mult)
                    v.tensor_tensor(EX[:, 2 * b + q, :].rearrange("p (h d) -> p h d", d=D1), heads[:, :, D1:2 * D1], scale,
                                    ALU.mult).then_inc(ot_out, 1)
            yield "var"
            dve.wait_ge(ot_out, due(ot_out, it, 4))
            step(v.tensor_tensor(SQ[:, :, :], MN[:, :, :], MN[:, :, :], ALU.mult))
            step(v.tensor_tensor(EX[:, :, :], EX[:, :, :], SQ[:, :, :], ALU.subtract))
            v.tensor_scalar(EX[:, :, :], EX[:, :, :], 0.0, None, ALU.max).then_inc(var_ready, 1)
            yield "x2"
            dve.wait_ge(ms_tr, due(ms_tr, it, 1))
            step(v.tensor_tensor(XN[:, :, :], XN[:, :, :], PA[:, 3, :].rearrange("p (b n) -> p b n", b=PAIR), ALU.mult))
            step(v.tensor_tensor(XN[:, :, :], XN[:, :, :], PA[:, 2, :].rearrange("p (b n) -> p b n", b=PAIR), ALU.add))
            v.tensor_tensor(X2[:, :, :], XN[:, :, :], MF[:, :, :], ALU.mult).then_inc(x2_ready, 1)
            dve.wait_ge(x2_ready, due(x2_ready, it, 1))
            chain_end("dve_a")

        def dve_stage_b(dve, it):
            v = nc.vector

            def step(ins):
                link(dve, "dve_b", it, ins)

            def ln(i, src, names, meanwhile=None):
                yield ("ln", i)
                for b in range(PAIR):
                    last = v.bn_stats(BST[:, b, :], src[:, b, :])
                step(last)
                v.memset(cell[:, :], 0.0)
                for b in range(PAIR):
                    last = v.bn_aggr(BMV[:, b, :], BST[:, b, :])
                last.then_inc(ln_var, 1)
                yield ("hat", i)
                dve.wait_ge(ln_sd, due(ln_sd, it, i + 1))
                step(v.reciprocal(RSD[:, :], SDV[:, :]))
                for b in range(PAIR):
                    last = v.tensor_scalar(XH[:, b, :], src[:, b, :], BMV[:, b, 0:1], RSD[:, b:b + 1], ALU.subtract, ALU.mult)
                last.then_inc(ln_hat, 1)
                if meanwhile:
                    meanwhile()
                dve.wait_ge(ln_tr, due(ln_tr, it, i + 1))
                v.tensor_scalar(LNT[:, 1, :], PB[:, 1, 0:T], cv(names[0], 1), cv(names[1], 1), ALU.mult, ALU.add).then_inc(ln_ready_dve, 1)

            def add_bias(i, src, name):
                dve.wait_ge(ln_hat, due(ln_hat, it, i + 1))
                step(v.tensor_tensor(X3[:, :, :], src[:, :, :], rv(name).unsqueeze(1).to_broadcast([P, PAIR, N]), ALU.add))

            def tail(u):
                yield ("tail", u)
                dve.wait_ge(ao_mm, due(ao_mm, it, u + 1))
                v.tensor_tensor(X3[:, u % 2, :], X3[:, u % 2, :], PB[:, half_at(u, 0) + 1, 0:N], ALU.add).then_inc(res_ready, 1)

            dve.wait_ge(wb_in, 16 * 13)
            for a in range(2):
                src = (X2, X3)[a]
                yield from ln(a, src, (("ln1_s", "ln1_b"), ("ln2_s", "ln2_b"))[a], lambda: add_bias(a, src, ("b_ao", "b_co")[a]))
                yield ("qk", a)
                if a == 0:
                    dve.wait_ge(cross_in, due(cross_in, it, 16))
                    v.tensor_scalar(CFILL[:, :, :], CMASK[:, :, :], -1.0, 10000.0, ALU.add, ALU.mult)
                    step(v.tensor_scalar(SFILL[:, :], SMASK[:, :], -1.0, 10000.0, ALU.add, ALU.mult))
                dve.wait_ge(qp_mm, due(qp_mm, it, a + 1))
                for c in range(2):
                    for par in range(2):
                        last = v.tensor_scalar(QT[:, 2 * c + par, :], PB[:, 0, c * T:(c + 1) * T], cv("parity", par),
                                               cv(("bq_self", "bq_cross")[a], 2 * c + par), ALU.mult, ALU.add)
                last.then_inc(qt_ready, 1)
                yield ("v", a)
                dve.wait_ge(vp_mm, due(vp_mm, it, a + 1))
                for par in range(2):
                    pair_of = lambda x: x.rearrange("p b (h r d) -> p b h r d", r=2, d=D2)[:, :, :, par, :]
                    bias = rv(("bv_self", "bv_cross")[a]).unsqueeze(1).to_broadcast([P, PAIR, N])
                    last = v.tensor_tensor(V2[:, :, :, :].rearrange("p b (h r) d -> p b h r d", r=2)[:, :, :, par, par * D2:(par + 1) * D2],
                                           pair_of(PB[:, 2, :].rearrange("p (b n) -> p b n", b=PAIR)), pair_of(bias), ALU.add)
                last.then_inc(v2_ready, 1)
                for b in range(PAIR):
                    u = 2 * a + b
                    mask, fill = (SMASK[:, :], SFILL[:, :]) if a == 0 else (CMASK[:, b, :], CFILL[:, b, :])
                    for i in range(2):
                        yield ("score", u, i)
                        dve.wait_ge(sc_mm, due(sc_mm, it, 2 * u + i + 1))
                        k = half_at(u, i)
                        hs = slice(4 * k, 4 * k + 8)
                        step(v.scalar_tensor_tensor(out=SM[:, hs, :], in0=PB[:, k:k + 2, :].rearrange("p g (t k) -> p (g t) k", k=C),
                                                    scalar=float(D2) ** -0.5, in1=mask.unsqueeze(1).to_broadcast([P, 8, C]),
                                                    op0=ALU.mult, op1=ALU.mult))
                        step(v.tensor_tensor(SM[:, hs, :], SM[:, hs, :], fill.unsqueeze(1).to_broadcast([P, 8, C]), ALU.add))
                        step(v.tensor_reduce(MX2[:, hs], SM[:, hs, :], AX.X, ALU.max))
                        v.tensor_scalar(NMX2[:, hs], MX2[:, hs], -1.0, None, ALU.mult).then_inc(sc_nmax, 1)
                        if b and i == 0:
                            yield from tail(u - 1)
                    for i in range(2):
                        yield ("norm", u, i)
                        dve.wait_ge(sc_exp, due(sc_exp, it, 2 * u + i + 1))
                        hs = slice(4 * half_at(u, i), 4 * half_at(u, i) + 8)
                        if i == 0:
                            v.reciprocal(RR2[:, hs], RS2[:, hs]).then_inc(rsum_inv, 1)
                        else:
                            step(v.reciprocal(RR2[:, hs], RS2[:, hs]))
                            v.tensor_tensor(SM[:, hs, :], SM[:, hs, :], RR2[:, hs].unsqueeze(2).to_broadcast([P, 8, C]),
                                            ALU.mult).then_inc(p_norm_dve, 1)
                    for i in range(2):
                        yield ("turn", u, i)
                        dve.wait_ge(p_tr, due(p_tr, it, 2 * u + i + 1))
                        k = half_at(u, i) + i
                        v.tensor_copy(PT2[:, 4 * k:4 * half_at(u, i) + 8, :],
                                      PB[:, k:half_at(u, i) + 2, :].rearrange("p g (t k) -> p (g t) k", k=C)).then_inc(p_out_dve, 1)
                yield from tail(2 * a + 1)
                dve.wait_ge(res_ready, due(res_ready, it, 2 * a + 2))
            yield from ln(2, X3, ("ln3_s", "ln3_b"), lambda: add_bias(2, X3, "b2"))
            yield "ff2"
            dve.wait_ge(ff2_mm, due(ff2_mm, it, 1))
            v.tensor_tensor(X3[:, :, :], X3[:, :, :], PB[:, 0, :].rearrange("p (b n) -> p b n", b=PAIR), ALU.add).then_inc(x4_ready, 1)
            dve.wait_ge(x4_ready, due(x4_ready, it, 1))

            def shift(i):
                dve.wait_ge(ln_ready_act, due(ln_ready_act, it, 4 + i))
                dve.wait_ge(ln_ready_dve, due(ln_ready_dve, it, 4 + i))
                new = LNT[:, :, :].rearrange("p e (b t) -> p (e b) t", b=PAIR)
                old = ENC[:, :, :].rearrange("p e (b t) -> p (e b) t", b=PAIR)
                to = SX[:, :, :].rearrange("p e (b t) -> p (e b) t", b=PAIR)
                v.tensor_tensor(to[:, :, 1:C], new[:, :, 0:C - 1], new[:, :, 1:C], ALU.subtract)
                step(v.tensor_tensor(to[:, :, 0:1], old[:, :, 1 - i:2 - i], new[:, :, 0:1], ALU.subtract))

            yield from ln(3, X3, ("l3ln1_s", "l3ln1_b"))
            yield "xi"
            shift(0)
            for e in range(2):
                last = v.scalar_tensor_tensor(out=XI[:, e, :], in0=SX[:, e, :], scalar=cv("maa_x", e), in1=LNT[:, e, :],
                                              op0=ALU.mult, op1=ALU.add)
            last.then_inc(xi_ready, 1)
            for f in range(NF):
                yield ("mix", f)
                dve.wait_ge(mix_mm, due(mix_mm, it, f + 1))
                for e in range(2):
                    last = v.scalar_tensor_tensor(out=XMX[:, f, e, :], in0=PB[:, f % 4, e * T:(e + 1) * T],
                                                  scalar=cv("stack", 2 * f + e), in1=SX[:, e, :], op0=ALU.add, op1=ALU.mult)
                last.then_inc(mix_used, 1)
            yield "v3"
            dve.wait_ge(v3_mm, due(v3_mm, it, 1))
            v.tensor_copy(V3[:, :, :], PB[:, 2, :].rearrange("p (e t) -> p e t", e=2)).then_inc(v3_ready, 1)
            yield "g3"
            dve.wait_ge(g3_tanh, due(g3_tanh, it, 1))
            v.scalar_tensor_tensor(out=G3[:, :, :], in0=Q3[:, :, :], scalar=1.0, in1=PB[:, 1, :].rearrange("p (e t) -> p e t", e=2),
                                   op0=ALU.add, op1=ALU.mult).then_inc(g3_ready, 1)
            yield "ruk"
            dve.wait_ge(k3_ready, due(k3_ready, it, 1))
            dve.wait_ge(r3_ready, due(r3_ready, it, 1))
            dve.wait_ge(w_ready, due(w_ready, it, 1))
            dve.wait_ge(state_in, due(state_in, it, 64))
            for e in range(2):
                last = v.scalar_tensor_tensor(out=RUK[:, e, :], in0=R3[:, e, :], scalar=cv("u", e), in1=K3[:, e, :],
                                              op0=ALU.mult, op1=ALU.mult)
            last.then_inc(ruk_ready, 1)
            for e in range(2):
                yield ("spread", e, 0)
                v.tensor_copy(KV3[:, :, :, 0:1].rearrange("p j b o -> p j (b o)"), S0[:, e, :, :].rearrange("p b j -> p j b"))
                for half in range(2):
                    if half:
                        yield ("spread", e, 1)
                    dve.wait_ge(sp_mm, due(sp_mm, it, 2 * e + half + 1))
                    js = slice(4 * half, 4 * half + 4)
                    k = K3[:, e, :].rearrange("p (b t) -> p b t", b=PAIR)[:, :, 0:C - 1]
                    v.tensor_tensor(KV3[:, js, :, 1:C],
                                    PB[:, 2 * half:2 * half + 2, :].rearrange("p x (y b t) -> p (x y) b t", y=2, b=PAIR)[:, :, :, 0:C - 1],
                                    k.unsqueeze(1).to_broadcast([P, 4, PAIR, C - 1]), ALU.mult).then_inc(kv_ready, 1)
                dve.wait_ge(kv_ready, due(kv_ready, it, 2 * e + 2))
                for j in range(D3):
                    last = v.tensor_tensor_scan(ST3[:, e, j, :], WS[:, e, :, :].rearrange("p b t -> p (b t)"),
                                                KV3[:, j, :, :].rearrange("p b t -> p (b t)"), 0.0, ALU.mult, ALU.add)
                step(last)
                v.tensor_tensor(ST3[:, e, :, :], ST3[:, e, :, :], R3[:, e, :].unsqueeze(1).to_broadcast([P, D3, T]),
                                ALU.mult).then_inc(y3_ready, 1)
            yield "bonus"
            dve.wait_ge(bonus_mm, due(bonus_mm, it, 1))
            step(v.tensor_tensor(O3[:, :, :], PB[:, 1, :].rearrange("p (e t) -> p e t", e=2), V3[:, :, :], ALU.mult))
            v.tensor_tensor(O3[:, :, :], O3[:, :, :], PB[:, 0, :].rearrange("p (e t) -> p e t", e=2), ALU.add).then_inc(o3_ready, 1)
            yield "og"
            dve.wait_ge(gsd_ready, due(gsd_ready, it, 1))
            step(v.reciprocal(XI[:, :, :], XI[:, :, :]))
            step(v.tensor_tensor(XI[:, :, :], PB[:, 2, :].rearrange("p (e t) -> p e t", e=2), XI[:, :, :], ALU.mult))
            for e in range(2):
                last = v.tensor_scalar(XI[:, e, :], XI[:, e, :], cv("gn_w", e), cv("gn_b", e), ALU.mult, ALU.add)
            step(last)
            v.tensor_tensor(XI[:, :, :], XI[:, :, :], G3[:, :, :], ALU.mult).then_inc(og_ready, 1)
            yield "wo"
            dve.wait_ge(wo_mm, due(wo_mm, it, 1))
            step(v.scalar_tensor_tensor(out=X3[:, :, :], in0=PB[:, 0, :].rearrange("p (b n) -> p b n", b=PAIR), scalar=0.5,
                                        in1=X3[:, :, :], op0=ALU.mult, op1=ALU.add))
            yield from ln(4, X3, ("l3ln2_s", "l3ln2_b"))
            yield "xk"
            shift(1)
            for e in range(2):
                v.scalar_tensor_tensor(out=XI[:, e, :], in0=SX[:, e, :], scalar=cv("mk", e), in1=LNT[:, e, :],
                                       op0=ALU.mult, op1=ALU.add)
                last = v.scalar_tensor_tensor(out=XR[:, e, :], in0=SX[:, e, :], scalar=cv("mr", e), in1=LNT[:, e, :],
                                              op0=ALU.mult, op1=ALU.add)
            last.then_inc(xk_ready, 1)
            yield "fv"
            dve.wait_ge(fr_tanh, due(fr_tanh, it, 1))
            dve.wait_ge(fv_mm, due(fv_mm, it, 1))
            step(v.scalar_tensor_tensor(out=FR[:, :, :], in0=FR[:, :, :], scalar=1.0,
                                        in1=PB[:, 2, :].rearrange("p (b n) -> p b n", b=PAIR), op0=ALU.add, op1=ALU.mult))
            v.scalar_tensor_tensor(out=FR[:, :, :], in0=FR[:, :, :], scalar=0.5, in1=X3[:, :, :], op0=ALU.mult,
                                   op1=ALU.add).then_inc(yo_ready, 1)
            dve.wait_ge(yo_ready, due(yo_ready, it, 1))
            chain_end("dve_b")

        @block.vector
        def _(dve):
            U32 = mybir.dt.uint32
            nc.vector.memset(QS[64:P, :, :].bitcast(U32), 0).then_inc(zero_ready, 1)
            nc.vector.memset(KS[64:P, :, :].bitcast(U32), 0).then_inc(zero_ready, 1)
            dve.wait_ge(zero_ready, 2)
            nc.vector.memset(KS[ROW_MAX:P, :, :], 1.0)
            nc.vector.memset(VV[:, :, :], 1.0)
            nc.vector.memset(V2[:, :, :, :], 0.0)
            nc.vector.memset(eps[:, :], EPS)
            nc.vector.memset(WS[:, :, :, 0:1], 0.0).then_inc(zero_ready, 1)
            dve.wait_ge(zero_ready, 3)
            dve.wait_ge(wa_in, 16 * 5)
            nc.vector.tensor_scalar(bn_s[:, 2:3], cv("bn_var"), EPS, None, ALU.add).then_inc(bn_var1, 1)
            dve.wait_ge(bn_sd, 1)
            nc.vector.reciprocal(bn_s[:, 1:2], bn_s[:, 1:2]).then_inc(bn_ready, 1)
            dve.wait_ge(bn_ready, 1)
            nc.vector.tensor_tensor(bn_s[:, 0:1], cv("bn_gamma"), bn_s[:, 1:2], ALU.mult)
            nc.vector.tensor_tensor(bn_s[:, 2:3], cv("w_b"), cv("bn_mean"), ALU.subtract).then_inc(bn_ready, 1)
            dve.wait_ge(bn_ready, 2)
            nc.vector.scalar_tensor_tensor(out=bn_s[:, 2:3], in0=bn_s[:, 2:3], scalar=bn_s[:, 0:1], in1=cv("bn_beta"),
                                           op0=ALU.mult, op1=ALU.add).then_inc(bn_ready, 1)
            dve.wait_ge(bn_ready, 3)
            dve.wait_ge(const_ready, 1)
            trips(dve, dve_stage_a, dve_stage_b)

        def pe_stage_a(pe, it):
            mm, tr = nc.tensor.matmul, nc.tensor.transpose
            yield "pg"
            pe.wait_ge(pair_in, due(pair_in, it, 48))
            for b in range(PAIR):
                for j in range(2):
                    last = mm(PA[:, 0, (2 * b + j) * 128:(2 * b + j + 1) * 128], CTX[:, b, j * 128:(j + 1) * 128], WA[:, 0, :],
                              start=True, stop=True)
            last.then_inc(pg_mm, 1)
            for c in range(2):
                for b in range(PAIR):
                    last = tr(PA[:, 3, (2 * c + b) * 128:(2 * c + b + 1) * 128], CTX[:, b, c * 128:(c + 1) * 128], ident[:, :])
            last.then_inc(enc_tr, 1)
            yield "mt"
            pe.wait_ge(pg_ready, due(pg_ready, it, 1))
            for b in range(PAIR):
                for j in range(2):
                    last = mm(PA[0:CI, 1, b * CI:(b + 1) * CI], PG[:, 2 * b + j, CI:2 * CI], PG[:, 2 * b + j, 0:CI],
                              start=(j == 0), stop=(j == 1))
            last.then_inc(mt_mm, 1)
            yield "k"
            pe.wait_ge(enc_ready, due(enc_ready, it, 1))
            pe.wait_ge(mt_ready, due(mt_ready, it, 1))
            mm(PA[:, 3, :], WA[:, 2, :], CTX[:, :, :], start=True, stop=True).then_inc(k_mm, 1)
            for b in range(PAIR):
                last = mm(PA[0:CI, 2, b * 128:(b + 1) * 128], MT[:, b, :], WWT[:, :], start=True, stop=True)
            last.then_inc(at_mm, 1)
            yield "bt"
            pe.wait_ge(at_ready, due(at_ready, it, 1))
            mm(PA[:, 1, 0:N], THW[:, :], AT[:, :, :], start=True, stop=True)
            for b in range(PAIR):
                last = mm(PA[:, 1, N + b:N + b + 1], AT[:, b, :], cv("theta_b", 0, CI), start=True, stop=True)
            last.then_inc(bt_mm, 1)
            for b in range(PAIR):
                for j in range(2):
                    last = mm(PA[:, 2, (2 * b + j) * 128:(2 * b + j + 1) * 128], CTX[:, b, j * 128:(j + 1) * 128], WA[:, 3, :],
                              start=True, stop=True)
            last.then_inc(v_mm, 1)
            yield "y"
            pe.wait_ge(bt_ready, due(bt_ready, it, 1))
            for b in range(PAIR):
                last = mm(PA[:, 0, b * N:(b + 1) * N], BT[:, b, :], X0[:, b, :], start=True, stop=True)
            last.then_inc(y_mm, 1)
            yield "q"
            pe.wait_ge(sh_ready, due(sh_ready, it, 1))
            pe.wait_ge(x1_ready, due(x1_ready, it, 1))
            mm(PA[:, 1, :], WA[:, 1, :], X1[:, :, :], start=True, stop=True).then_inc(q_mm, 1)
            def scores(b):
                for h in range(H1):
                    u = b * H1 + h
                    yield ("s", b, h)
                    if u == 0:
                        pe.wait_ge(q_ready, due(q_ready, it, 1))
                        pe.wait_ge(k_ready, due(k_ready, it, 1))
                        pe.wait_ge(v_ready, due(v_ready, it, 1))
                        pe.wait_ge(stack_in, due(stack_in, it, 19 * 16))
                    if u >= 2:
                        pe.wait_ge(s_max, due(s_max, it, u - 1))
                    for q in range(2):
                        o = b * N + q * 128
                        last = mm(PA[:, u % 2, q * N:(q + 1) * N], QS[0:K_SCORES, h, o:o + 128], KS[0:K_SCORES, h, b * N:(b + 1) * N],
                                  start=True, stop=True)
                    last.then_inc(s_mm, 1)
                yield ("max", b)
                pe.wait_ge(s_max, due(s_max, it, (b + 1) * H1))
                if b:
                    pe.wait_ge(m_parts, due(m_parts, it, b))
                for q in range(2):
                    last = tr(PA[0:H1, 3, q * 128:(q + 1) * 128], MX[:, b, q, :], ident[:, :])
                last.then_inc(m_tr, 1)

            def shifted(b):
                for h in range(H1 + G):
                    u = b * H1 + h
                    yield ("t", b, h)
                    if h == 0:
                        pe.wait_ge(maxp_in[b], due(maxp_in[b], it, 16))
                        if b == 0:
                            pe.wait_ge(m_parts, due(m_parts, it, PAIR))
                            pe.wait_ge(vsq_ready, due(vsq_ready, it, 1))
                    if h < H1:
                        if u >= 2:
                            pe.wait_ge(t_exp, due(t_exp, it, u - 1))
                        for k in range(2):
                            o = b * N + k * 128
                            last = mm(PA[:, u % 2, k * N:(k + 1) * N], KS[0:K_SHIFTED, h, o:o + 128],
                                      QS[0:K_SHIFTED, h, b * N:(b + 1) * N], start=True, stop=True)
                        last.then_inc(t_mm, 1)
                    if h >= G and h % G == G - 1:
                        t = h // G - 1
                        n = b * HT + t
                        pe.wait_ge(t_exp, due(t_exp, it, b * H1 + (t + 1) * G))
                        if b and t == 0:
                            pe.wait_ge(ot_out, due(ot_out, it, 2 * b))
                        if n >= 2:
                            pe.wait_ge(pv_out, due(pv_out, it, n - 1))
                        for k in range(2):
                            for g in range(G):
                                hh = G * t + g
                                last = mm(PA[32 * g:32 * g + 32, 2 + t % 2, 0:N], VV[:, 2 * b + k, VC * hh:VC * hh + 32],
                                          PT[:, (b * H1 + hh) % (2 * G), k, :], start=(k == 0), stop=(k == 1),
                                          skip_group_check=True)
                        last.then_inc(pv_mm, 1)
                for q in range(2):
                    yield ("o", b, q)
                    pe.wait_ge(pv_out, due(pv_out, it, (b + 1) * HT))
                    if 2 * b + q:
                        pe.wait_ge(ot_out, due(ot_out, it, 2 * b + q))
                    for t in range(HT):
                        last = tr(PA[:, 2, t * 128:(t + 1) * 128], OT[:, t, q * 128:(q + 1) * 128], ident[:, :])
                    last.then_inc(ot_tr, 1)

            for b in range(PAIR):
                yield from scores(b)
            for b in range(PAIR):
                yield from shifted(b)
            yield "x2"
            pe.wait_ge(std_ready, due(std_ready, it, 1))
            for i in range(2 * PAIR):
                tr(PA[:, 2, i * 128:(i + 1) * 128], MN[:, i, :], ident[:, :])
            for i in range(2 * PAIR):
                last = tr(PA[:, 3, i * 128:(i + 1) * 128], SQ[:, i, :], ident[:, :])
            last.then_inc(ms_tr, 1)
            pe.wait_ge(x2_ready, due(x2_ready, it, 1))

        def pe_stage_b(pe, it):
            mm, tr = nc.tensor.matmul, nc.tensor.transpose

            def ln(i):
                yield ("hat", i)
                if i == 0:
                    pe.wait_ge(wb_in, 16 * 13)
                pe.wait_ge(ln_hat, due(ln_hat, it, i + 1))
                for c in range(2):
                    for b in range(PAIR):
                        last = tr(PB[:, c, b * C:(b + 1) * C], XH[:, b, c * 128:(c + 1) * 128], ident[:, :])
                last.then_inc(ln_tr, 1)

            def project(bank, w, src):
                for e in range(2):
                    for c in range(2):
                        last = mm(PB[:, bank, e * T:(e + 1) * T], w(c, e), src(c), start=(c == 0), stop=(c == 1))
                return last

            def project_rows(bank, w, src, n=2):
                for b in range(PAIR):
                    for c in range(n):
                        last = mm(PB[:, bank, b * N:(b + 1) * N], src(c, b), w(c), start=(c == 0), stop=(c == n - 1))
                return last

            def tail(u):
                yield ("tail", u)
                pe.wait_ge(ct_ready, due(ct_ready, it, u + 1))
                for c in range(2):
                    last = mm(PB[:, half_at(u, 0) + 1, 0:N], CT2[:, c, :], WO[:, u // 2, c, :], start=(c == 0), stop=(c == 1))
                last.then_inc(ao_mm, 1)
                if u % 2 == 0:
                    pe.wait_ge(res_ready, due(res_ready, it, u + 1))

            for a in range(2):
                yield from ln(a)
                yield ("qk", a)
                pe.wait_ge(ln_ready_act, due(ln_ready_act, it, a + 1))
                pe.wait_ge(ln_ready_dve, due(ln_ready_dve, it, a + 1))
                kv = LNT if a == 0 else ENC
                weight = lambda part: lambda c, e: WH[:, c, (3 * a + part) * N + e * P:(3 * a + part) * N + (e + 1) * P]
                project(0, weight(0), lambda c: LNT[:, c, :]).then_inc(qp_mm, 1)
                project(1, weight(1), lambda c: kv[:, c, :]).then_inc(kp_mm, 1)
                yield ("v", a)
                project_rows(2, lambda c: WH[:, c, (3 * a + 2) * N:(3 * a + 3) * N], lambda c, b: kv[:, c, b * C:(b + 1) * C]).then_inc(vp_mm, 1)
                pe.wait_ge(qt_ready, due(qt_ready, it, a + 1))
                pe.wait_ge(kt_ready, due(kt_ready, it, a + 1))
                for b in range(PAIR):
                    u = 2 * a + b
                    for i in range(2):
                        yield ("score", u, i)
                        if b == 0 and i == 1:
                            pe.wait_ge(v2_ready, due(v2_ready, it, a + 1))
                        for t in range(HT):
                            for g in (half_at(u, i), half_at(u, i) + 1):
                                last = mm(PB[:, g, t * C:(t + 1) * C], QT[32 * g:32 * g + 32, t, b * C:(b + 1) * C],
                                          KT[32 * g:32 * g + 32, t // 2, b * C:(b + 1) * C], start=True, stop=True)
                        last.then_inc(sc_mm, 1)
                        if b and i == 0:
                            yield from tail(u - 1)
                    for i in range(2):
                        yield ("turn", u, i)
                        if i == 0:
                            pe.wait_ge(p_norm_pool, due(p_norm_pool, it, u + 1))
                        else:
                            pe.wait_ge(p_norm_dve, due(p_norm_dve, it, u + 1))
                        for h in range(4 * half_at(u, i), 4 * half_at(u, i) + 8):
                            last = tr(PB[:, h // 4, (h % 4) * C:(h % 4 + 1) * C], SM[:, h, :], ident[:, :])
                        last.then_inc(p_tr, 1)
                    for i in range(2):
                        yield ("ctx", u, i)
                        pe.wait_ge(p_out_dve, due(p_out_dve, it, 2 * u + i + 1))
                        if i:
                            pe.wait_ge(p_out_act, due(p_out_act, it, u + 1))
                        for t in range(HT):
                            for g in (half_at(u, i), half_at(u, i) + 1):
                                last = mm(PB[32 * g:32 * g + 32, half_at(u, 0), (t // 2) * C:(t // 2 + 1) * C],
                                          V2[:, b, 8 * (t // 2) + 2 * g + t % 2, :], PT2[:, 4 * g + t, :],
                                          start=(t % 2 == 0), stop=(t % 2 == 1), skip_group_check=True)
                    last.then_inc(ctx_mm, 1)
                yield from tail(2 * a + 1)
            yield from ln(2)
            for o in range(FF // P):
                if o % 2 == 0:
                    yield ("ff", o // 2)
                if o == 0:
                    pe.wait_ge(ln_ready_act, due(ln_ready_act, it, 3))
                    pe.wait_ge(ln_ready_dve, due(ln_ready_dve, it, 3))
                for c in range(2):
                    last = mm(PB[:, o // 2, (o % 2) * T:(o % 2 + 1) * T], W1[:, c, o * P:(o + 1) * P], LNT[:, c, :],
                              start=(c == 0), stop=(c == 1))
                last.then_inc(ff_mm, 1)
            yield "ff2"
            pe.wait_ge(ff_act, due(ff_act, it, 8))
            project_rows(0, lambda c: W2[:, c, :], lambda c, b: HF[:, c, b * C:(b + 1) * C], FF // P).then_inc(ff2_mm, 1)
            yield from ln(3)
            yield "tx"
            pe.wait_ge(xi_ready, due(xi_ready, it, 1))
            for c in range(2):
                mm(PB[:, 0, 0:T], MW1[:, c, 0:128], XI[:, c, :], start=(c == 0), stop=(c == 1))
            for c in range(2):
                last = mm(PB[0:DM, 0, T:2 * T], MW1[:, c, 128:160], XI[:, c, :], start=(c == 0), stop=(c == 1))
            last.then_inc(tx_mm, 1)
            for f in range(4):
                yield ("mix", f)
                if f == 0:
                    pe.wait_ge(tx_ready, due(tx_ready, it, 1))
                for e in range(2):
                    last = mm(PB[:, f, e * T:(e + 1) * T], MW2[DM * f:DM * f + DM, e * P:(e + 1) * P], TX[DM * f:DM * f + DM, :],
                              start=True, stop=True)
                last.then_inc(mix_mm, 1)
            yield ("mix", 4)
            pe.wait_ge(mix_used, due(mix_used, it, 1))
            for e in range(2):
                last = mm(PB[:, 0, e * T:(e + 1) * T], MW2B[:, e * P:(e + 1) * P], TXB[:, :], start=True, stop=True)
            last.then_inc(mix_mm, 1)
            yield "td1"
            pe.wait_ge(mix_ready, due(mix_ready, it, 2))
            for c in range(2):
                last = mm(PB[0:DD, 1, 0:T], TW1[:, c, :], XMX[:, 1, c, :], start=(c == 0), stop=(c == 1))
            last.then_inc(td1_mm, 1)
            yield "v3"
            pe.wait_ge(mix_ready, due(mix_ready, it, 3))
            project(2, lambda c, e: W3[:, c, 2, e * P:(e + 1) * P], lambda c: XMX[:, 2, c, :]).then_inc(v3_mm, 1)
            yield "td2"
            pe.wait_ge(td1_ready, due(td1_ready, it, 1))
            for e in range(2):
                last = mm(PB[:, 1, e * T:(e + 1) * T], TW2[:, e * P:(e + 1) * P], TD[:, :], start=True, stop=True)
            last.then_inc(td2_mm, 1)
            yield "k3"
            pe.wait_ge(mix_ready, due(mix_ready, it, 4))
            project(3, lambda c, e: W3[:, c, 1, e * P:(e + 1) * P], lambda c: XMX[:, 0, c, :]).then_inc(k3_mm, 1)
            yield "r3"
            pe.wait_ge(mix_ready, due(mix_ready, it, 5))
            project(0, lambda c, e: W3[:, c, 0, e * P:(e + 1) * P], lambda c: XMX[:, 3, c, :]).then_inc(r3_mm, 1)
            yield "g3"
            pe.wait_ge(w_ready, due(w_ready, it, 1))
            project(1, lambda c, e: W3[:, c, 3, e * P:(e + 1) * P], lambda c: XMX[:, 4, c, :]).then_inc(g3_mm, 1)
            for e in range(2):
                for half in range(2):
                    yield ("spread", e, half)
                    if e == 0 and half == 0:
                        pe.wait_ge(v3_ready, due(v3_ready, it, 1))
                        pe.wait_ge(k3_ready, due(k3_ready, it, 1))
                        pe.wait_ge(r3_ready, due(r3_ready, it, 1))
                        pe.wait_ge(g3_ready, due(g3_ready, it, 1))
                    if e:
                        pe.wait_ge(kv_ready, due(kv_ready, it, half + 1))
                    for j in range(4 * half, 4 * half + 4):
                        last = mm(PB[:, j // 2, (j % 2) * T:(j % 2 + 1) * T], SEL[:, 3 + j, :], V3[:, e, :], start=True, stop=True)
                    last.then_inc(sp_mm, 1)
            yield "sum"
            pe.wait_ge(ruk_ready, due(ruk_ready, it, 1))
            pe.wait_ge(kv_ready, due(kv_ready, it, 4))
            for e in range(2):
                pe.wait_ge(y3_ready, due(y3_ready, it, e + 1))
                for j in range(D3):
                    last = mm(PB[:, 0, e * T:(e + 1) * T], GATHER[:, D3 - 1 - j:D3 - 1 - j + P], ST3[:, e, j, :], start=(j == 0), stop=(j == D3 - 1))
            for e in range(2):
                last = mm(PB[:, 1, e * T:(e + 1) * T], SEL[:, 0, :], RUK[:, e, :], start=True, stop=True)
            last.then_inc(bonus_mm, 1)
            yield "centre"
            pe.wait_ge(o3_ready, due(o3_ready, it, 1))
            mm(PB[:, 2, :], SEL[:, 1, :], O3[:, :, :], start=True, stop=True).then_inc(cen_mm, 1)
            yield "gvar"
            pe.wait_ge(cen_sq, due(cen_sq, it, 1))
            mm(PB[:, 3, :], SEL[:, 2, :], Q3[:, :, :], start=True, stop=True).then_inc(gvar_mm, 1)
            yield "wo"
            pe.wait_ge(og_ready, due(og_ready, it, 1))
            project_rows(0, lambda c: W3[:, c, 4, :], lambda c, b: XI[:, c, b * C:(b + 1) * C]).then_inc(wo_mm, 1)
            yield from ln(4)
            yield "xk"
            pe.wait_ge(xk_ready, due(xk_ready, it, 1))
            project(0, lambda c, e: W3[:, c, 5, e * P:(e + 1) * P], lambda c: XI[:, c, :]).then_inc(fk_mm, 1)
            yield "fr"
            project_rows(1, lambda c: W3[:, c, 6, :], lambda c, b: XR[:, c, b * C:(b + 1) * C]).then_inc(fr_mm, 1)
            yield "fv"
            pe.wait_ge(fk_ready, due(fk_ready, it, 1))
            project_rows(2, lambda c: W3[:, c, 7, :], lambda c, b: Q3[:, c, b * C:(b + 1) * C]).then_inc(fv_mm, 1)
            pe.wait_ge(yo_ready, due(yo_ready, it, 1))

        @block.tensor
        def _(pe):
            pe.wait_ge(wa_in, 16 * 5)
            pe.wait_ge(const_ready, 1)
            pe.wait_ge(zero_ready, 3)
            trips(pe, pe_stage_a, pe_stage_b)


def kernel(**inputs):
    import concourse.bacc as _bacc
    from concourse.bass_utils import run_bass_kernel_spmd as _run

    a = {k: np.ascontiguousarray(v) for k, v in inputs.items()}
    l0, l1, l2, l3 = ({k[9:]: v for k, v in a.items() if k.startswith(f"L{i}_")} for i in range(4))
    halves = lambda w: w.reshape(-1, P, w.shape[-1]).transpose(1, 0, 2)

    def column(v):
        v = v.reshape(-1)
        if v.size < P:
            v = np.concatenate([v, np.zeros(P - v.size, v.dtype)])
        return v.reshape(-1, P).T


    def by_parity(v):
        o = np.zeros((2, 2, HC // 4, 2, D2), v.dtype)
        for par in range(2):
            o[:, par, :, par] = v.reshape(2, HC // 4, 2, D2)[:, :, par]
        return o.reshape(-1)

    vectors = dict(
        bn_gamma=l0["bn_gamma"], bn_beta=l0["bn_beta"], bn_mean=l0["bn_mean"], bn_var=l0["bn_var"], w_b=l0["w_b"],
        bq1=l1["bq"], bk1=l1["bk"], theta_b=l0["theta_b"], ln1_s=l2["ln1_s"], ln1_b=l2["ln1_b"], ln2_s=l2["ln2_s"],
        ln2_b=l2["ln2_b"], ln3_s=l2["ln3_s"], ln3_b=l2["ln3_b"], bq_self=by_parity(l2["b_qkv"][0:N]),
        bk_self=l2["b_qkv"][N:2 * N], bq_cross=by_parity(l2["b_q"]), bk_cross=l2["b_kv"][0:N], b1=l2["b1"],
        l3ln1_s=l3["ln1_w"], l3ln1_b=l3["ln1_b"], l3ln2_s=l3["ln2_w"], l3ln2_b=l3["ln2_b"], maa_x=l3["maa_x"],
        stack=l3["maa_stack"], decay=l3["time_decay"], u=l3["u"], gn_w=l3["gn_w"], gn_b=l3["gn_b"],
        parity=np.stack([np.arange(P) // D2 % 2 == par for par in range(2)]).astype(np.float32),
        mk=l3["ffn_maa_k"], mr=l3["ffn_maa_r"])
    rows = np.concatenate([l0["phi_b"], l0["g_b"], l1["bv"], l2["b_qkv"][2 * N:], l2["b_kv"][N:], l2["b_ao"], l2["b_co"], l2["b2"]])
    channel = np.arange(P)
    same_head = (channel[:, None] // D3 == channel[None, :] // D3).astype(np.float32)
    eye = np.eye(P, dtype=np.float32)
    spread = [same_head * (channel[:, None] % D3 == j) for j in range(D3)]
    sel = np.stack([same_head, eye - same_head / D3, same_head / D3] + spread, 1).astype(np.float32)
    gather = (np.arange(P + D3 - 1)[None, :] == D3 * (channel[:, None] // D3) + D3 - 1).astype(np.float32)
    laid = dict(
        x=a["x"], ctxt=a["ctx_2048"], kv_mask=a["mask_Bx1x2048_bf1"].reshape(NB, N).view(np.uint8),
        self_mask=a["mask_1x1xSxS2_fc1"].reshape(C, C), cross_mask=a["mask_Bx1xSxS2_ff1"].reshape(NB, C, C),
        cols=np.concatenate([column(vectors[k]) for k in COLS], 1), rows=rows,
        wa=np.stack([np.concatenate([l0["phi_w"], l0["g_w"]], 0).T, l1["Wq"].T, l1["Wk"].T, l1["Wv"].T], 1),
        ww_t=l0["w_w"].T, theta_w=l0["theta_w"],
        wh=np.concatenate([halves(l2["w_qkv"]), halves(l2["w_q"]), halves(l2["w_kv"])], 2),
        wo=np.stack([halves(l2["w_ao"]), halves(l2["w_co"])], 1),
        w_ff1=halves(l2["w1"]), w_ff2=halves(l2["w2"]),
        w3=np.stack([halves(l3[k].T) for k in ("Wr", "Wk", "Wv", "Wg", "Wo", "Wfk", "Wfr", "Wfv")], 2),
        maa_w1=l3["maa_w1"], maa_w2=l3["maa_w2"].reshape(NF * DM, N), td_w1=l3["td_w1"], td_w2=l3["td_w2"], sel=sel, gather=gather)
    nc = _bacc.Bacc("TRN2", target_bir_lowering=False, num_devices=1)
    arrays, ap = {}, {}
    for name, v in laid.items():
        v = np.ascontiguousarray(v)
        arrays[f"in_{name}_dram"] = v
        ap[name] = nc.dram_tensor(f"in_{name}_dram", v.shape, mybir.dt.from_np(v.dtype), kind="ExternalInput").ap()
    ap["out"] = nc.dram_tensor("out_0_dram", (NB, C, N), F32, kind="ExternalOutput").ap()
    four_layers(nc, **ap)
    return _run(nc, [arrays], core_ids=[0]).results[0]["out_0_dram"]
```

```python
from contextlib import ExitStack

import concourse.bass as bass
from concourse import mybir
import numpy as np

F32 = mybir.dt.float32
BF16 = mybir.dt.bfloat16
U8 = mybir.dt.uint8
ALU = mybir.AluOpType
ACT = mybir.ActivationFunctionType
AX = mybir.AxisListType

P = 128
NB = 8
PAIR = 2
TRIPS = NB // PAIR
C = 128
N = 256
T = PAIR * C
CI = 64
H1, D1 = 16, 8
H2, D2 = 16, 16
G = 4
HT = H2 // G
FF = 4 * N
H3, D3 = 32, 8
NF, DM, DD = 5, 32, 64
EPS = 1e-5
VC = 2 * D1 + 1
NSPLIT = 3
KSTACK = NSPLIT * NSPLIT * D1
ROW_MASK = KSTACK
ROW_MAX = 96
K_SCORES = ROW_MAX
K_SHIFTED = ROW_MAX + NSPLIT

COLS = {}
for _name, _n in (("bn_gamma", 1), ("bn_beta", 1), ("bn_mean", 1), ("bn_var", 1), ("w_b", 1), ("bq1", 1), ("bk1", 1),
                  ("theta_b", 1), ("ln1_s", 2), ("ln1_b", 2), ("ln2_s", 2), ("ln2_b", 2), ("ln3_s", 2), ("ln3_b", 2),
                  ("bq_self", 4), ("bk_self", 2), ("bq_cross", 4), ("bk_cross", 2), ("b1", 8), ("parity", 2),
                  ("l3ln1_s", 2), ("l3ln1_b", 2), ("l3ln2_s", 2), ("l3ln2_b", 2), ("maa_x", 2), ("stack", 10),
                  ("decay", 2), ("u", 2), ("gn_w", 2), ("gn_b", 2), ("mk", 2), ("mr", 2)):
    COLS[_name] = (sum(n for _, n in COLS.values()), _n)
NCOL = sum(n for _, n in COLS.values())
ROWS = {}
for _name, _n in (("phi_g_b", 128), ("bv1", 128), ("bv_self", 256), ("bv_cross", 256), ("b_ao", 256), ("b_co", 256),
                  ("b2", 256)):
    ROWS[_name] = (sum(n for _, n in ROWS.values()), _n)
NROW = sum(n for _, n in ROWS.values())

CHAIN = {"dve_a": 32, "dve_b": 69, "act_b": 2}


def four_layers(nc, x, ctxt, kv_mask, self_mask, cross_mask, cols, rows, wa, ww_t, theta_w, wh, wo, w_ff1, w_ff2,
                w3, maa_w1, maa_w2, td_w1, td_w2, sel, gather, out):
    with ExitStack() as stack:
        def sb(name, shape, dt=F32):
            return stack.enter_context(nc.sbuf_tensor(name, shape, dt))

        per_trip = {}

        def sem(name, n=1):
            s = stack.enter_context(nc.semaphore(name))
            per_trip[name] = n
            names[id(s)] = name
            keep.append(s)
            return s

        names, keep = {}, []

        def due(s, it, k):
            return it * per_trip[names[id(s)]] + k

        q_dram = nc.dram_tensor("q_parts", (NSPLIT, C, PAIR * N), BF16, kind="Internal").ap()
        k_dram = nc.dram_tensor("k_parts", (NSPLIT, C, PAIR * N), BF16, kind="Internal").ap()
        max_dram = nc.dram_tensor("max_parts", (PAIR, H1, NSPLIT, N), BF16, kind="Internal").ap()
        mask_dram = nc.dram_tensor("mask_rows", (H1, PAIR * N), BF16, kind="Internal").ap()

        col = sb("col", [P, NCOL])
        row = sb("row", [P, NROW])
        WA = sb("WA", [P, 5, 128])
        WWT = sb("WWT", [CI, 128])
        THW = sb("THW", [CI, 128])
        WH = sb("WH", [P, 2, 6 * N])
        WO = sb("WO", [P, 2, 2, N])
        W1 = sb("W1", [P, 2, FF])
        W2 = sb("W2", [P, FF // P, N])
        W3 = sb("W3", [P, 2, 8, N])
        MW1 = sb("MW1", [P, 2, NF * DM])
        MW2 = sb("MW2", [P, N])
        MW2B = sb("MW2B", [DM, N])
        TW1 = sb("TW1", [P, 2, DD])
        TW2 = sb("TW2", [DD, N])
        SEL = sb("SEL", [P, 3 + D3, 128])
        GATHER = sb("GATHER", [P, P + D3 - 1])
        ident = sb("ident", [P, P])
        bn_s = sb("bn_s", [P, 3])
        bq1s = sb("bq1s", [P, 1])

        eps = sb("eps", [P, 1])

        def cv(name, i=0, parts=P):
            o = COLS[name][0] + i
            return col[0:parts, o:o + 1]

        def rv(name):
            o, n = ROWS[name]
            return row[:, o:o + n]

        X0 = sb("X0", [P, PAIR, N])
        CTX = sb("CTX", [P, PAIR, N])
        MASK8 = sb("MASK8", [P, PAIR, N], U8)
        MF = sb("MF", [P, PAIR, N])
        MBIAS = sb("MBIAS", [P, PAIR * N], BF16)
        MT = sb("MT", [CI, PAIR, CI])
        AT = sb("AT", [CI, PAIR, 128])
        BT = sb("BT", [P, PAIR, 128])
        SH = sb("SH", [P, PAIR])
        X1 = sb("X1", [P, PAIR, N])
        QS = sb("QS", [P, H1, PAIR * N], BF16)
        KS = sb("KS", [P, H1, PAIR * N], BF16)
        VV = sb("VV", [P, PAIR * 2, H1 * VC + 32 - VC])
        VH = VV[:, :, 0:H1 * VC].rearrange("p a (h c) -> p a h c", c=VC)
        MX = sb("MX", [P, PAIR, 2, H1])
        NMP = sb("NMP", [H1, NSPLIT, N], BF16)
        AREA_A = sb("AREA_A", [P, 2 * G * 2 * N])
        PT = AREA_A[:, :].rearrange("p (s k n) -> p s k n", s=2 * G, k=2)
        QK = AREA_A[:, 0:1024].rearrange("p (i n) -> p i n", i=2)
        RES = AREA_A[:, 1024:2048].rearrange("p (i n) -> p i n", i=2)
        QKP = AREA_A[:, 2048:3584].bitcast(BF16).rearrange("p (i s n) -> p i s n", i=2, s=NSPLIT)
        PG = AREA_A[:, 3584:4096].rearrange("p (a n) -> p a n", n=128)
        OT = sb("OT", [P, HT, N])
        NM = OT[0:H1, 0:2, :]
        SQ = OT[:, 0:2, :].rearrange("p a (b n) -> p (a b) n", n=128)
        RSUM = sb("RSUM", [P, H1])
        MN = sb("MN", [P, PAIR * 2, 128])
        EX = CTX[:, :, :].rearrange("p b (q c) -> p (b q) c", q=2)
        IST = sb("IST", [P, 8, PAIR])
        XN = X0
        ENC = sb("ENC", [P, 2, T])
        X2 = sb("X2", [P, PAIR, N])
        ENC_A, ENC = ENC, sb("ENC_B", [P, 2, T])

        AREA_B = sb("AREA_B", [P, 6144])
        QT = AREA_B[:, 0:1024].rearrange("p (t n) -> p t n", t=HT)
        KT = AREA_B[:, 1024:1536].rearrange("p (c n) -> p c n", c=2)
        SM = AREA_B[:, 2048:4096].rearrange("p (h k) -> p h k", h=H2)
        PT2 = SM
        HF = AREA_B[:, 2048:4096].rearrange("p (o n) -> p o n", n=T)
        CT2 = AREA_B[:, 4096:4352].rearrange("p (c n) -> p c n", c=2)
        XM4 = AREA_B[:, 0:2048].rearrange("p (f e n) -> p f e n", f=NF - 1, e=2)
        KV3 = AREA_B[:, 0:2048].rearrange("p (j b n) -> p j b n", j=D3, b=PAIR)
        ST3 = AREA_B[:, 2048:6144].rearrange("p (e j n) -> p e j n", e=2, j=D3)
        SMASK = sb("SMASK", [P, C])
        SFILL = sb("SFILL", [P, C])
        CMASK = sb("CMASK", [P, PAIR, C])
        CFILL = sb("CFILL", [P, PAIR, C])
        X3 = sb("X3", [P, PAIR, N])
        BST = sb("BST", [P, PAIR, 6])
        BMV = sb("BMV", [P, PAIR, 2])
        cell = sb("cell", [P, 1])
        SDV = sb("SDV", [P, PAIR])
        RSD = sb("RSD", [P, PAIR])
        LNT = sb("LNT", [P, 2, T])
        V2 = sb("V2", [P, PAIR, H2, 2 * D2])
        RS2 = sb("RS2", [P, H2])
        RR2 = sb("RR2", [P, H2])
        MX2 = sb("MX2", [P, H2])
        NMX2 = sb("NMX2", [P, H2])
        SX = sb("SX", [P, 2, T])
        XH = SX
        XI = sb("XI", [P, 2, T])
        XMX = [XM4[:, f] for f in range(NF - 1)] + [XI]
        TX = sb("TX", [P, T])
        TD = TX[0:DD, :]
        TXB = sb("TXB", [DM, T])
        WS = sb("WS", [P, 2, PAIR, C])
        R3 = sb("R3", [P, 2, T])
        K3 = sb("K3", [P, 2, T])
        V3 = sb("V3", [P, 2, T])
        G3 = sb("G3", [P, 2, T])
        S0 = sb("S0", [P, 2, PAIR, D3])
        RUK = sb("RUK", [P, 2, T])
        EX3 = RUK
        O3 = sb("O3", [P, 2, T])
        XR = O3
        Q3 = sb("Q3", [P, 2, T])
        FR = R3

        PA = stack.enter_context(nc.psum_tensor("PA", [P, 4, 512], F32))
        PB = stack.enter_context(nc.psum_tensor("PB", [P, 4, 512], F32))

        wa_in, wb_in = sem("wa_in"), sem("wb_in")
        const_step, const_ready, bn_ready = sem("const_step"), sem("const_ready"), sem("bn_ready")
        zero_ready = sem("zero_ready")
        bn_sd, bn_var1 = sem("bn_sd"), sem("bn_var1")
        pair_in, out_stored = sem("pair_in", 3 * 16), sem("out_stored", 16)
        cross_in = sem("cross_in", 16)
        state_in = sem("state_in", PAIR * 2 * 16)
        parts_out, mask_out = sem("parts_out", 2 * 16), sem("mask_out", 16)
        stack_in = sem("stack_in", 19 * 16)
        maxp_out, maxp_in = sem("maxp_out", PAIR * 16), [sem(f"maxp_in{b}", 16) for b in range(PAIR)]
        enc_tr, enc_ready = sem("enc_tr"), sem("enc_ready")
        pg_mm, pg_ready = sem("pg_mm"), sem("pg_ready")
        mt_mm, mt_ready = sem("mt_mm"), sem("mt_ready")
        at_mm, at_ready = sem("at_mm"), sem("at_ready")
        bt_mm, bt_ready, sh_ready = sem("bt_mm"), sem("bt_ready"), sem("sh_ready")
        y_mm, y_added, x1_ready = sem("y_mm"), sem("y_added"), sem("x1_ready")
        k_mm, q_mm, v_mm = sem("k_mm"), sem("q_mm"), sem("v_mm")
        k_ready, q_ready, v_ready = sem("k_ready"), sem("q_ready"), sem("v_ready")
        kp_ready, qp_ready, mbias_ready = sem("kp_ready"), sem("qp_ready"), sem("mbias_ready")
        vsq_ready = sem("vsq_ready")
        s_mm, s_max = sem("s_mm", PAIR * H1), sem("s_max", PAIR * H1)
        m_tr, m_parts = sem("m_tr", PAIR), sem("m_parts", PAIR)
        t_mm, t_exp = sem("t_mm", PAIR * H1), sem("t_exp", PAIR * H1)
        pv_mm, pv_out = sem("pv_mm", PAIR * HT), sem("pv_out", PAIR * HT)
        ot_tr, ot_out = sem("ot_tr", PAIR * 2), sem("ot_out", PAIR * 2)
        var_ready, std_ready = sem("var_ready"), sem("std_ready")
        ivar_ready, istd_ready = sem("ivar_ready"), sem("istd_ready")
        ms_tr, x2_ready = sem("ms_tr"), sem("x2_ready")
        ln_var, ln_sd, ln_hat = sem("ln_var", 5), sem("ln_sd", 5), sem("ln_hat", 5)
        enc_moved = sem("enc_moved")
        ln_tr, ln_ready_act, ln_ready_dve = sem("ln_tr", 5), sem("ln_ready_act", 5), sem("ln_ready_dve", 5)
        qp_mm, kp_mm, vp_mm = sem("qp_mm", 4), sem("kp_mm", 2), sem("vp_mm", 2)
        qt_ready_dve, qt_ready_act = sem("qt_ready_dve", 2), sem("qt_ready_act", 2)
        kt_ready, v2_ready = sem("kt_ready", 2), sem("v2_ready", 2)
        sc_mm, sc_masked, sc_filled = sem("sc_mm", 8), sem("sc_masked", 8), sem("sc_filled", 8)
        sc_nmax, sc_exp = sem("sc_nmax", 16), sem("sc_exp", 16)
        p_norm, p_tr, p_out_dve, p_out_act = sem("p_norm", 12), sem("p_tr", 12), sem("p_out_dve", 8), sem("p_out_act", 4)
        ctx_mm, ct_ready = sem("ctx_mm", 4), sem("ct_ready", 4)
        ao_mm, res_ready = sem("ao_mm", 4), sem("res_ready", 4)
        ff_mm, ff_act, ff2_mm, x4_ready = sem("ff_mm", 8), sem("ff_act", 8), sem("ff2_mm"), sem("x4_ready")
        xi_ready = sem("xi_ready")
        tx_mm, tx_ready = sem("tx_mm"), sem("tx_ready")
        mix_mm, mix_used, mix_ready = sem("mix_mm", NF), sem("mix_used", NF), sem("mix_ready", NF)
        td1_mm, td1_ready, td2_mm, w_ready = sem("td1_mm"), sem("td1_ready"), sem("td2_mm"), sem("w_ready")
        v3_mm, k3_mm, r3_mm, g3_mm = sem("v3_mm"), sem("k3_mm"), sem("r3_mm"), sem("g3_mm")
        v3_ready, k3_ready, r3_ready = sem("v3_ready"), sem("k3_ready"), sem("r3_ready")
        g3_tanh, g3_ready = sem("g3_tanh"), sem("g3_ready")
        sp_mm, kv_ready = sem("sp_mm", 4), sem("kv_ready", 4)
        y3_ready, ruk_ready = sem("y3_ready", 4), sem("ruk_ready")
        bonus_mm, o3_ready = sem("bonus_mm"), sem("o3_ready")
        cen_mm, cen_sq, gvar_mm, gsd_ready, og_ready = (
            sem("cen_mm"), sem("cen_sq"), sem("gvar_mm"), sem("gsd_ready"), sem("og_ready"))
        wo_mm = sem("wo_mm")
        xk_ready, fk_mm, fr_mm = sem("xk_ready"), sem("fk_mm"), sem("fr_mm")
        fk_ready, fr_tanh, fv_mm, yo_ready = sem("fk_ready"), sem("fr_tanh"), sem("fv_mm"), sem("yo_ready")
        chain_sem = {k: sem(k, n) for k, n in CHAIN.items()}
        chain_at = {}

        def link(eng, name, it, ins):
            chain_at[name] = chain_at.get(name, 0) + 1
            ins.then_inc(chain_sem[name], 1)
            eng.wait_ge(chain_sem[name], it * CHAIN[name] + chain_at[name])

        def chain_end(name):
            assert chain_at.get(name, 0) == CHAIN[name], (name, chain_at.get(name, 0))
            chain_at[name] = 0

        def half_at(u, i):
            return 2 * ((u + i) % 2)

        def parts(u):
            return ((half_at(u, 0), 2), (half_at(u, 1), 1), (half_at(u, 1) + 1, 1))

        def layer_ln(i):
            return [("ln", i), ("hat", i)]

        PHASES_A = ["pg", "mt", "k", "bt", "y", "q"]
        PHASES_A += [("s", 0, h) for h in range(H1)] + [("max", 0)]
        PHASES_A += [("s", 1, h) for h in range(H1)] + [("max", 1), "norm", "unit"]
        for b in range(PAIR):
            PHASES_A += [("t", b, h) for h in range(H1 + G)] + [("o", b, 0), ("o", b, 1)]
        PHASES_A += ["var", "x2"]
        PHASES_B = []
        for a in range(2):
            PHASES_B += layer_ln(a) + [("q", a), ("kv", a)] if a == 0 else [("ln", 1), ("kv", 1), ("hat", 1), ("q", 1)]
            for u in (2 * a, 2 * a + 1):
                PHASES_B += [("score", u, 0)] + ([("tail", u - 1)] if u % 2 else []) + [("score", u, 1), ("exp", u, 0), ("exp", u, 1)]
                PHASES_B += [("norm", u)] + [("turn", u, n) for n in range(3)] + [("ctx", u, 0), ("ctx", u, 1)]
            PHASES_B += [("tail", 2 * a + 1)]
        PHASES_B += layer_ln(2) + [("ff", k) for k in range(4)] + ["ff2"]
        PHASES_B += layer_ln(3) + ["xi", "tx"] + [("mix", f) for f in range(NF)]
        PHASES_B += ["td1", "v3", "td2", "k3", "r3", "ruk"]
        PHASES_B += [("spread", e, half) for e in range(2) for half in range(2)]
        PHASES_B += ["g3", "sum", "bonus", "centre", "gvar", "og", "wo"] + layer_ln(4) + ["xk", "fr", "fv"]
        assert len(set(PHASES_A)) == len(PHASES_A) and len(set(PHASES_B)) == len(PHASES_B)

        AMONG = (("pg", "q", ("ln", 0), ("kv", 0)),
                 ("q", ("s", 0, 0), ("ctx", 0, 0), ("ctx", 0, 1)),
                 (("s", 0, 0), "norm", ("turn", 1, 0), ("ff", 3)),
                 ("norm", ("t", 0, 0), ("ff", 3), "ff2"),
                 (("t", 0, 0), None, "ff2", "fv"))

        def order():
            after = {}
            for a0, a1, b0, b1 in AMONG:
                group = PHASES_A[PHASES_A.index(a0):PHASES_A.index(a1) if a1 else None]
                first, last = PHASES_B.index(b0), PHASES_B.index(b1)
                for i, phase in enumerate(group):
                    after.setdefault(first + i * (last - first) // len(group), []).append(phase)
            return [x for i, phase in enumerate(PHASES_B) for x in [("B", phase)] + [("A", p) for p in after.get(i, [])]]

        def walk(**stages):
            now = {k: next(g, None) for k, g in stages.items()}
            for k, phase in order():
                if k in stages and now[k] == phase:
                    now[k] = next(stages[k], None)
            assert all(v is None for v in now.values()), now

        def trips(eng, stage_a, stage_b):
            walk(A=stage_a(eng, 0))
            with eng.Fori(1, TRIPS) as it:
                walk(A=stage_a(eng, it), B=stage_b(eng, it - 1))
            walk(B=stage_b(eng, TRIPS - 1))

        block = stack.enter_context(nc.Block())

        def sp_stage_a(sp, it):
            at = it * PAIR if isinstance(it, int) else sp.snap(it * PAIR)
            yield "pg"
            if not isinstance(it, int):
                sp.wait_ge(x2_ready, due(x2_ready, it, 0))
            sp.dma_start(CTX[:, :, :], ctxt[bass.ds(at, PAIR)].rearrange("b c n -> c b n")).then_inc(pair_in, 16)
            sp.dma_start(X0[:, :, :], x[bass.ds(at, PAIR)].rearrange("b c n -> c b n")).then_inc(pair_in, 16)
            sp.dma_start(MASK8[:, :, :], kv_mask[bass.ds(at, PAIR)].partition_broadcast(P)).then_inc(pair_in, 16)
            yield "k"
            sp.wait_ge(mbias_ready, due(mbias_ready, it, 1))
            sp.dma_start(mask_dram, MBIAS[0:H1, :]).then_inc(mask_out, 16)
            sp.wait_ge(kp_ready, due(kp_ready, it, 1))
            sp.dma_start(k_dram.rearrange("s c n -> c s n"), QKP[:, 1, :, :]).then_inc(parts_out, 16)
            sp.wait_ge(mask_out, due(mask_out, it, 16))
            if isinstance(it, int):
                sp.wait_ge(const_ready, 1)
                sp.wait_ge(zero_ready, 1)
            sp.dma_start(KS[ROW_MASK:ROW_MASK + 1, :, :], mask_dram.rearrange("(o h) n -> o h n", o=1)).then_inc(stack_in, 16)
            sp.wait_ge(parts_out, due(parts_out, it, 16))
            for i in range(NSPLIT * NSPLIT):
                sp.dma_start(KS[D1 * i:D1 * i + D1, :, :],
                             k_dram[i % NSPLIT].rearrange("(h d) n -> d h n", d=D1)).then_inc(stack_in, 16)
            yield "q"
            sp.wait_ge(qp_ready, due(qp_ready, it, 1))
            sp.dma_start(q_dram.rearrange("s c n -> c s n"), QKP[:, 0, :, :]).then_inc(parts_out, 16)
            sp.wait_ge(parts_out, due(parts_out, it, 32))
            for i in range(NSPLIT * NSPLIT):
                sp.dma_start(QS[D1 * i:D1 * i + D1, :, :],
                             q_dram[i // NSPLIT].rearrange("(h d) n -> d h n", d=D1)).then_inc(stack_in, 16)
            for b in range(PAIR):
                yield ("max", b)
                sp.wait_ge(m_parts, due(m_parts, it, b + 1))
                sp.dma_start(max_dram[b], NMP[:, :, :]).then_inc(maxp_out, 16)
                sp.wait_ge(maxp_out, due(maxp_out, it, 16 * (b + 1)))
                sp.dma_start(QS[ROW_MAX:ROW_MAX + NSPLIT, :, b * N:(b + 1) * N],
                             max_dram[b].rearrange("h s n -> s h n")).then_inc(maxp_in[b], 16)

        def nothing(eng, it):
            return
            yield

        @block.sync
        def _(sp):
            sp.dma_start(col[:, :], cols).then_inc(wa_in, 16)
            sp.dma_start(WA[:, 0:4, :], wa).then_inc(wa_in, 16)
            sp.dma_start(WWT[:, :], ww_t).then_inc(wa_in, 16)
            sp.dma_start(THW[:, :], theta_w).then_inc(wa_in, 16)
            trips(sp, sp_stage_a, nothing)
            sp.wait_ge(out_stored, 16 * (TRIPS + 1))

        def load_stage_b(eng, at):
            eng.dma_start(CMASK[:, :, :], cross_mask[bass.ds(at, PAIR)].rearrange("b s t -> s b t")).then_inc(cross_in, 16)
            for b in range(PAIR):
                for e in range(2):
                    eng.dma_start(S0[:, e, b, :], ctxt[bass.ds(at + b, 1), 2:2 + D3, :].rearrange("o r n -> (o r n)")
                                  .rearrange("(e p j) -> e p j", e=2, j=D3)[e]).then_inc(state_in, 16)

        def pool_stage_a(pool, it):
            yield "bt"
            pool.wait_ge(v_ready, due(v_ready, it, 1))
            nc.gpsimd.tensor_tensor(VH[:, :, :, D1:2 * D1], VH[:, :, :, 0:D1], VH[:, :, :, 0:D1], ALU.mult).then_inc(vsq_ready, 1)

            yield "x2"
            pool.wait_ge(x2_ready, due(x2_ready, it, 1))
            pool.wait_ge(const_step, 1)

        def pool_stage_b(pool, it):
            for u in range(4):
                fill = SFILL[:, :] if u < 2 else CFILL[:, u % 2, :]
                for i in range(2):
                    yield ("score", u, i)
                    hs = slice(4 * half_at(u, i) + 4, 4 * half_at(u, i) + 8)
                    pool.wait_ge(sc_masked, due(sc_masked, it, 2 * u + i + 1))
                    nc.gpsimd.tensor_tensor(SM[:, hs, :], SM[:, hs, :], fill.unsqueeze(1).to_broadcast([P, 4, C]),
                                            ALU.add).then_inc(sc_filled, 1)
            for f in range(NF):
                yield ("mix", f)
                pool.wait_ge(mix_used, due(mix_used, it, f + 1))
                nc.gpsimd.tensor_tensor(XMX[f][:, :, :], XMX[f][:, :, :], LNT[:, :, :], ALU.add).then_inc(mix_ready, 1)
            yield "wo"
            if not isinstance(it, int):
                pool.wait_ge(y3_ready, due(y3_ready, it, 4))
                load_stage_b(pool, pool.snap((it + 1) * PAIR))
            yield "fv"
            pool.wait_ge(yo_ready, due(yo_ready, it, 1))
            pool.wait_ge(const_step, 1)

        @block.gpsimd
        def _(pool):
            pool.memset(ident[:, :], 0.0).then_inc(const_step, 1)
            pool.wait_ge(const_step, 1)
            pool.affine_select(out=ident[:, :], in_=ident[:, :], compare_op=ALU.not_equal, fill=1.0, base=0,
                               pattern=[[-1, P]], channel_multiplier=1).then_inc(const_step, 1)
            pool.wait_ge(const_step, 2)
            nc.gpsimd.memset(QS[64:P, :, :].bitcast(mybir.dt.uint32), 0).then_inc(const_step, 1)
            pool.wait_ge(const_step, 3)
            pool.affine_select(out=QS[64:ROW_MAX, :, :], in_=QS[64:ROW_MAX, :, :], compare_op=ALU.not_equal, fill=1.0,
                               base=64 - ROW_MASK, pattern=[[0, H1], [0, PAIR * N]], channel_multiplier=1).then_inc(const_ready, 1)
            load_stage_b(pool, 0)
            pool.wait_ge(const_ready, 1)
            trips(pool, pool_stage_a, pool_stage_b)

        def act_stage_a(act, it):
            yield "pg"
            if not isinstance(it, int):
                act.wait_ge(enc_moved, due(enc_moved, it, 0))
            act.wait_ge(enc_tr, due(enc_tr, it, 1))
            nc.scalar.activation(ENC_A[:, :, :], PA[:, 3, :], ACT.Copy).then_inc(enc_ready, 1)
            yield "mt"
            act.wait_ge(mt_mm, due(mt_mm, it, 1))
            nc.scalar.activation(MT[:, :, :], PA[0:CI, 1, 0:PAIR * CI], ACT.Copy, scale=1.0 / N).then_inc(mt_ready, 1)
            yield "k"
            act.wait_ge(k_mm, due(k_mm, it, 1))
            nc.scalar.activation(QK[:, 1, :], PA[:, 3, :], ACT.Identity, bias=cv("bk1")).then_inc(k_ready, 1)
            yield "bt"
            act.wait_ge(bt_mm, due(bt_mm, it, 1))
            nc.scalar.activation(BT[:, :, :], PA[:, 1, 0:N], ACT.Copy).then_inc(bt_ready, 1)
            yield "y"
            act.wait_ge(y_added, due(y_added, it, 1))
            for b in range(PAIR):
                last = nc.scalar.activation(X1[:, b, :], X1[:, b, :], ACT.Identity, bias=SH[:, b:b + 1])
            last.then_inc(x1_ready, 1)
            yield "q"
            act.wait_ge(q_mm, due(q_mm, it, 1))
            nc.scalar.activation(QK[:, 0, :], PA[:, 1, :], ACT.Identity, bias=bq1s[:, :], scale=float(D1) ** -0.5).then_inc(q_ready, 1)
            yield ("s", 0, 0)
            if isinstance(it, int):
                act.wait_ge(stack_in, 19 * 16)
                act.dma_start(WH[:, :, :], wh).then_inc(wb_in, 16)
                act.dma_start(WO[:, :, :, :], wo).then_inc(wb_in, 16)
                act.dma_start(SMASK[:, :], self_mask).then_inc(wb_in, 16)
                act.dma_start(W1[:, :, :], w_ff1).then_inc(wb_in, 16)
                act.dma_start(W2[:, :, :], w_ff2).then_inc(wb_in, 16)
                act.dma_start(W3[:, :, :, :], w3).then_inc(wb_in, 16)
                act.dma_start(MW1[:, :, :], maa_w1.rearrange("(c p) n -> p c n", p=P)).then_inc(wb_in, 16)
                act.dma_start(MW2[:, :], maa_w2[0:P]).then_inc(wb_in, 16)
                act.dma_start(MW2B[:, :], maa_w2[P:P + DM]).then_inc(wb_in, 16)
                act.dma_start(TW1[:, :, :], td_w1.rearrange("(c p) n -> p c n", p=P)).then_inc(wb_in, 16)
                act.dma_start(TW2[:, :], td_w2).then_inc(wb_in, 16)
                act.dma_start(SEL[:, :, :], sel).then_inc(wb_in, 16)
                act.dma_start(GATHER[:, :], gather).then_inc(wb_in, 16)
            yield "norm"
            act.wait_ge(ivar_ready, due(ivar_ready, it, 1))
            nc.scalar.activation(IST[:, 6, :], IST[:, 5, :], ACT.Sqrt).then_inc(istd_ready, 1)
            for u in range(PAIR * H1):
                yield ("t", u // H1, u % H1)
                act.wait_ge(t_mm, due(t_mm, it, u + 1))
                if u >= 2 * G:
                    act.wait_ge(pv_mm, due(pv_mm, it, (u - 2 * G) // G + 1))
                nc.scalar.activation(PT[:, u % (2 * G), :, :], PA[:, u % 2, :], ACT.Exp).then_inc(t_exp, 1)
            yield "var"
            act.wait_ge(var_ready, due(var_ready, it, 1))
            nc.scalar.activation(SQ[:, :, :], EX[:, :, :], ACT.Sqrt).then_inc(std_ready, 1)
            yield "x2"
            act.wait_ge(x2_ready, due(x2_ready, it, 1))

        def act_ln(act, it, i, s, b):
            yield ("ln", i)
            act.wait_ge(ln_var, due(ln_var, it, i + 1))
            nc.scalar.activation(SDV[:, :], BMV[:, :, 1], ACT.Sqrt, bias=eps[:, :]).then_inc(ln_sd, 1)
            if i == 0:
                nc.scalar.activation(ENC[:, :, :], ENC_A[:, :, :], ACT.Copy).then_inc(enc_moved, 1)
            yield ("hat", i)
            act.wait_ge(ln_tr, due(ln_tr, it, i + 1))
            nc.scalar.activation(LNT[:, 0, :], PB[:, 0, 0:T], ACT.Identity, bias=cv(b, 0), scale=cv(s, 0)).then_inc(ln_ready_act, 1)

        def act_tail(act, it, u):
            yield ("tail", u)
            act.wait_ge(ctx_mm, due(ctx_mm, it, u + 1))
            nc.scalar.activation(CT2[:, :, :], PB[:, half_at(u, 0), 0:N], ACT.Copy).then_inc(ct_ready, 1)

        def act_stage_b(act, it):
            for a in range(2):
                def keys():
                    yield ("kv", a)
                    act.wait_ge(kp_mm, due(kp_mm, it, a + 1))
                    for c in range(2):
                        last = nc.scalar.activation(KT[:, c, :], PB[:, 2, c * T:(c + 1) * T], ACT.Identity,
                                                    bias=cv(("bk_self", "bk_cross")[a], c))
                    last.then_inc(kt_ready, 1)

                ln_phases = act_ln(act, it, a, *(("ln1_s", "ln1_b"), ("ln2_s", "ln2_b"))[a])
                yield next(ln_phases)
                if a:
                    now = next(ln_phases)
                    yield from keys()
                    yield now
                yield from ln_phases
                yield ("q", a)
                act.wait_ge(qp_mm, due(qp_mm, it, 2 * a + 2))
                for par in range(2):
                    last = nc.scalar.activation(QT[:, 2 + par, :], PB[:, 1, 0:T], ACT.Identity, scale=cv("parity", par),
                                                bias=cv(("bq_self", "bq_cross")[a], 2 + par))
                last.then_inc(qt_ready_act, 1)
                if a == 0:
                    yield from keys()
                for b in range(PAIR):
                    u = 2 * a + b
                    if b:
                        yield from act_tail(act, it, u - 1)
                    for i in range(2):
                        yield ("exp", u, i)
                        for g in (half_at(u, i), half_at(u, i) + 1):
                            act.wait_ge(sc_nmax, due(sc_nmax, it, 4 * u + 2 * i + g % 2 + 1))
                            for h in range(4 * g, 4 * g + 4):
                                last = nc.scalar.activation(SM[:, h, :], SM[:, h, :], ACT.Exp, bias=NMX2[:, h:h + 1],
                                                            accum_out=RS2[:, h:h + 1])
                            last.then_inc(sc_exp, 1)
                    yield ("turn", u, 1)
                    act.wait_ge(p_tr, due(p_tr, it, 3 * u + 2))
                    k = half_at(u, 1)
                    nc.scalar.activation(PT2[:, 4 * k:4 * k + 4, :], PB[:, k, :], ACT.Copy).then_inc(p_out_act, 1)
                yield from act_tail(act, it, 2 * a + 1)
            yield from act_ln(act, it, 2, "ln3_s", "ln3_b")
            for o in range(FF // P):
                if o % 2 == 0:
                    yield ("ff", o // 2)
                act.wait_ge(ff_mm, due(ff_mm, it, o // 2 * 2 + 2))
                nc.scalar.activation(HF[:, o, :], PB[:, o // 2, (o % 2) * T:(o % 2 + 1) * T], ACT.Gelu_apprx_tanh,
                                     bias=cv("b1", o)).then_inc(ff_act, 1)
            yield from act_ln(act, it, 3, "l3ln1_s", "l3ln1_b")
            yield "tx"
            act.wait_ge(tx_mm, due(tx_mm, it, 1))
            nc.scalar.activation(TX[:, :], PB[:, 0, 0:T], ACT.Tanh)
            nc.scalar.activation(TXB[:, :], PB[0:DM, 0, T:2 * T], ACT.Tanh).then_inc(tx_ready, 1)
            yield "td1"
            act.wait_ge(td1_mm, due(td1_mm, it, 1))
            nc.scalar.activation(TD[:, :], PB[0:DD, 1, 0:T], ACT.Tanh).then_inc(td1_ready, 1)
            yield "td2"
            act.wait_ge(td2_mm, due(td2_mm, it, 1))
            for e in range(2):
                last = nc.scalar.activation(EX3[:, e, :], PB[:, 1, e * T:(e + 1) * T], ACT.Exp, bias=cv("decay", e))
            link(act, "act_b", it, last)
            nc.scalar.activation(WS[:, :, :, 1:C].rearrange("p e b t -> p (e b) t"),
                                 EX3[:, :, :].rearrange("p e (b t) -> p (e b) t", b=PAIR)[:, :, 0:C - 1], ACT.Exp,
                                 scale=-1.0).then_inc(w_ready, 1)
            yield "k3"
            act.wait_ge(k3_mm, due(k3_mm, it, 1))
            nc.scalar.activation(K3[:, :, :], PB[:, 3, :], ACT.Copy).then_inc(k3_ready, 1)
            yield "r3"
            act.wait_ge(r3_mm, due(r3_mm, it, 1))
            act.wait_ge(out_stored, due(out_stored, it, 16))
            nc.scalar.activation(R3[:, :, :], PB[:, 0, :], ACT.Copy).then_inc(r3_ready, 1)
            yield "g3"
            act.wait_ge(g3_mm, due(g3_mm, it, 1))
            nc.scalar.activation(Q3[:, :, :], PB[:, 3, :], ACT.Tanh, scale=0.5).then_inc(g3_tanh, 1)
            yield "centre"
            act.wait_ge(cen_mm, due(cen_mm, it, 1))
            act.wait_ge(g3_ready, due(g3_ready, it, 1))
            nc.scalar.activation(Q3[:, :, :], PB[:, 2, :], ACT.Square).then_inc(cen_sq, 1)
            yield "gvar"
            act.wait_ge(gvar_mm, due(gvar_mm, it, 1))
            nc.scalar.activation(XI[:, :, :], PB[:, 3, :], ACT.Sqrt, bias=eps[:, :]).then_inc(gsd_ready, 1)
            yield from act_ln(act, it, 4, "l3ln2_s", "l3ln2_b")
            yield "xk"
            act.wait_ge(fk_mm, due(fk_mm, it, 1))
            link(act, "act_b", it, nc.scalar.activation(Q3[:, :, :], PB[:, 0, :], ACT.Relu))
            nc.scalar.activation(Q3[:, :, :], Q3[:, :, :], ACT.Square).then_inc(fk_ready, 1)
            yield "fr"
            act.wait_ge(fr_mm, due(fr_mm, it, 1))
            nc.scalar.activation(FR[:, :, :], PB[:, 1, :], ACT.Tanh, scale=0.5).then_inc(fr_tanh, 1)
            yield "fv"
            at = it * PAIR if isinstance(it, int) else act.snap(it * PAIR)
            act.wait_ge(yo_ready, due(yo_ready, it, 1))
            act.dma_start(out[bass.ds(at, PAIR)].rearrange("b s n -> s b n"), FR[:, :, :]).then_inc(out_stored, 16)
            chain_end("act_b")

        @block.scalar
        def _(act):
            act.dma_start(row[:, :], rows.partition_broadcast(P)).then_inc(wa_in, 16)
            act.wait_ge(bn_var1, 1)
            nc.scalar.activation(bn_s[:, 1:2], bn_s[:, 2:3], ACT.Sqrt).then_inc(bn_sd, 1)
            nc.scalar.activation(bq1s[:, :], cv("bq1"), ACT.Copy, scale=float(D1) ** -0.5).then_inc(bn_sd, 1)
            act.wait_ge(bn_sd, 2)
            nc.scalar.activation(R3[:, 0, 0:1], cv("bq1"), ACT.Copy).then_inc(out_stored, 16)
            trips(act, act_stage_a, act_stage_b)
            act.wait_ge(out_stored, 16 * (TRIPS + 1))

        def dve_stage_a(dve, it):
            v = nc.vector

            def step(ins):
                link(dve, "dve_a", it, ins)

            def split(i):
                step(v.tensor_copy(QKP[:, i, 0, :], QK[:, i, :]))
                step(v.tensor_tensor(RES[:, i, :], QK[:, i, :], QKP[:, i, 0, :], ALU.subtract))
                step(v.tensor_copy(QKP[:, i, 1, :], RES[:, i, :]))
                return v.tensor_tensor(QKP[:, i, 2, :], RES[:, i, :], QKP[:, i, 1, :], ALU.subtract)

            yield "pg"
            dve.wait_ge(pair_in, due(pair_in, it, 48))
            v.tensor_copy(MF[:, :, :], MASK8[:, :, :])
            v.tensor_scalar(MBIAS[:, :].rearrange("p (b n) -> p b n", b=PAIR), MASK8[:, :, :], -1.0, 1e30, ALU.add,
                            ALU.mult).then_inc(mbias_ready, 1)
            dve.wait_ge(pg_mm, due(pg_mm, it, 1))
            v.tensor_tensor(PG[:, :, :], PA[:, 0, :].rearrange("p (a n) -> p a n", n=128),
                            rv("phi_g_b").unsqueeze(1).to_broadcast([P, 4, 128]), ALU.add).then_inc(pg_ready, 1)
            yield "k"
            dve.wait_ge(at_mm, due(at_mm, it, 1))
            v.tensor_copy(AT[:, :, :], PA[0:CI, 2, 0:N].rearrange("p (b n) -> p b n", b=PAIR)).then_inc(at_ready, 1)
            dve.wait_ge(k_ready, due(k_ready, it, 1))
            split(1).then_inc(kp_ready, 1)
            yield "bt"
            dve.wait_ge(bt_ready, due(bt_ready, it, 1))
            v.tensor_scalar(SH[:, :], PA[:, 1, N:N + PAIR], bn_s[:, 0:1], bn_s[:, 2:3], ALU.mult, ALU.add).then_inc(sh_ready, 1)
            dve.wait_ge(v_mm, due(v_mm, it, 1))
            v.tensor_tensor(VH[:, :, :, 0:D1], PA[:, 2, :].rearrange("p (a h d) -> p a h d", a=4, d=D1),
                            rv("bv1").rearrange("p (h d) -> p h d", d=D1).unsqueeze(1).to_broadcast([P, 4, H1, D1]),
                            ALU.add).then_inc(v_ready, 1)
            yield "y"
            dve.wait_ge(y_mm, due(y_mm, it, 1))
            v.scalar_tensor_tensor(out=X1[:, :, :], in0=PA[:, 0, :].rearrange("p (b n) -> p b n", b=PAIR), scalar=bn_s[:, 0:1],
                                   in1=X0[:, :, :], op0=ALU.mult, op1=ALU.add).then_inc(y_added, 1)
            yield "q"
            dve.wait_ge(q_ready, due(q_ready, it, 1))
            split(0).then_inc(qp_ready, 1)
            for b in range(PAIR):
                for h in range(H1):
                    u = b * H1 + h
                    yield ("s", b, h)
                    dve.wait_ge(s_mm, due(s_mm, it, u + 1))
                    v.tensor_reduce(MX[:, b, :, h], PA[:, u % 3, :].rearrange("p (q k) -> p q k", q=2), AX.X,
                                    ALU.max).then_inc(s_max, 1)
                yield ("max", b)
                dve.wait_ge(m_tr, due(m_tr, it, b + 1))
                if b:
                    dve.wait_ge(maxp_out, due(maxp_out, it, 16 * b))
                step(v.tensor_scalar(NM[:, 0, :], PA[0:H1, 3, 0:N], -1.0, None, ALU.mult))
                step(v.tensor_copy(NMP[:, 0, :], NM[:, 0, :]))
                step(v.tensor_tensor(NM[:, 1, :], NM[:, 0, :], NMP[:, 0, :], ALU.subtract))
                step(v.tensor_copy(NMP[:, 1, :], NM[:, 1, :]))
                v.tensor_tensor(NMP[:, 2, :], NM[:, 1, :], NMP[:, 1, :], ALU.subtract).then_inc(m_parts, 1)
            yield "norm"
            dve.wait_ge(mbias_ready, due(mbias_ready, it, 1))
            step(v.tensor_tensor(X1[:, :, :], X1[:, :, :], MF[:, :, :], ALU.mult))
            step(v.tensor_tensor(XN[:, :, :], X1[:, :, :], X1[:, :, :], ALU.mult))
            v.tensor_reduce(IST[:, 0, :], MF[:, :, :], AX.X, ALU.add)
            v.tensor_reduce(IST[:, 1, :], X1[:, :, :], AX.X, ALU.add)
            step(v.tensor_reduce(IST[:, 2, :], XN[:, :, :], AX.X, ALU.add))
            step(v.reciprocal(IST[:, 3, :], IST[:, 0, :]))
            step(v.tensor_tensor(IST[:, 4, :], IST[:, 1, :], IST[:, 3, :], ALU.mult))
            v.tensor_tensor(IST[:, 2, :], IST[:, 2, :], IST[:, 3, :], ALU.mult)
            step(v.tensor_tensor(IST[:, 5, :], IST[:, 4, :], IST[:, 4, :], ALU.mult))
            step(v.tensor_tensor(IST[:, 5, :], IST[:, 2, :], IST[:, 5, :], ALU.subtract))
            v.tensor_scalar(IST[:, 5, :], IST[:, 5, :], 0.0, EPS, ALU.max, ALU.add).then_inc(ivar_ready, 1)
            yield "unit"
            dve.wait_ge(istd_ready, due(istd_ready, it, 1))
            step(v.reciprocal(IST[:, 7, :], IST[:, 6, :]))
            for b in range(PAIR):
                last = v.tensor_scalar(XN[:, b, :], X1[:, b, :], IST[:, 4, b:b + 1], IST[:, 7, b:b + 1], ALU.subtract, ALU.mult)
            step(last)
            step(v.tensor_tensor(XN[:, :, :], XN[:, :, :], MF[:, :, :], ALU.mult))
            for b in range(PAIR):
                for t in range(HT):
                    yield ("t", b, G * t + 2 * G - 1)
                    dve.wait_ge(pv_mm, due(pv_mm, it, b * HT + t + 1))
                    if b and t == 0:
                        dve.wait_ge(ot_tr, due(ot_tr, it, 2 * b))
                    v.tensor_copy(OT[:, t, :], PA[:, 2 + t % 2, 0:N]).then_inc(pv_out, 1)
                for q in range(2):
                    yield ("o", b, q)
                    dve.wait_ge(ot_tr, due(ot_tr, it, 2 * b + q + 1))
                    heads = PA[:, 2, :].rearrange("p (h d) -> p h d", d=32)
                    step(v.reciprocal(RSUM[:, :], heads[:, :, 2 * D1]))
                    scale = RSUM[:, :].unsqueeze(2).to_broadcast([P, H1, D1])
                    v.tensor_tensor(MN[:, 2 * b + q, :].rearrange("p (h d) -> p h d", d=D1), heads[:, :, 0:D1], scale, ALU.mult)
                    v.tensor_tensor(EX[:, 2 * b + q, :].rearrange("p (h d) -> p h d", d=D1), heads[:, :, D1:2 * D1], scale,
                                    ALU.mult).then_inc(ot_out, 1)
            yield "var"
            dve.wait_ge(ot_out, due(ot_out, it, 4))
            step(v.tensor_tensor(SQ[:, :, :], MN[:, :, :], MN[:, :, :], ALU.mult))
            step(v.tensor_tensor(EX[:, :, :], EX[:, :, :], SQ[:, :, :], ALU.subtract))
            v.tensor_scalar(EX[:, :, :], EX[:, :, :], 0.0, None, ALU.max).then_inc(var_ready, 1)
            yield "x2"
            dve.wait_ge(ms_tr, due(ms_tr, it, 1))
            step(v.tensor_tensor(XN[:, :, :], XN[:, :, :], PA[:, 3, :].rearrange("p (b n) -> p b n", b=PAIR), ALU.mult))
            step(v.tensor_tensor(XN[:, :, :], XN[:, :, :], PA[:, 2, :].rearrange("p (b n) -> p b n", b=PAIR), ALU.add))
            v.tensor_tensor(X2[:, :, :], XN[:, :, :], MF[:, :, :], ALU.mult).then_inc(x2_ready, 1)
            dve.wait_ge(x2_ready, due(x2_ready, it, 1))
            chain_end("dve_a")

        def dve_stage_b(dve, it):
            v = nc.vector

            def step(ins):
                link(dve, "dve_b", it, ins)

            def ln(i, src, names, meanwhile=None):
                yield ("ln", i)
                for b in range(PAIR):
                    last = v.bn_stats(BST[:, b, :], src[:, b, :])
                step(last)
                v.memset(cell[:, :], 0.0)
                for b in range(PAIR):
                    last = v.bn_aggr(BMV[:, b, :], BST[:, b, :])
                last.then_inc(ln_var, 1)
                yield ("hat", i)
                dve.wait_ge(ln_sd, due(ln_sd, it, i + 1))
                step(v.reciprocal(RSD[:, :], SDV[:, :]))
                for b in range(PAIR):
                    last = v.tensor_scalar(XH[:, b, :], src[:, b, :], BMV[:, b, 0:1], RSD[:, b:b + 1], ALU.subtract, ALU.mult)
                last.then_inc(ln_hat, 1)
                if meanwhile:
                    meanwhile()
                dve.wait_ge(ln_tr, due(ln_tr, it, i + 1))
                v.tensor_scalar(LNT[:, 1, :], PB[:, 1, 0:T], cv(names[0], 1), cv(names[1], 1), ALU.mult, ALU.add).then_inc(ln_ready_dve, 1)

            def add_bias(i, src, name):
                dve.wait_ge(ln_hat, due(ln_hat, it, i + 1))
                step(v.tensor_tensor(X3[:, :, :], src[:, :, :], rv(name).unsqueeze(1).to_broadcast([P, PAIR, N]), ALU.add))

            def tail(u):
                yield ("tail", u)
                dve.wait_ge(ao_mm, due(ao_mm, it, u + 1))
                v.tensor_tensor(X3[:, u % 2, :], X3[:, u % 2, :], PB[:, half_at(u, 0) + 1, 0:N], ALU.add).then_inc(res_ready, 1)

            dve.wait_ge(wb_in, 16 * 13)
            for a in range(2):
                src = (X2, X3)[a]
                def values():
                    dve.wait_ge(vp_mm, due(vp_mm, it, a + 1))
                    for par in range(2):
                        pair_of = lambda x: x.rearrange("p b (h r d) -> p b h r d", r=2, d=D2)[:, :, :, par, :]
                        bias = rv(("bv_self", "bv_cross")[a]).unsqueeze(1).to_broadcast([P, PAIR, N])
                        to = V2[:, :, :, par * D2:(par + 1) * D2].rearrange("p b (h r) d -> p b h r d", r=2)[:, :, :, par, :]
                        last = v.tensor_tensor(to,
                                               pair_of(PB[:, 3, :].rearrange("p (b n) -> p b n", b=PAIR)), pair_of(bias), ALU.add)
                    last.then_inc(v2_ready, 1)

                def meanwhile():
                    add_bias(a, src, ("b_ao", "b_co")[a])
                    if a:
                        values()

                yield from ln(a, src, (("ln1_s", "ln1_b"), ("ln2_s", "ln2_b"))[a], meanwhile)
                yield ("q", a)
                if a == 0:
                    dve.wait_ge(cross_in, due(cross_in, it, 16))
                    v.tensor_scalar(CFILL[:, :, :], CMASK[:, :, :], -1.0, 10000.0, ALU.add, ALU.mult)
                    step(v.tensor_scalar(SFILL[:, :], SMASK[:, :], -1.0, 10000.0, ALU.add, ALU.mult))
                dve.wait_ge(qp_mm, due(qp_mm, it, 2 * a + 1))
                for par in range(2):
                    last = v.tensor_scalar(QT[:, par, :], PB[:, 0, 0:T], cv("parity", par),
                                           cv(("bq_self", "bq_cross")[a], par), ALU.mult, ALU.add)
                last.then_inc(qt_ready_dve, 1)
                if a == 0:
                    yield ("kv", a)
                    values()
                for b in range(PAIR):
                    u = 2 * a + b
                    mask, fill = (SMASK[:, :], SFILL[:, :]) if a == 0 else (CMASK[:, b, :], CFILL[:, b, :])
                    def masked(g):
                        return v.scalar_tensor_tensor(out=SM[:, 4 * g:4 * g + 4, :], in0=PB[:, g, :].rearrange("p (t k) -> p t k", k=C),
                                                      scalar=float(D2) ** -0.5, in1=mask.unsqueeze(1).to_broadcast([P, 4, C]),
                                                      op0=ALU.mult, op1=ALU.mult)

                    def maxima(g):
                        hs = slice(4 * g, 4 * g + 4)
                        step(v.tensor_reduce(MX2[:, hs], SM[:, hs, :], AX.X, ALU.max))
                        v.tensor_scalar(NMX2[:, hs], MX2[:, hs], -1.0, None, ALU.mult).then_inc(sc_nmax, 1)

                    for i in range(2):
                        yield ("score", u, i)
                        g = half_at(u, i)
                        dve.wait_ge(sc_mm, due(sc_mm, it, 2 * u + i + 1))
                        masked(g + 1).then_inc(sc_masked, 1)
                        step(masked(g))
                        step(v.tensor_tensor(SM[:, 4 * g:4 * g + 4, :], SM[:, 4 * g:4 * g + 4, :],
                                             fill.unsqueeze(1).to_broadcast([P, 4, C]), ALU.add))
                        maxima(g)
                        if b and i == 0:
                            yield from tail(u - 1)
                        dve.wait_ge(sc_filled, due(sc_filled, it, 2 * u + i + 1))
                        maxima(g + 1)
                    yield ("norm", u)
                    for n, (g, banks) in enumerate(parts(u)):
                        dve.wait_ge(sc_exp, due(sc_exp, it, 4 * u + 2 + n))
                        hs = slice(4 * g, 4 * (g + banks))
                        step(v.reciprocal(RR2[:, hs], RS2[:, hs]))
                        v.tensor_tensor(SM[:, hs, :], SM[:, hs, :], RR2[:, hs].unsqueeze(2).to_broadcast([P, 4 * banks, C]),
                                        ALU.mult).then_inc(p_norm, 1)
                    for n in (0, 2):
                        yield ("turn", u, n)
                        dve.wait_ge(p_tr, due(p_tr, it, 3 * u + n + 1))
                        g, banks = parts(u)[n]
                        v.tensor_copy(PT2[:, 4 * g:4 * (g + banks), :],
                                      PB[:, g:g + banks, :].rearrange("p g (t k) -> p (g t) k", k=C)).then_inc(p_out_dve, 1)
                yield from tail(2 * a + 1)
                dve.wait_ge(res_ready, due(res_ready, it, 2 * a + 2))
            yield from ln(2, X3, ("ln3_s", "ln3_b"), lambda: add_bias(2, X3, "b2"))
            yield "ff2"
            dve.wait_ge(ff2_mm, due(ff2_mm, it, 1))
            v.tensor_tensor(X3[:, :, :], X3[:, :, :], PB[:, 0, :].rearrange("p (b n) -> p b n", b=PAIR), ALU.add).then_inc(x4_ready, 1)
            dve.wait_ge(x4_ready, due(x4_ready, it, 1))

            def shift(i):
                dve.wait_ge(ln_ready_act, due(ln_ready_act, it, 4 + i))
                dve.wait_ge(ln_ready_dve, due(ln_ready_dve, it, 4 + i))
                new = LNT[:, :, :].rearrange("p e (b t) -> p (e b) t", b=PAIR)
                old = ENC[:, :, :].rearrange("p e (b t) -> p (e b) t", b=PAIR)
                to = SX[:, :, :].rearrange("p e (b t) -> p (e b) t", b=PAIR)
                v.tensor_tensor(to[:, :, 1:C], new[:, :, 0:C - 1], new[:, :, 1:C], ALU.subtract)
                step(v.tensor_tensor(to[:, :, 0:1], old[:, :, 1 - i:2 - i], new[:, :, 0:1], ALU.subtract))

            yield from ln(3, X3, ("l3ln1_s", "l3ln1_b"))
            yield "xi"
            shift(0)
            for e in range(2):
                last = v.scalar_tensor_tensor(out=XI[:, e, :], in0=SX[:, e, :], scalar=cv("maa_x", e), in1=LNT[:, e, :],
                                              op0=ALU.mult, op1=ALU.add)
            last.then_inc(xi_ready, 1)
            for f in range(NF):
                yield ("mix", f)
                dve.wait_ge(mix_mm, due(mix_mm, it, f + 1))
                for e in range(2):
                    last = v.scalar_tensor_tensor(out=XMX[f][:, e, :], in0=PB[:, f % 4, e * T:(e + 1) * T],
                                                  scalar=cv("stack", 2 * f + e), in1=SX[:, e, :], op0=ALU.add, op1=ALU.mult)
                last.then_inc(mix_used, 1)
            yield "v3"
            dve.wait_ge(v3_mm, due(v3_mm, it, 1))
            v.tensor_copy(V3[:, :, :], PB[:, 2, :].rearrange("p (e t) -> p e t", e=2)).then_inc(v3_ready, 1)
            yield "ruk"
            dve.wait_ge(k3_ready, due(k3_ready, it, 1))
            dve.wait_ge(r3_ready, due(r3_ready, it, 1))
            dve.wait_ge(w_ready, due(w_ready, it, 1))
            dve.wait_ge(state_in, due(state_in, it, 64))
            for e in range(2):
                last = v.scalar_tensor_tensor(out=RUK[:, e, :], in0=R3[:, e, :], scalar=cv("u", e), in1=K3[:, e, :],
                                              op0=ALU.mult, op1=ALU.mult)
            last.then_inc(ruk_ready, 1)
            for e in range(2):
                yield ("spread", e, 0)
                v.tensor_copy(KV3[:, :, :, 0:1].rearrange("p j b o -> p j (b o)"), S0[:, e, :, :].rearrange("p b j -> p j b"))
                for half in range(2):
                    if half:
                        yield ("spread", e, 1)
                    dve.wait_ge(sp_mm, due(sp_mm, it, 2 * e + half + 1))
                    js = slice(4 * half, 4 * half + 4)
                    k = K3[:, e, :].rearrange("p (b t) -> p b t", b=PAIR)[:, :, 0:C - 1]
                    v.tensor_tensor(KV3[:, js, :, 1:C],
                                    PB[:, 2 * half:2 * half + 2, :].rearrange("p x (y b t) -> p (x y) b t", y=2, b=PAIR)[:, :, :, 0:C - 1],
                                    k.unsqueeze(1).to_broadcast([P, 4, PAIR, C - 1]), ALU.mult).then_inc(kv_ready, 1)
                dve.wait_ge(kv_ready, due(kv_ready, it, 2 * e + 2))
                for js in (range(4), range(4, D3)):
                    for j in js:
                        last = v.tensor_tensor_scan(ST3[:, e, j, :], WS[:, e, :, :].rearrange("p b t -> p (b t)"),
                                                    KV3[:, j, :, :].rearrange("p b t -> p (b t)"), 0.0, ALU.mult, ALU.add)
                    step(last)
                    v.tensor_tensor(ST3[:, e, js[0]:js[0] + 4, :], ST3[:, e, js[0]:js[0] + 4, :],
                                    R3[:, e, :].unsqueeze(1).to_broadcast([P, 4, T]), ALU.mult).then_inc(y3_ready, 1)
            yield "bonus"
            dve.wait_ge(g3_tanh, due(g3_tanh, it, 1))
            v.scalar_tensor_tensor(out=G3[:, :, :], in0=Q3[:, :, :], scalar=1.0, in1=PB[:, 3, :].rearrange("p (e t) -> p e t", e=2),
                                   op0=ALU.add, op1=ALU.mult).then_inc(g3_ready, 1)
            dve.wait_ge(bonus_mm, due(bonus_mm, it, 1))
            step(v.tensor_tensor(O3[:, :, :], PB[:, 1, :].rearrange("p (e t) -> p e t", e=2), V3[:, :, :], ALU.mult))
            v.tensor_tensor(O3[:, :, :], O3[:, :, :], PB[:, 0, :].rearrange("p (e t) -> p e t", e=2), ALU.add).then_inc(o3_ready, 1)
            yield "gvar"
            dve.wait_ge(cen_sq, due(cen_sq, it, 1))
            for e in range(2):
                last = v.tensor_scalar(RUK[:, e, :], PB[:, 2, e * T:(e + 1) * T], cv("gn_w", e), None, ALU.mult)
            yield "og"
            dve.wait_ge(gsd_ready, due(gsd_ready, it, 1))
            step(v.reciprocal(XI[:, :, :], XI[:, :, :]))
            step(v.tensor_tensor(RUK[:, :, :], RUK[:, :, :], XI[:, :, :], ALU.mult))
            for e in range(2):
                last = v.scalar_tensor_tensor(out=XI[:, e, :], in0=RUK[:, e, :], scalar=cv("gn_b", e), in1=G3[:, e, :],
                                              op0=ALU.add, op1=ALU.mult)
            last.then_inc(og_ready, 1)
            yield "wo"
            dve.wait_ge(wo_mm, due(wo_mm, it, 1))
            step(v.scalar_tensor_tensor(out=X3[:, :, :], in0=PB[:, 0, :].rearrange("p (b n) -> p b n", b=PAIR), scalar=0.5,
                                        in1=X3[:, :, :], op0=ALU.mult, op1=ALU.add))
            yield from ln(4, X3, ("l3ln2_s", "l3ln2_b"))
            yield "xk"
            shift(1)
            for e in range(2):
                v.scalar_tensor_tensor(out=XI[:, e, :], in0=SX[:, e, :], scalar=cv("mk", e), in1=LNT[:, e, :],
                                       op0=ALU.mult, op1=ALU.add)
                last = v.scalar_tensor_tensor(out=XR[:, e, :], in0=SX[:, e, :], scalar=cv("mr", e), in1=LNT[:, e, :],
                                              op0=ALU.mult, op1=ALU.add)
            last.then_inc(xk_ready, 1)
            yield "fv"
            dve.wait_ge(fr_tanh, due(fr_tanh, it, 1))
            dve.wait_ge(fv_mm, due(fv_mm, it, 1))
            step(v.scalar_tensor_tensor(out=FR[:, :, :], in0=FR[:, :, :], scalar=1.0,
                                        in1=PB[:, 2, :].rearrange("p (b n) -> p b n", b=PAIR), op0=ALU.add, op1=ALU.mult))
            v.scalar_tensor_tensor(out=FR[:, :, :], in0=FR[:, :, :], scalar=0.5, in1=X3[:, :, :], op0=ALU.mult,
                                   op1=ALU.add).then_inc(yo_ready, 1)
            dve.wait_ge(yo_ready, due(yo_ready, it, 1))
            chain_end("dve_b")

        @block.vector
        def _(dve):
            U32 = mybir.dt.uint32
            nc.vector.memset(KS[64:ROW_MAX, :, :].bitcast(U32), 0)
            nc.vector.memset(KS[ROW_MAX:P, :, :].bitcast(U32), 0x3F803F80).then_inc(zero_ready, 1)
            nc.vector.memset(VV[:, :, :], 1.0)
            nc.vector.memset(V2[:, :, :, :], 0.0)
            nc.vector.memset(eps[:, :], EPS)
            nc.vector.memset(WS[:, :, :, 0:1], 0.0).then_inc(zero_ready, 1)
            dve.wait_ge(zero_ready, 2)
            dve.wait_ge(wa_in, 16 * 5)
            nc.vector.tensor_scalar(bn_s[:, 2:3], cv("bn_var"), EPS, None, ALU.add).then_inc(bn_var1, 1)
            dve.wait_ge(bn_sd, 1)
            nc.vector.reciprocal(bn_s[:, 1:2], bn_s[:, 1:2]).then_inc(bn_ready, 1)
            dve.wait_ge(bn_ready, 1)
            nc.vector.tensor_tensor(bn_s[:, 0:1], cv("bn_gamma"), bn_s[:, 1:2], ALU.mult)
            nc.vector.tensor_tensor(bn_s[:, 2:3], cv("w_b"), cv("bn_mean"), ALU.subtract).then_inc(bn_ready, 1)
            dve.wait_ge(bn_ready, 2)
            nc.vector.scalar_tensor_tensor(out=bn_s[:, 2:3], in0=bn_s[:, 2:3], scalar=bn_s[:, 0:1], in1=cv("bn_beta"),
                                           op0=ALU.mult, op1=ALU.add).then_inc(bn_ready, 1)
            dve.wait_ge(bn_ready, 3)
            trips(dve, dve_stage_a, dve_stage_b)

        def pe_stage_a(pe, it):
            mm, tr = nc.tensor.matmul, nc.tensor.transpose
            yield "pg"
            pe.wait_ge(pair_in, due(pair_in, it, 48))
            for b in range(PAIR):
                for j in range(2):
                    last = mm(PA[:, 0, (2 * b + j) * 128:(2 * b + j + 1) * 128], CTX[:, b, j * 128:(j + 1) * 128], WA[:, 0, :],
                              start=True, stop=True)
            last.then_inc(pg_mm, 1)
            for c in range(2):
                for b in range(PAIR):
                    last = tr(PA[:, 3, (2 * c + b) * 128:(2 * c + b + 1) * 128], CTX[:, b, c * 128:(c + 1) * 128], ident[:, :])
            last.then_inc(enc_tr, 1)
            yield "mt"
            pe.wait_ge(pg_ready, due(pg_ready, it, 1))
            for b in range(PAIR):
                for j in range(2):
                    last = mm(PA[0:CI, 1, b * CI:(b + 1) * CI], PG[:, 2 * b + j, CI:2 * CI], PG[:, 2 * b + j, 0:CI],
                              start=(j == 0), stop=(j == 1))
            last.then_inc(mt_mm, 1)
            yield "k"
            pe.wait_ge(enc_ready, due(enc_ready, it, 1))
            pe.wait_ge(mt_ready, due(mt_ready, it, 1))
            mm(PA[:, 3, :], WA[:, 2, :], CTX[:, :, :], start=True, stop=True).then_inc(k_mm, 1)
            for b in range(PAIR):
                last = mm(PA[0:CI, 2, b * 128:(b + 1) * 128], MT[:, b, :], WWT[:, :], start=True, stop=True)
            last.then_inc(at_mm, 1)
            yield "bt"
            pe.wait_ge(at_ready, due(at_ready, it, 1))
            mm(PA[:, 1, 0:N], THW[:, :], AT[:, :, :], start=True, stop=True)
            for b in range(PAIR):
                last = mm(PA[:, 1, N + b:N + b + 1], AT[:, b, :], cv("theta_b", 0, CI), start=True, stop=True)
            last.then_inc(bt_mm, 1)
            for b in range(PAIR):
                for j in range(2):
                    last = mm(PA[:, 2, (2 * b + j) * 128:(2 * b + j + 1) * 128], CTX[:, b, j * 128:(j + 1) * 128], WA[:, 3, :],
                              start=True, stop=True)
            last.then_inc(v_mm, 1)
            yield "y"
            pe.wait_ge(bt_ready, due(bt_ready, it, 1))
            for b in range(PAIR):
                last = mm(PA[:, 0, b * N:(b + 1) * N], BT[:, b, :], X0[:, b, :], start=True, stop=True)
            last.then_inc(y_mm, 1)
            yield "q"
            pe.wait_ge(sh_ready, due(sh_ready, it, 1))
            pe.wait_ge(x1_ready, due(x1_ready, it, 1))
            mm(PA[:, 1, :], WA[:, 1, :], X1[:, :, :], start=True, stop=True).then_inc(q_mm, 1)
            def scores(b):
                for h in range(H1):
                    u = b * H1 + h
                    yield ("s", b, h)
                    if u == 0:
                        pe.wait_ge(q_ready, due(q_ready, it, 1))
                        pe.wait_ge(k_ready, due(k_ready, it, 1))
                        pe.wait_ge(v_ready, due(v_ready, it, 1))
                        pe.wait_ge(stack_in, due(stack_in, it, 19 * 16))
                    if u >= 3:
                        pe.wait_ge(s_max, due(s_max, it, u - 2))
                    for q in range(2):
                        o = b * N + q * 128
                        last = mm(PA[:, u % 3, q * N:(q + 1) * N], QS[0:K_SCORES, h, o:o + 128], KS[0:K_SCORES, h, b * N:(b + 1) * N],
                                  start=True, stop=True)
                    last.then_inc(s_mm, 1)
                yield ("max", b)
                pe.wait_ge(s_max, due(s_max, it, (b + 1) * H1))
                if b:
                    pe.wait_ge(m_parts, due(m_parts, it, b))
                for q in range(2):
                    last = tr(PA[0:H1, 3, q * 128:(q + 1) * 128], MX[:, b, q, :], ident[:, :])
                last.then_inc(m_tr, 1)

            def shifted(b):
                for h in range(H1 + G):
                    u = b * H1 + h
                    yield ("t", b, h)
                    if h == 0:
                        pe.wait_ge(maxp_in[b], due(maxp_in[b], it, 16))
                        if b == 0:
                            pe.wait_ge(m_parts, due(m_parts, it, PAIR))
                            pe.wait_ge(vsq_ready, due(vsq_ready, it, 1))
                    if h < H1:
                        if u >= 2:
                            pe.wait_ge(t_exp, due(t_exp, it, u - 1))
                        for k in range(2):
                            o = b * N + k * 128
                            last = mm(PA[:, u % 2, k * N:(k + 1) * N], KS[0:K_SHIFTED, h, o:o + 128],
                                      QS[0:K_SHIFTED, h, b * N:(b + 1) * N], start=True, stop=True)
                        last.then_inc(t_mm, 1)
                    if h >= G and h % G == G - 1:
                        t = h // G - 1
                        n = b * HT + t
                        pe.wait_ge(t_exp, due(t_exp, it, b * H1 + (t + 1) * G))
                        if b and t == 0:
                            pe.wait_ge(ot_out, due(ot_out, it, 2 * b))
                        if n >= 2:
                            pe.wait_ge(pv_out, due(pv_out, it, n - 1))
                        for k in range(2):
                            for g in range(G):
                                hh = G * t + g
                                last = mm(PA[32 * g:32 * g + 32, 2 + t % 2, 0:N], VV[:, 2 * b + k, VC * hh:VC * hh + 32],
                                          PT[:, (b * H1 + hh) % (2 * G), k, :], start=(k == 0), stop=(k == 1),
                                          skip_group_check=True)
                        last.then_inc(pv_mm, 1)
                for q in range(2):
                    yield ("o", b, q)
                    pe.wait_ge(pv_out, due(pv_out, it, (b + 1) * HT))
                    if 2 * b + q:
                        pe.wait_ge(ot_out, due(ot_out, it, 2 * b + q))
                    for t in range(HT):
                        last = tr(PA[:, 2, t * 128:(t + 1) * 128], OT[:, t, q * 128:(q + 1) * 128], ident[:, :])
                    last.then_inc(ot_tr, 1)

            for b in range(PAIR):
                yield from scores(b)
            for b in range(PAIR):
                yield from shifted(b)
            yield "x2"
            pe.wait_ge(std_ready, due(std_ready, it, 1))
            for i in range(2 * PAIR):
                tr(PA[:, 2, i * 128:(i + 1) * 128], MN[:, i, :], ident[:, :])
            for i in range(2 * PAIR):
                last = tr(PA[:, 3, i * 128:(i + 1) * 128], SQ[:, i, :], ident[:, :])
            last.then_inc(ms_tr, 1)
            pe.wait_ge(x2_ready, due(x2_ready, it, 1))

        def pe_stage_b(pe, it):
            mm, tr = nc.tensor.matmul, nc.tensor.transpose

            def ln(i):
                yield ("hat", i)
                if i == 0:
                    pe.wait_ge(wb_in, 16 * 13)
                pe.wait_ge(ln_hat, due(ln_hat, it, i + 1))
                for c in range(2):
                    for b in range(PAIR):
                        last = tr(PB[:, c, b * C:(b + 1) * C], XH[:, b, c * 128:(c + 1) * 128], ident[:, :])
                last.then_inc(ln_tr, 1)

            def project(bank, w, src):
                for e in range(2):
                    for c in range(2):
                        last = mm(PB[:, bank, e * T:(e + 1) * T], w(c, e), src(c), start=(c == 0), stop=(c == 1))
                return last

            def project_apart(w, src):
                for e in range(2):
                    for c in range(2):
                        last = mm(PB[:, e, 0:T], w(c, e), src(c), start=(c == 0), stop=(c == 1))
                    last.then_inc(qp_mm, 1)

            def project_rows(bank, w, src, n=2):
                for b in range(PAIR):
                    for c in range(n):
                        last = mm(PB[:, bank, b * N:(b + 1) * N], src(c, b), w(c), start=(c == 0), stop=(c == n - 1))
                return last

            def tail(u):
                yield ("tail", u)
                pe.wait_ge(ct_ready, due(ct_ready, it, u + 1))
                for c in range(2):
                    last = mm(PB[:, half_at(u, 0) + 1, 0:N], CT2[:, c, :], WO[:, u // 2, c, :], start=(c == 0), stop=(c == 1))
                last.then_inc(ao_mm, 1)
                if u % 2 == 0:
                    pe.wait_ge(res_ready, due(res_ready, it, u + 1))

            for a in range(2):
                kv = LNT if a == 0 else ENC
                weight = lambda part: lambda c, e: WH[:, c, (3 * a + part) * N + e * P:(3 * a + part) * N + (e + 1) * P]

                def keys_values():
                    yield ("kv", a)
                    project(2, weight(1), lambda c: kv[:, c, :]).then_inc(kp_mm, 1)
                    if a:
                        pe.wait_ge(res_ready, due(res_ready, it, 2))
                    project_rows(3, lambda c: WH[:, c, (3 * a + 2) * N:(3 * a + 3) * N],
                                 lambda c, b: kv[:, c, b * C:(b + 1) * C]).then_inc(vp_mm, 1)

                if a:
                    yield from keys_values()
                yield from ln(a)
                yield ("q", a)
                pe.wait_ge(ln_ready_act, due(ln_ready_act, it, a + 1))
                pe.wait_ge(ln_ready_dve, due(ln_ready_dve, it, a + 1))
                project_apart(weight(0), lambda c: LNT[:, c, :])
                if a == 0:
                    yield from keys_values()
                pe.wait_ge(qt_ready_dve, due(qt_ready_dve, it, a + 1))
                pe.wait_ge(qt_ready_act, due(qt_ready_act, it, a + 1))
                pe.wait_ge(kt_ready, due(kt_ready, it, a + 1))
                for b in range(PAIR):
                    u = 2 * a + b
                    for i in range(2):
                        yield ("score", u, i)
                        if b == 0 and i == 1:
                            pe.wait_ge(v2_ready, due(v2_ready, it, a + 1))
                        for t in range(HT):
                            for g in (half_at(u, i), half_at(u, i) + 1):
                                last = mm(PB[:, g, t * C:(t + 1) * C], QT[32 * g:32 * g + 32, t, b * C:(b + 1) * C],
                                          KT[32 * g:32 * g + 32, t // 2, b * C:(b + 1) * C], start=True, stop=True)
                        last.then_inc(sc_mm, 1)
                        if b and i == 0:
                            yield from tail(u - 1)
                    for n, (g, banks) in enumerate(parts(u)):
                        yield ("turn", u, n)
                        pe.wait_ge(p_norm, due(p_norm, it, 3 * u + n + 1))
                        for h in range(4 * g, 4 * (g + banks)):
                            last = tr(PB[:, h // 4, (h % 4) * C:(h % 4 + 1) * C], SM[:, h, :], ident[:, :])
                        last.then_inc(p_tr, 1)
                    for i in range(2):
                        yield ("ctx", u, i)
                        pe.wait_ge(p_out_dve, due(p_out_dve, it, 2 * u + i + 1))
                        if i:
                            pe.wait_ge(p_out_act, due(p_out_act, it, u + 1))
                        for t in range(HT):
                            for g in (half_at(u, i), half_at(u, i) + 1):
                                last = mm(PB[32 * g:32 * g + 32, half_at(u, 0), (t // 2) * C:(t // 2 + 1) * C],
                                          V2[:, b, 8 * (t // 2) + 2 * g + t % 2, :], PT2[:, 4 * g + t, :],
                                          start=(t % 2 == 0), stop=(t % 2 == 1), skip_group_check=True)
                    last.then_inc(ctx_mm, 1)
                yield from tail(2 * a + 1)
            yield from ln(2)
            for o in range(FF // P):
                if o % 2 == 0:
                    yield ("ff", o // 2)
                if o == 0:
                    pe.wait_ge(ln_ready_act, due(ln_ready_act, it, 3))
                    pe.wait_ge(ln_ready_dve, due(ln_ready_dve, it, 3))
                for c in range(2):
                    last = mm(PB[:, o // 2, (o % 2) * T:(o % 2 + 1) * T], W1[:, c, o * P:(o + 1) * P], LNT[:, c, :],
                              start=(c == 0), stop=(c == 1))
                last.then_inc(ff_mm, 1)
            yield "ff2"
            pe.wait_ge(ff_act, due(ff_act, it, 8))
            project_rows(0, lambda c: W2[:, c, :], lambda c, b: HF[:, c, b * C:(b + 1) * C], FF // P).then_inc(ff2_mm, 1)
            yield from ln(3)
            yield "tx"
            pe.wait_ge(xi_ready, due(xi_ready, it, 1))
            for c in range(2):
                mm(PB[:, 0, 0:T], MW1[:, c, 0:128], XI[:, c, :], start=(c == 0), stop=(c == 1))
            for c in range(2):
                last = mm(PB[0:DM, 0, T:2 * T], MW1[:, c, 128:160], XI[:, c, :], start=(c == 0), stop=(c == 1))
            last.then_inc(tx_mm, 1)
            for f in range(4):
                yield ("mix", f)
                if f == 0:
                    pe.wait_ge(tx_ready, due(tx_ready, it, 1))
                for e in range(2):
                    last = mm(PB[:, f, e * T:(e + 1) * T], MW2[DM * f:DM * f + DM, e * P:(e + 1) * P], TX[DM * f:DM * f + DM, :],
                              start=True, stop=True)
                last.then_inc(mix_mm, 1)
            yield ("mix", 4)
            pe.wait_ge(mix_used, due(mix_used, it, 1))
            for e in range(2):
                last = mm(PB[:, 0, e * T:(e + 1) * T], MW2B[:, e * P:(e + 1) * P], TXB[:, :], start=True, stop=True)
            last.then_inc(mix_mm, 1)
            yield "td1"
            pe.wait_ge(mix_ready, due(mix_ready, it, 2))
            for c in range(2):
                last = mm(PB[0:DD, 1, 0:T], TW1[:, c, :], XMX[1][:, c, :], start=(c == 0), stop=(c == 1))
            last.then_inc(td1_mm, 1)
            yield "v3"
            pe.wait_ge(mix_ready, due(mix_ready, it, 3))
            project(2, lambda c, e: W3[:, c, 2, e * P:(e + 1) * P], lambda c: XMX[2][:, c, :]).then_inc(v3_mm, 1)
            yield "td2"
            pe.wait_ge(td1_ready, due(td1_ready, it, 1))
            for e in range(2):
                last = mm(PB[:, 1, e * T:(e + 1) * T], TW2[:, e * P:(e + 1) * P], TD[:, :], start=True, stop=True)
            last.then_inc(td2_mm, 1)
            yield "k3"
            pe.wait_ge(mix_ready, due(mix_ready, it, 4))
            project(3, lambda c, e: W3[:, c, 1, e * P:(e + 1) * P], lambda c: XMX[0][:, c, :]).then_inc(k3_mm, 1)
            yield "r3"
            pe.wait_ge(mix_ready, due(mix_ready, it, 5))
            project(0, lambda c, e: W3[:, c, 0, e * P:(e + 1) * P], lambda c: XMX[3][:, c, :]).then_inc(r3_mm, 1)
            for e in range(2):
                for half in range(2):
                    yield ("spread", e, half)
                    if e == 0 and half == 0:
                        pe.wait_ge(v3_ready, due(v3_ready, it, 1))
                        pe.wait_ge(k3_ready, due(k3_ready, it, 1))
                        pe.wait_ge(r3_ready, due(r3_ready, it, 1))
                        pe.wait_ge(w_ready, due(w_ready, it, 1))
                    if e:
                        pe.wait_ge(kv_ready, due(kv_ready, it, half + 1))
                    for j in range(4 * half, 4 * half + 4):
                        last = mm(PB[:, j // 2, (j % 2) * T:(j % 2 + 1) * T], SEL[:, 3 + j, :], V3[:, e, :], start=True, stop=True)
                    last.then_inc(sp_mm, 1)
            yield "g3"
            pe.wait_ge(kv_ready, due(kv_ready, it, 4))
            project(3, lambda c, e: W3[:, c, 3, e * P:(e + 1) * P], lambda c: XMX[4][:, c, :]).then_inc(g3_mm, 1)
            yield "sum"
            pe.wait_ge(ruk_ready, due(ruk_ready, it, 1))
            for e in range(2):
                for j in range(D3):
                    if j % 4 == 0:
                        pe.wait_ge(y3_ready, due(y3_ready, it, 2 * e + j // 4 + 1))
                    last = mm(PB[:, 0, e * T:(e + 1) * T], GATHER[:, D3 - 1 - j:D3 - 1 - j + P], ST3[:, e, j, :],
                              start=(j == 0), stop=(j == D3 - 1))
                if e == 0:
                    for c in range(2):
                        mm(PB[:, 1, c * T:(c + 1) * T], SEL[:, 0, :], RUK[:, c, :], start=True, stop=True)
            last.then_inc(bonus_mm, 1)
            yield "centre"
            pe.wait_ge(o3_ready, due(o3_ready, it, 1))
            mm(PB[:, 2, :], SEL[:, 1, :], O3[:, :, :], start=True, stop=True).then_inc(cen_mm, 1)
            yield "gvar"
            pe.wait_ge(cen_sq, due(cen_sq, it, 1))
            pe.wait_ge(g3_ready, due(g3_ready, it, 1))
            mm(PB[:, 3, :], SEL[:, 2, :], Q3[:, :, :], start=True, stop=True).then_inc(gvar_mm, 1)
            yield "wo"
            pe.wait_ge(og_ready, due(og_ready, it, 1))
            project_rows(0, lambda c: W3[:, c, 4, :], lambda c, b: XI[:, c, b * C:(b + 1) * C]).then_inc(wo_mm, 1)
            yield from ln(4)
            yield "xk"
            pe.wait_ge(xk_ready, due(xk_ready, it, 1))
            project(0, lambda c, e: W3[:, c, 5, e * P:(e + 1) * P], lambda c: XI[:, c, :]).then_inc(fk_mm, 1)
            yield "fr"
            project_rows(1, lambda c: W3[:, c, 6, :], lambda c, b: XR[:, c, b * C:(b + 1) * C]).then_inc(fr_mm, 1)
            yield "fv"
            pe.wait_ge(fk_ready, due(fk_ready, it, 1))
            project_rows(2, lambda c: W3[:, c, 7, :], lambda c, b: Q3[:, c, b * C:(b + 1) * C]).then_inc(fv_mm, 1)
            pe.wait_ge(yo_ready, due(yo_ready, it, 1))

        @block.tensor
        def _(pe):
            pe.wait_ge(wa_in, 16 * 5)
            pe.wait_ge(const_step, 2)
            pe.wait_ge(zero_ready, 2)
            trips(pe, pe_stage_a, pe_stage_b)


def kernel(**inputs):
    import concourse.bacc as _bacc
    from concourse.bass_utils import run_bass_kernel_spmd as _run

    a = {k: np.ascontiguousarray(v) for k, v in inputs.items()}
    l0, l1, l2, l3 = ({k[9:]: v for k, v in a.items() if k.startswith(f"L{i}_")} for i in range(4))
    halves = lambda w: w.reshape(-1, P, w.shape[-1]).transpose(1, 0, 2)

    def column(v):
        v = v.reshape(-1)
        if v.size < P:
            v = np.concatenate([v, np.zeros(P - v.size, v.dtype)])
        return v.reshape(-1, P).T


    def by_parity(v):
        o = np.zeros((2, 2, P // (2 * D2), 2, D2), v.dtype)
        for par in range(2):
            o[:, par, :, par] = v.reshape(2, P // (2 * D2), 2, D2)[:, :, par]
        return o.reshape(-1)

    vectors = dict(
        bn_gamma=l0["bn_gamma"], bn_beta=l0["bn_beta"], bn_mean=l0["bn_mean"], bn_var=l0["bn_var"], w_b=l0["w_b"],
        bq1=l1["bq"], bk1=l1["bk"], theta_b=l0["theta_b"], ln1_s=l2["ln1_s"], ln1_b=l2["ln1_b"], ln2_s=l2["ln2_s"],
        ln2_b=l2["ln2_b"], ln3_s=l2["ln3_s"], ln3_b=l2["ln3_b"], bq_self=by_parity(l2["b_qkv"][0:N]),
        bk_self=l2["b_qkv"][N:2 * N], bq_cross=by_parity(l2["b_q"]), bk_cross=l2["b_kv"][0:N], b1=l2["b1"],
        l3ln1_s=l3["ln1_w"], l3ln1_b=l3["ln1_b"], l3ln2_s=l3["ln2_w"], l3ln2_b=l3["ln2_b"], maa_x=l3["maa_x"],
        stack=l3["maa_stack"], decay=l3["time_decay"], u=l3["u"], gn_w=l3["gn_w"], gn_b=l3["gn_b"],
        parity=np.stack([np.arange(P) // D2 % 2 == par for par in range(2)]).astype(np.float32),
        mk=l3["ffn_maa_k"], mr=l3["ffn_maa_r"])
    rows = np.concatenate([l0["phi_b"], l0["g_b"], l1["bv"], l2["b_qkv"][2 * N:], l2["b_kv"][N:], l2["b_ao"], l2["b_co"], l2["b2"]])
    channel = np.arange(P)
    same_head = (channel[:, None] // D3 == channel[None, :] // D3).astype(np.float32)
    eye = np.eye(P, dtype=np.float32)
    spread = [same_head * (channel[:, None] % D3 == j) for j in range(D3)]
    sel = np.stack([same_head, eye - same_head / D3, same_head / D3] + spread, 1).astype(np.float32)
    gather = (np.arange(P + D3 - 1)[None, :] == D3 * (channel[:, None] // D3) + D3 - 1).astype(np.float32)
    laid = dict(
        x=a["x"], ctxt=a["ctx_2048"], kv_mask=a["mask_Bx1x2048_bf1"].reshape(NB, N).view(np.uint8),
        self_mask=a["mask_1x1xSxS2_fc1"].reshape(C, C), cross_mask=a["mask_Bx1xSxS2_ff1"].reshape(NB, C, C),
        cols=np.concatenate([column(vectors[k]) for k in COLS], 1), rows=rows,
        wa=np.stack([np.concatenate([l0["phi_w"], l0["g_w"]], 0).T, l1["Wq"].T, l1["Wk"].T, l1["Wv"].T], 1),
        ww_t=l0["w_w"].T, theta_w=l0["theta_w"],
        wh=np.concatenate([halves(l2["w_qkv"]), halves(l2["w_q"]), halves(l2["w_kv"])], 2),
        wo=np.stack([halves(l2["w_ao"]), halves(l2["w_co"])], 1),
        w_ff1=halves(l2["w1"]), w_ff2=halves(l2["w2"]),
        w3=np.stack([halves(l3[k].T) for k in ("Wr", "Wk", "Wv", "Wg", "Wo", "Wfk", "Wfr", "Wfv")], 2),
        maa_w1=l3["maa_w1"], maa_w2=l3["maa_w2"].reshape(NF * DM, N), td_w1=l3["td_w1"], td_w2=l3["td_w2"], sel=sel, gather=gather)
    nc = _bacc.Bacc("TRN2", target_bir_lowering=False, num_devices=1)
    arrays, ap = {}, {}
    for name, v in laid.items():
        v = np.ascontiguousarray(v)
        arrays[f"in_{name}_dram"] = v
        ap[name] = nc.dram_tensor(f"in_{name}_dram", v.shape, mybir.dt.from_np(v.dtype), kind="ExternalInput").ap()
    ap["out"] = nc.dram_tensor("out_0_dram", (NB, C, N), F32, kind="ExternalOutput").ap()
    four_layers(nc, **ap)
    return _run(nc, [arrays], core_ids=[0]).results[0]["out_0_dram"]
```
